# Optimizing a Trainium2 kernel written in Bass

```python
import numpy as np
import jax
import jax.numpy as jnp

def _softmax(x, axis=-1):
    return jax.nn.softmax(x, axis=axis)

def _gelu(x):
    return jax.nn.gelu(x, approximate=True)

def _silu(x):
    return jax.nn.silu(x)

def _sigmoid(x):
    return jax.nn.sigmoid(x)

def _layernorm(x, axis=-1, eps=1e-05):
    m = jnp.mean(x, axis=axis, keepdims=True)
    v = jnp.var(x, axis=axis, keepdims=True)
    return (x - m) / jnp.sqrt(v + eps)

def _scatter_add(tgt, idx, src, axis=0):
    return tgt.at[idx].add(src)

def _segment_sum(src, seg, n):
    return jax.ops.segment_sum(src, seg, n)
kernel_name = 'mk_early_fusion_embed_d1_tok_img1024_r4_af8871'

def setup_inputs(seed: int=0):
    np.random.seed(seed)
    _w = jnp.asarray

    def _rec_inputs():
        import jax
        import jax.numpy as jnp
        _rk = jax.random.key(seed)
        x = -0.00016672 + 0.999947 * jax.random.normal(jax.random.fold_in(_rk, 1), (32, 96, 96, 3), jnp.float32)
        x_txt = jax.random.randint(jax.random.fold_in(_rk, 51), (32, 32), 0, 250, jnp.int32)
        return (x, x_txt)
    x, x_txt = _rec_inputs()

    def _L0_tok_setup():
        import jax, jax.numpy as jnp
        import numpy as np
        P = 16
        E = 256

        def patchify(images, patch_size):
            B, H, W, C = images.shape
            hp, wp = (H // patch_size, W // patch_size)
            x = images.reshape(B, hp, patch_size, wp, patch_size, C)
            x = x.transpose(0, 1, 3, 2, 4, 5)
            return x.reshape(B, hp * wp, patch_size * patch_size * C)
        key = jax.random.key(seed)
        k_img, k_w, k_b, k_pos = jax.random.split(key, 4)
        B, H, W, C = (64, 96, 96, 3)
        patch_dim = P * P * C
        patch_count = H // P * (W // P)
        images = jax.random.normal(k_img, (B, H, W, C), dtype=jnp.float32)
        W_proj = jax.random.normal(k_w, (E, patch_dim), dtype=jnp.float32) * patch_dim ** (-0.5)
        b_proj = jax.random.normal(k_b, (E,), dtype=jnp.float32) * 0.02
        pos_emb = jax.random.normal(k_pos, (patch_count, E), dtype=jnp.float32) * 0.02
        return {'images': images, 'W_proj': W_proj, 'b_proj': b_proj, 'pos_emb': pos_emb}
    _L0_tok_all = _L0_tok_setup()
    _L0_tok_in = {k: v for k, v in _L0_tok_all.items() if k in ('W_proj', 'b_proj', 'pos_emb')}
    del _L0_tok_all

    def _L0_txt_setup():
        import math
        import jax, jax.numpy as jnp
        import numpy as np
        PAD_IDX = 1
        SEP_ID = 4
        STARTPOS = 1025
        BSZ, SEQ_LEN, EMBED_DIM = (32, 1024, 256)

        def _build_table(num_cons, dim, padding_idx, startpos):
            half = dim // 2
            freqs = jnp.exp(jnp.arange(half, dtype=jnp.float32) * -(math.log(10000.0) / (half - 1)))
            ang = jnp.arange(startpos, startpos + num_cons, dtype=jnp.float32)[:, None] * freqs[None, :]
            tab = jnp.concatenate([jnp.sin(ang), jnp.cos(ang)], axis=1)
            return tab.at[padding_idx].set(0.0)

        def _positions(tokens):
            L = tokens.shape[1]
            valid = jnp.cumprod((tokens != PAD_IDX).astype(jnp.int32), axis=1).astype(bool)
            j = jnp.arange(L, dtype=jnp.int32)
            sep_j = jnp.where(tokens == SEP_ID, j, 0)
            last_sep = jax.lax.associative_scan(jnp.maximum, sep_j, axis=1)
            pos = j - last_sep + 2
            return jnp.where(valid, pos, 1)
        key = jax.random.key(seed)
        tokens = jax.random.randint(key, (BSZ, SEQ_LEN), 0, 250, dtype=jnp.int64)
        num_cons = PAD_IDX + 1 + SEQ_LEN
        weights = _build_table(num_cons, EMBED_DIM, PAD_IDX, STARTPOS)
        return {'input': tokens, 'weights': weights}
    _L0_txt_all = _L0_txt_setup()
    _L0_txt_in = {k: v for k, v in _L0_txt_all.items() if k in ('weights',)}
    del _L0_txt_all

    def _L0_attn_setup():
        import jax, jax.numpy as jnp
        import numpy as np
        D_MODEL = 256
        HIDDEN = 512
        D_STATE = 16
        KERN = 3
        BATCH = 2
        SEQ = 512

        def _layernorm(x, g, b, eps=1e-05):
            m = jnp.mean(x, axis=-1, keepdims=True)
            v = jnp.var(x, axis=-1, keepdims=True)
            return (x - m) * jax.lax.rsqrt(v + eps) * g + b
        key = jax.random.key(seed)
        ks = jax.random.split(key, 10)
        w_scale = 0.02
        return {'x': jax.random.normal(ks[0], (BATCH, SEQ, D_MODEL), jnp.float32), 'W_x': jax.random.normal(ks[1], (HIDDEN, D_MODEL), jnp.float32) * w_scale, 'b_x': jnp.zeros((HIDDEN,), jnp.float32), 'W_g': jax.random.normal(ks[2], (HIDDEN, D_MODEL), jnp.float32) * w_scale, 'b_g': jnp.zeros((HIDDEN,), jnp.float32), 'conv_w': jax.random.normal(ks[3], (HIDDEN, 1, KERN), jnp.float32) * 0.3, 'conv_b': jnp.zeros((HIDDEN,), jnp.float32), 'A_raw': jax.random.normal(ks[4], (HIDDEN, D_STATE), jnp.float32), 'B_ssm': jax.random.normal(ks[5], (HIDDEN, D_STATE), jnp.float32), 'C_ssm': jax.random.normal(ks[6], (HIDDEN, D_STATE), jnp.float32), 'W_dt': jax.random.normal(ks[7], (HIDDEN, D_MODEL), jnp.float32) * w_scale, 'b_dt': jnp.zeros((HIDDEN,), jnp.float32), 'W_out': jax.random.normal(ks[8], (D_MODEL, HIDDEN), jnp.float32) * w_scale, 'b_out': jnp.zeros((D_MODEL,), jnp.float32), 'ln_g': jnp.ones((D_MODEL,), jnp.float32), 'ln_b': jnp.zeros((D_MODEL,), jnp.float32)}
    _L0_attn_all = _L0_attn_setup()
    _L0_attn_in = {k: v for k, v in _L0_attn_all.items() if k in ('W_x', 'b_x', 'W_g', 'b_g', 'conv_w', 'conv_b', 'A_raw', 'B_ssm', 'C_ssm', 'W_dt', 'b_dt', 'W_out', 'b_out', 'ln_g', 'ln_b')}
    del _L0_attn_all

    def _L0_ffn_setup():
        import jax, jax.numpy as jnp
        import numpy as np
        EPS_LN = 1e-05
        EPS_GATE = 1e-08

        def layer_norm(x, gamma, beta):
            mu = jnp.mean(x, axis=-1, keepdims=True)
            var = jnp.mean(jnp.square(x - mu), axis=-1, keepdims=True)
            return (x - mu) * jax.lax.rsqrt(var + EPS_LN) * gamma + beta
        key = jax.random.key(seed)
        ks = jax.random.split(key, 8)
        B, S, D, E, H = (4, 1024, 256, 4, 512)
        s_in = 1.0 / np.sqrt(D)
        s_h = 1.0 / np.sqrt(H)
        return {'h': jax.random.normal(ks[0], (B, S, D), dtype=jnp.float32), 'router_w': jax.random.uniform(ks[1], (E, D), jnp.float32, -s_in, s_in), 'rn_g': jnp.ones((D,), jnp.float32), 'rn_b': jnp.zeros((D,), jnp.float32), 'w1': jax.random.uniform(ks[2], (E, D, H), jnp.float32, -s_in, s_in), 'ln_g': jnp.ones((E, H), jnp.float32), 'ln_b': jnp.zeros((E, H), jnp.float32), 'w2': jax.random.uniform(ks[3], (E, H, D), jnp.float32, -s_h, s_h), 'on_g': jnp.ones((D,), jnp.float32), 'on_b': jnp.zeros((D,), jnp.float32)}
    _L0_ffn_all = _L0_ffn_setup()
    _L0_ffn_in = {k: v for k, v in _L0_ffn_all.items() if k in ('router_w', 'rn_g', 'rn_b', 'w1', 'ln_g', 'ln_b', 'w2', 'on_g', 'on_b')}
    del _L0_ffn_all
    return {'x': x, 'x_txt': x_txt, 'L0_tok_W_proj': _L0_tok_in['W_proj'], 'L0_tok_b_proj': _L0_tok_in['b_proj'], 'L0_tok_pos_emb': _L0_tok_in['pos_emb'], 'L0_txt_weights': _L0_txt_in['weights'], 'L0_attn_W_x': _L0_attn_in['W_x'], 'L0_attn_b_x': _L0_attn_in['b_x'], 'L0_attn_W_g': _L0_attn_in['W_g'], 'L0_attn_b_g': _L0_attn_in['b_g'], 'L0_attn_conv_w': _L0_attn_in['conv_w'], 'L0_attn_conv_b': _L0_attn_in['conv_b'], 'L0_attn_A_raw': _L0_attn_in['A_raw'], 'L0_attn_B_ssm': _L0_attn_in['B_ssm'], 'L0_attn_C_ssm': _L0_attn_in['C_ssm'], 'L0_attn_W_dt': _L0_attn_in['W_dt'], 'L0_attn_b_dt': _L0_attn_in['b_dt'], 'L0_attn_W_out': _L0_attn_in['W_out'], 'L0_attn_b_out': _L0_attn_in['b_out'], 'L0_attn_ln_g': _L0_attn_in['ln_g'], 'L0_attn_ln_b': _L0_attn_in['ln_b'], 'L0_ffn_router_w': _L0_ffn_in['router_w'], 'L0_ffn_rn_g': _L0_ffn_in['rn_g'], 'L0_ffn_rn_b': _L0_ffn_in['rn_b'], 'L0_ffn_w1': _L0_ffn_in['w1'], 'L0_ffn_ln_g': _L0_ffn_in['ln_g'], 'L0_ffn_ln_b': _L0_ffn_in['ln_b'], 'L0_ffn_w2': _L0_ffn_in['w2'], 'L0_ffn_on_g': _L0_ffn_in['on_g'], 'L0_ffn_on_b': _L0_ffn_in['on_b']}

def reference(x, x_txt, L0_tok_W_proj, L0_tok_b_proj, L0_tok_pos_emb, L0_txt_weights, L0_attn_W_x, L0_attn_b_x, L0_attn_W_g, L0_attn_b_g, L0_attn_conv_w, L0_attn_conv_b, L0_attn_A_raw, L0_attn_B_ssm, L0_attn_C_ssm, L0_attn_W_dt, L0_attn_b_dt, L0_attn_W_out, L0_attn_b_out, L0_attn_ln_g, L0_attn_ln_b, L0_ffn_router_w, L0_ffn_rn_g, L0_ffn_rn_b, L0_ffn_w1, L0_ffn_ln_g, L0_ffn_ln_b, L0_ffn_w2, L0_ffn_on_g, L0_ffn_on_b):
    import jax
    import jax.numpy as jnp

    def _L0_tok_ref(images, W_proj, b_proj, pos_emb):
        import jax, jax.numpy as jnp
        import numpy as np
        P = 16
        E = 256

        def patchify(images, patch_size):
            B, H, W, C = images.shape
            hp, wp = (H // patch_size, W // patch_size)
            x = images.reshape(B, hp, patch_size, wp, patch_size, C)
            x = x.transpose(0, 1, 3, 2, 4, 5)
            return x.reshape(B, hp * wp, patch_size * patch_size * C)
        patches = patchify(images, P)
        out = jnp.einsum('bnd,ed->bne', patches, W_proj) + b_proj + pos_emb[None, :, :]
        return out

    def _L0_txt_ref(input, weights):
        import math
        import jax, jax.numpy as jnp
        import numpy as np
        PAD_IDX = 1
        SEP_ID = 4
        STARTPOS = 1025
        BSZ, SEQ_LEN, EMBED_DIM = (32, 1024, 256)

        def _build_table(num_cons, dim, padding_idx, startpos):
            half = dim // 2
            freqs = jnp.exp(jnp.arange(half, dtype=jnp.float32) * -(math.log(10000.0) / (half - 1)))
            ang = jnp.arange(startpos, startpos + num_cons, dtype=jnp.float32)[:, None] * freqs[None, :]
            tab = jnp.concatenate([jnp.sin(ang), jnp.cos(ang)], axis=1)
            return tab.at[padding_idx].set(0.0)

        def _positions(tokens):
            L = tokens.shape[1]
            valid = jnp.cumprod((tokens != PAD_IDX).astype(jnp.int32), axis=1).astype(bool)
            j = jnp.arange(L, dtype=jnp.int32)
            sep_j = jnp.where(tokens == SEP_ID, j, 0)
            last_sep = jax.lax.associative_scan(jnp.maximum, sep_j, axis=1)
            pos = j - last_sep + 2
            return jnp.where(valid, pos, 1)
        pos = _positions(input)
        return jnp.take(weights, pos, axis=0)

    def _L0_attn_ref(x, W_x, b_x, W_g, b_g, conv_w, conv_b, A_raw, B_ssm, C_ssm, W_dt, b_dt, W_out, b_out, ln_g, ln_b):
        import jax, jax.numpy as jnp
        import numpy as np
        D_MODEL = 256
        HIDDEN = 512
        D_STATE = 16
        KERN = 3
        BATCH = 2
        SEQ = 512

        def _layernorm(x, g, b, eps=1e-05):
            m = jnp.mean(x, axis=-1, keepdims=True)
            v = jnp.var(x, axis=-1, keepdims=True)
            return (x - m) * jax.lax.rsqrt(v + eps) * g + b
        u = jnp.einsum('bld,hd->blh', x, W_x) + b_x
        g = jax.nn.sigmoid(jnp.einsum('bld,hd->blh', x, W_g) + b_g)
        pad = conv_w.shape[-1] // 2
        h = jax.lax.conv_general_dilated(jnp.transpose(u, (0, 2, 1)), conv_w, window_strides=(1,), padding=[(pad, pad)], feature_group_count=conv_w.shape[0], dimension_numbers=('NCH', 'OIH', 'NCH')) + conv_b[None, :, None]
        h = jnp.transpose(h, (0, 2, 1))
        u = u * g + h * (1.0 - g)
        dt = jax.nn.softplus(jnp.einsum('bld,hd->blh', x, W_dt) + b_dt).mean(axis=(0, 1))
        dt = jnp.clip(dt, 0.001, 2.0)
        A = -jax.nn.softplus(A_raw)
        A_d = jnp.exp(A * dt[:, None])
        B_d = (A_d - 1.0) / (A + 1e-06) * B_ssm
        Bsz, L, H = u.shape
        S = A_d.shape[1]

        def step(carry, u_t):
            new = A_d[None] * carry + B_d[None] * u_t[:, :, None]
            y_t = jnp.einsum('bhs,hs->bh', new, C_ssm)
            return (new, y_t)
        init = jnp.zeros((Bsz, H, S), dtype=u.dtype)
        _, ys = jax.lax.scan(step, init, jnp.transpose(u, (1, 0, 2)))
        y = jnp.transpose(ys, (1, 0, 2))
        out = jnp.einsum('blh,dh->bld', y, W_out) + b_out
        return _layernorm(x + out, ln_g, ln_b)

    def _L0_ffn_ref(h, router_w, rn_g, rn_b, w1, ln_g, ln_b, w2, on_g, on_b):
        import jax, jax.numpy as jnp
        import numpy as np
        EPS_LN = 1e-05
        EPS_GATE = 1e-08

        def layer_norm(x, gamma, beta):
            mu = jnp.mean(x, axis=-1, keepdims=True)
            var = jnp.mean(jnp.square(x - mu), axis=-1, keepdims=True)
            return (x - mu) * jax.lax.rsqrt(var + EPS_LN) * gamma + beta
        D = h.shape[-1]
        h_norm = layer_norm(h, rn_g, rn_b)
        g = jax.nn.softmax(jnp.einsum('bsd,ed->bse', h_norm, router_w), axis=-1)
        top2_w, top2_idx = jax.lax.top_k(g, 2)
        top2_w = top2_w / (jnp.sum(top2_w, axis=-1, keepdims=True) + EPS_GATE)
        hid = jnp.einsum('bsd,edh->bseh', h, w1)
        hid = jax.nn.relu(layer_norm(hid, ln_g, ln_b))
        expert_out = jnp.einsum('bseh,ehd->bsed', hid, w2)
        idx = jnp.broadcast_to(top2_idx[..., None], top2_idx.shape + (D,))
        top2_out = jnp.take_along_axis(expert_out, idx, axis=-2)
        out = jnp.sum(top2_out * top2_w[..., None], axis=-2)
        return layer_norm(out, on_g, on_b)
    h = _L0_tok_ref(x, L0_tok_W_proj, L0_tok_b_proj, L0_tok_pos_emb)
    h = jnp.concatenate([h, _L0_txt_ref(x_txt, L0_txt_weights)], axis=1)
    h = h + _L0_attn_ref(_layernorm(h, axis=-1), L0_attn_W_x, L0_attn_b_x, L0_attn_W_g, L0_attn_b_g, L0_attn_conv_w, L0_attn_conv_b, L0_attn_A_raw, L0_attn_B_ssm, L0_attn_C_ssm, L0_attn_W_dt, L0_attn_b_dt, L0_attn_W_out, L0_attn_b_out, L0_attn_ln_g, L0_attn_ln_b)
    h = h + _L0_ffn_ref(_layernorm(h, axis=-1), L0_ffn_router_w, L0_ffn_rn_g, L0_ffn_rn_b, L0_ffn_w1, L0_ffn_ln_g, L0_ffn_ln_b, L0_ffn_w2, L0_ffn_on_g, L0_ffn_on_b)
    return h

_drawn_inputs = setup_inputs


def setup_inputs(seed=0):
    import zlib

    import numpy as np

    out = dict(_drawn_inputs(seed))
    spreads = {'L0_attn_b_x': (0.0, 0.1),
     'L0_attn_b_g': (0.0, 0.1),
     'L0_attn_conv_b': (0.0, 0.1),
     'L0_attn_b_dt': (0.0, 0.1),
     'L0_attn_b_out': (0.0, 0.1),
     'L0_attn_ln_g': (1.0, 0.2),
     'L0_attn_ln_b': (0.0, 0.1),
     'L0_ffn_rn_g': (1.0, 0.2),
     'L0_ffn_rn_b': (0.0, 0.1),
     'L0_ffn_ln_g': (1.0, 0.2),
     'L0_ffn_ln_b': (0.0, 0.1),
     'L0_ffn_on_g': (1.0, 0.2),
     'L0_ffn_on_b': (0.0, 0.1)}
    factors = {}
    for name, (base, spread) in spreads.items():
        noise = np.random.default_rng([zlib.crc32(name.encode()), seed]).standard_normal(out[name].shape)
        drawn = base * np.exp(spread * noise) if base else spread * noise
        out[name] = jnp.asarray(drawn.astype(out[name].dtype))
    for name, factor in factors.items():
        out[name] = (out[name] * factor).astype(out[name].dtype)
    return out
```

```python
from contextlib import ExitStack

import concourse.bass as bass
from concourse import mybir

F32 = mybir.dt.float32
F32R = mybir.dt.float32r
I32 = mybir.dt.int32
ALU = mybir.AluOpType
ACT = mybir.ActivationFunctionType
AX = mybir.AxisListType.X
P = 128


def build_kernel(nc, ins, out):
    B, IMG, _, CH = ins["x"].shape
    LT = ins["x_txt"].shape[1]
    D, PD = ins["L0_tok_W_proj"].shape
    PS = 16
    HP = IMG // PS
    LI = HP * HP
    L = LI + LT
    H, S = ins["L0_attn_A_raw"].shape
    E, _, HF = ins["L0_ffn_w1"].shape
    N = L * B
    NT = N // P
    TPT = P // B
    NTI = LI // TPT
    DC, HC = D // P, H // P
    EPS = 1e-5
    BLOCKS = [(n, min(512, N - n)) for n in range(0, N, 512)]
    NB = len(BLOCKS)
    GB = B // 2
    ROWS = GB * HP
    CK = PD // P
    KT = CK // 2
    PWC = PS * CH
    QN, QH = 16, H // HC // 16
    QC = QH * HC

    stack = ExitStack()
    with stack:
        def sb(name, shape, dt=F32):
            return stack.enter_context(nc.sbuf_tensor(name, shape, dt))

        sems = {}

        def sem(name):
            if name not in sems:
                sems[name] = stack.enter_context(nc.semaphore(name))
            return sems[name]

        ident = sb("ident", [P, P])
        vec_rows = sb("vec_rows", [52, P])
        vec = sb("vec", [P, 52])
        cw = sb("cw", [P, HC, 3])
        c1 = sb("c1", [P, HC])
        araw = sb("araw", [P, HC, S])
        bcs = sb("bcs", [P, 2, HC, S])
        amat = sb("amat", [P, HC, S])
        atmp = sb("atmp", [P, HC, S])
        adt = sb("adt", [P, HC, S])
        wmix = sb("wmix", [P, HC, S])
        winv = sb("winv", [P, HC, S])
        kio = sb("kio", [P, L])
        rowid = sb("rowid", [P, 1])
        mv0 = sb("mv0", [P, NT, 2])
        sd0 = sb("sd0", [P, NT])
        rs0 = sb("rs0", [P, NT])
        nmr0 = sb("nmr0", [P, NT])
        bst = sb("bst", [P, 6])
        bst1 = sb("bst1", [P, 6])
        bst2 = sb("bst2", [P, 6])
        bst3 = sb("bst3", [P, 6])
        mv1 = sb("mv1", [P, NT, 2])
        sd1 = sb("sd1", [P, NT])
        rs1 = sb("rs1", [P, NT])
        mv2 = sb("mv2", [P, NT, 2])
        sd2 = sb("sd2", [P, NT])
        rs2 = sb("rs2", [P, NT])
        v2n = sb("v2n", [P, NT])
        rs2r = sb("rs2r", [P, NT])
        ones_b = sb("ones_b", [B, LT + 2])
        mv3 = sb("mv3", [P, NT, 2])
        sd3 = sb("sd3", [P, NT])
        rs3 = sb("rs3", [P, NT])
        epsc = sb("epsc", [P, 1])
        onec = sb("onec", [P, 1])
        dts = sb("dts", [P, HC, NB])
        dt1 = sb("dt1", [P, HC])
        dtc = sb("dtc", [P, HC])
        rwT = sb("rwT", [P, DC, E])
        rg = sb("rg", [P, DC, E])
        rg_hi = sb("rg_hi", [P, DC, E], F32R)
        rg_lo = sb("rg_lo", [P, DC, E], F32R)
        cbc = sb("cbc", [P, E])
        bout_b = sb("bout_b", [P, D])
        lng_b = sb("lng_b", [P, D])
        lnb_b = sb("lnb_b", [P, D])
        ong_b = sb("ong_b", [P, D])
        onb_b = sb("onb_b", [P, D])
        varE = sb("varE", [P, NT, E])
        stdE = sb("stdE", [P, NT, E])
        rstE = sb("rstE", [P, NT, E])
        s3 = sb("s3", [P, 2, 3, E], F32R)
        lg = sb("lg", [P, NT, E])
        gx = sb("gx", [P, NT, E])
        rank = sb("rank", [P, NT, E])
        cmp = sb("cmp", [P, NT, E])
        rsum = sb("rsum", [P, NT])
        wE = sb("wE", [P, NT, E])
        eid = sb("eid", [P, E])
        m12 = sb("m12", [12, E])
        mA = sb("mA", [12, 1])
        mB = sb("mB", [12, 1])
        w1m = sb("w1m", [P, E * DC])

        base = (nc.sbuf_base + 63) // 64 * 64

        def at(name, shape, offset, dt=F32):
            return nc.alloc_sbuf_tensor_at(name, shape, dt, offset=offset)

        def size(*shape):
            n = 4
            for s in shape:
                n *= s
            return (n + 63) // 64 * 64

        def place(start, end, *wanted):
            got = []
            for name, shape, *dt in wanted:
                got.append(at(name, shape, start, *dt))
                start += size(*shape[1:])
            assert start <= end, (wanted[-1][0], start, end)
            return got

        R1 = base
        R2 = R1 + 2 * size(DC, N)
        R3 = R2 + 6 * size(DC, H)
        R4 = R3 + size(5 * N + 4 * B)
        R5 = R4 + size(H * B)
        R6 = R5 + 3 * size(L * QC)
        TOP = nc.sbuf_usable_end

        xT_hi, xT_lo = place(R1, R2, ("xT_hi", [P, DC, N], F32R), ("xT_lo", [P, DC, N], F32R))
        y = at("y", [P, H // HC, L], R1)
        WT = place(R2, R3, *[(f"WT{w}_{v}", [P, DC, H], F32R) for w in ("dt", "x", "g") for v in ("hi", "lo")])
        WT = [WT[0:2], WT[2:4], WT[4:6]]
        w1c, gfb = place(R2, R3, ("w1c", [P, E, DC, HF]), ("gfb", [P, E, HF]))
        h0r, xb, r1, x2s, yT, acc = place(R2, R2 + size(E, DC, HF), ("h0r", [P, 2, D]), ("xb", [P, 2, D]),
                                          ("r1", [P, 2, D]), ("x2s", [P, 2, D]), ("yT", [P, 2, HC, P]), ("acc", [P, 2, 2, D]))
        (w1p,) = place(R3 + size(E, DC, HF), R4, ("w1p", [P, E, DC, HF]))
        (Bst,) = place(R2 + size(E, DC, HF), R3, ("Bst", [P, E, HF], F32R))
        (XI,) = place(R3, R4, ("XI", [ROWS, 2, HP, PD]))
        ur, hb, gb0 = place(R3, R4, ("ur", [P, 2, N + 2 * B]), ("hb", [P, 2, N]), ("gb0", [P, N]))
        w1g_hi, w1g_lo, x2T_hi, x2T_lo, stdT = place(
            R3, R4, ("w1g_hi", [P, E, DC, HF], F32R), ("w1g_lo", [P, E, DC, HF], F32R),
            ("x2T_hi", [P, 2, DC, 2 * P], F32R), ("x2T_lo", [P, 2, DC, 2 * P], F32R), ("stdT", [P, 2, 2 * P], F32R))
        patchT, WpT, Wpr, Wr0, Wr1, Wr2, posD = place(
            R4, R5, ("patchT", [P, CK, LI, B]), ("WpT", [P, CK, D]), ("Wpr", [P, DC, PD]), ("Wr0", [P, HC, D]),
            ("Wr1", [P, HC, D]), ("Wr2", [P, HC, D]), ("posD", [B, LT, B]))
        Wr = [Wr0, Wr1, Wr2]
        spt, spj = place(R4, R5, ("spt", [P, 4, 512]), ("spj", [P, 2, 512]))
        (U2,) = place(R4, R5, ("U2", [L, HC, H // HC, B]))
        w2_hi, w2_lo, hid_hi, hid_lo, G_hi, G_lo = place(
            R4, R5, ("w2_hi", [P, E, HC, D], F32R), ("w2_lo", [P, E, HC, D], F32R),
            ("hid_hi", [P, 2, HC, 2 * P], F32R), ("hid_lo", [P, 2, HC, 2 * P], F32R),
            ("G_hi", [P, DC, E * D], F32R), ("G_lo", [P, DC, E * D], F32R))
        _, w2raw, Wor, _, _ = place(R4, R5, ("_w2", [P, E, HC, D]), ("w2raw", [P, E, HC, D]), ("Wor", [P, DC, H]),
                                    ("_h", [P, HC, 2 * P]), ("_h2", [P, HC, 2 * P]))
        OH, tabl, posb, bpb, sel, h0s, xs, tok, tf, zrow = place(
            R5, R6, ("OH", [LT + 2, LT * B]), ("tabl", [LT + 2, D]), ("posb", [LI, D]), ("bpb", [LI, D]),
            ("sel", [LI, LI, B]), ("h0s", [P, 3, D]), ("xs", [P, 2, D]), ("tok", [B, LT], I32), ("tf", [B, 8, LT]),
            ("zrow", [QN, (L - 1) * QC // 4]))
        Eb, gb1 = place(R5, R6, ("Eb", [P, HC, L, S]), ("gb1", [P, N]))
        gb = [gb0, gb1]
        Tb = place(R5, R6, *[(f"Tb{i}", [L, L, QC]) for i in range(3)])
        h1, WoT, w1cT = place(R5, R6, ("h1", [P, NT, D]), ("WoT", [P, HC, D]), ("w1cT", [P, HC, D]))
        zjunk, rwt, Kk = place(R6, TOP, ("zjunk", [P, D]), ("rwt", [E, D]), ("Kk", [P, HC, L]))
        (kt,) = place(R6, TOP, ("kt", [L, QN, HC, QH]))
        (lb12,) = place(R3 + size(E, DC, HF) * 2, R4, ("lb12", [12, E, HF]))

        h0d = nc.dram_tensor("h0_spill", [NT, P, D], F32).ap()
        kpd = nc.dram_tensor("ssm_kernels", [QN, 2 * L - 1, QC], F32).ap()
        bank = [stack.enter_context(nc.psum_tensor(f"bank{i}", [P, 512], F32)) for i in range(8)]

        x = ins["x"]
        img = x.rearrange("(g b) (hp py) w c -> g (b hp) py (w c)", g=2, py=PS)
        w_dram = [ins[n].rearrange("(c p) d -> p c d", p=P) for n in ("L0_attn_W_dt", "L0_attn_W_x", "L0_attn_W_g")]

        def rows(name):
            a = ins[name]
            while len(a.shape) > 1:
                a = a.rearrange("a b -> (a b)")
            return a.rearrange("(r p) -> r p", p=P)

        def vecs(name):
            first = 0
            for n in VECS:
                count = rows(n).shape[0]
                if n == name:
                    return first, count
                first += count

        VECS = ["L0_attn_b_x", "L0_attn_b_g", "L0_attn_b_dt", "L0_attn_conv_b", "L0_ffn_rn_g", "L0_ffn_rn_b"]
        NV = sum(rows(n).shape[0] for n in VECS)
        bx0, bg0, bdt0, cb0, rng0, rnb0 = (vecs(n)[0] for n in VECS)
        state = lambda n: ins[n].rearrange("(c p) s -> p c s", p=P)

        TILE_ORDER = list(range(NTI, NT)) + [NTI - 1] + list(range(NTI - 1))
        BLOCK_ORDER = [3, 4, 2, 0, 1]

        def ready_tiles(nb):
            t0, t1 = BLOCKS[nb][0] // P, (BLOCKS[nb][0] + BLOCKS[nb][1]) // P
            return 1 + max(TILE_ORDER.index(t) for t in range(t0, t1))

        PREP = ([("vec",), ("pos", 0), ("pos", 1)] + [("wp", c) for c in range(0, CK, 2)]
                + [("w", w, dc) for w in range(3) for dc in range(DC)])
        IMAGES = [("img", half, g, wp) for g in range(2) for wp in range(HP) for half in range(2)]
        A_RING = PREP + IMAGES

        def a_reader(q):
            kind = A_RING[q][0]
            if kind == "img":
                return "act" if q % 2 else "dve"
            return "act" if kind == "wp" else "dve"

        def a_read(q):
            who = a_reader(q)
            return who, sum(a_reader(k) == who for k in range(q + 1))

        def wavefront(tiles, stages):
            return [(s, tiles[k - n]) for k in range(len(tiles) + len(stages) - 1)
                    for n, s in reversed(list(enumerate(stages))) if 0 <= k - n < len(tiles)]

        A_STEPS = ([("ring", q) for q in range(len(PREP))] + wavefront(TILE_ORDER[:8], ["a1", "a2", "a3", "a4"])
                   + [("ring", q) for q in range(len(PREP), len(A_RING))]
                   + wavefront(TILE_ORDER[8:], ["a1", "a2", "a3", "a4"]))

        FB = [list(range(i, min(i + 2, NT))) for i in range(0, NT, 2)]
        STAGES = ["yT", "out", "ln1", "h1", "x2", "x2T", "z0", "z1", "std", "stdT"]

        def front(b):
            return wavefront(FB[b], STAGES) + [("route1", b), ("route2", b)]

        def experts(b):
            hid = [("hid", b, e, k) for e in range(E) for k in range(2)]
            w2 = [("w2", b, e) for e in range(E)]
            return hid[0:4] + [w2[0]] + hid[4:6] + [w2[1]] + hid[6:8] + [w2[2], w2[3], ("fin1", b), ("fin2", b)]

        F_STEPS = front(0)
        for b in range(len(FB)):
            main, side = experts(b), front(b + 1) if b + 1 < len(FB) else []
            done = 0
            for n, step in enumerate(main):
                F_STEPS.append(step)
                upto = len(side) * (n + 1) // (len(main) - 4)
                F_STEPS += side[done:upto]
                done = max(done, min(upto, len(side)))
        AUX = [s for s in F_STEPS if s[0] in ("yT", "out", "x2T", "z0", "z1", "stdT")]
        AUX = [j for s in AUX for j in ([("lg", s[1]), s] if s[0] == "z0" else [s])]
        C_STEPS = [("proj", 0), ("proj", 1), ("turn", 0), ("kernels",), ("proj", 2), ("turn", 1), ("proj", 3), ("turn", 2),
                   ("turn", 3)]
        C_RING = []
        for step in C_STEPS:
            if step[0] == "kernels":
                C_RING.append(("kT",))
            if step[0] == "turn":
                C_RING += [("uT", step[1], k) for k in range(B // 4)]

        def c_reader(q):
            return "act" if C_RING[q][0] == "uT" and C_RING[q][2] % 2 == 0 else "dve"

        def c_read(q):
            who = c_reader(q)
            return who, sum(c_reader(k) == who for k in range(q + 1))

        G_RING = [("wo", 0), ("wo", 1), ("rw",), ("cbc",)] + [
            j for e in range(E) for j in (("w1T", e, 0), ("w1T", e, 1), ("gram", e))]

        def g_read(q):
            who = {"wo": "act", "w1T": "act", "rw": "dve", "cbc": "dve", "gram": "dve"}
            return who[G_RING[q][0]], sum(who[j[0]] == who[G_RING[q][0]] for j in G_RING[:q + 1])

        AUX_READER = {"yT": "act", "stdT": "act", "out": "dve", "x2T": "dve", "z0": "dve", "z1": "dve", "lg": "dve"}

        def aux_read(q):
            who = AUX_READER[AUX[q][0]]
            return who, sum(AUX_READER[j[0]] == who for j in AUX[:q + 1])

        def hid_job(b, e, k):
            return (b * E + e) * 2 + k

        def store(eng, i):
            if i < 0:
                return
            eng.wait_ge(sem("result"), i + 1)
            src = acc[:, i // 2 % 2, i % 2, :]
            eng.dma_start(out[:, TPT * i:TPT * (i + 1), :].rearrange("b t d -> t b d"), src).then_inc(
                sem(f"out_stored{i % 4}"), 16)

        def residual(pool, i):
            pool.wait_ge(sem("x2"), i + 1)
            pool.tensor_tensor(h1[:, i, :], h1[:, i, :], onb_b[:], ALU.add).then_inc(sem("h1b"), 1)

        def split3(pe, out_ap, a_hi, a_lo, b_hi, b_lo, start, stop):
            pe.matmul(out_ap, a_hi, b_hi, start=start, stop=False)
            pe.matmul(out_ap, a_hi, b_lo, start=False, stop=False)
            return pe.matmul(out_ap, a_lo, b_hi, start=False, stop=stop)

        def copy_b(act, o, i, bias):
            return act.activation(o, i, ACT.Identity, bias=bias)

        def log1p(act, q):
            w = BLOCKS[BLOCK_ORDER[q // HC]][1]
            act.wait_ge(sem("dt_exp"), q + 1)
            act.activation(spt[:, q % 4, 0:w], spt[:, q % 4, 0:w], ACT.Ln, bias=onec[:]).then_inc(sem("dt_ln"), 1)

        def patches(ps, half, g, wp):
            dst = patchT[:].rearrange("p c (hp wp) b -> p c hp wp b", wp=HP)[
                :, half * KT:(half + 1) * KT, :, wp, g * GB:(g + 1) * GB]
            return dst, ps[:, 0:KT * ROWS].rearrange("p (k b hp) -> p k hp b", k=KT, hp=HP)

        def turned(eng, j, who):
            for k in range(B // 4):
                q = C_RING.index(("uT", j, k))
                if c_reader(q) != who:
                    continue
                eng.wait_ge(sem("c_ps"), q + 1)
                dst = U2[:, j, :, 4 * k:4 * k + 4]
                src = bank[4 + q % 4][0:L, :].rearrange("p (b h) -> p h b", b=4)
                ins_ = (eng.activation(dst, src, ACT.Identity) if who == "act" else eng.tensor_copy(dst, src))
                ins_.then_inc(sem(f"c_read_{who}"), 1)

        Z_ORDER = [s for s in F_STEPS if s[0] in ("z0", "z1")]

        def z_count(kind, i):
            return Z_ORDER.index((kind, i)) + 1

        def var_count(kind, i):
            return 2 * z_count(kind, i)

        def spread(a, w):
            return a.rearrange("p (t o) -> p t o", o=1).broadcast_to([P, w, E])
        block = stack.enter_context(nc.Block())

        @block.sync
        def _(sp):
            sp.dma_start(tok[:], ins["x_txt"]).then_inc(sem("tok_in"), 16)
            at_row = 0
            for n in VECS:
                a = rows(n)
                sp.dma_start(vec_rows[at_row:at_row + a.shape[0], :], a).then_inc(sem("vecs_in"), 16)
                at_row += a.shape[0]
            sp.wait_ge(sem("zrow"), 1)
            for k in range(4):
                part = (L - 1) * QC // 4
                sp.dma_start(kpd.rearrange("q k c -> q (k c)")[:, L * QC + k * part:L * QC + (k + 1) * part], zrow[:]).then_inc(
                    sem("zrow_stored"), 16)
            sp.dma_start(tabl[:], ins["L0_txt_weights"][0:LT + 2, :]).then_inc(sem("table_in"), 16)
            for g in range(2):
                for wp in range(HP):
                    sp.dma_start(XI[:, g, wp].rearrange("p (y k) -> p y k", k=PWC),
                                 img[g][:, :, wp * PWC:(wp + 1) * PWC]).then_inc(sem(f"img_in{g}{wp // 2}"), 16)
            for m, i in enumerate(TILE_ORDER):
                sp.wait_ge(sem("h0_copied"), m + 1)
                sp.dma_start(h0d[i], h0s[:, m % 3, :]).then_inc(sem(f"h0_stored{m % 3}"), 16)
            sp.wait_ge(sem("kt_ready"), 1)
            sp.wait_ge(sem("zrow_stored"), 64)
            sp.dma_start(kpd[:, 0:L, :].rearrange("q k c -> k q c"),
                         kt[:].rearrange("k q j h -> k q (j h)")).then_inc(sem("kernels_stored"), 16)
            sp.wait_ge(sem("kernels_stored"), 16)
            sp.dma_start(rwt[:], ins["L0_ffn_router_w"]).then_inc(sem("router_in"), 16)
            for q in range(QN):
                if q == 0:
                    sp.wait_ge(sem("kernel_sum"), HC)
                if q == 2:
                    sp.wait_ge(sem("gated"), HC)
                if q == 3:
                    sp.wait_ge(sem("g_mm"), HC * NB)
                    sp.dma_start(w1c[:], ins["L0_ffn_w1"].rearrange("e (c p) h -> p e c h", p=P)).then_inc(
                        sem("w1_in"), 16)
                    sp.dma_start(gfb[:], ins["L0_ffn_ln_g"].partition_broadcast(P)).then_inc(sem("gfb_in"), 16)
                if q >= 3:
                    sp.wait_ge(sem("ssm_mm"), 2 * (q - 2))
                src = bass.AP(kpd.tensor, kpd.offset + q * (2 * L - 1) * QC, [[QC, L], [1, L * QC]])
                sp.dma_start(Tb[q % 3][:].rearrange("s t c -> s (t c)"), src).then_inc(sem(f"toep_in{q % 3}"), 16)
            sp.wait_ge(sem("ssm_mm"), 2 * QN)
            sp.dma_start(Wor[:], ins["L0_attn_W_out"].rearrange("(c p) h -> p c h", p=P)).then_inc(sem("wo_in"), 16)
            sp.dma_start(w2raw[:], ins["L0_ffn_w2"].rearrange("e (c p) d -> p e c d", p=P)).then_inc(sem("w2_in"), 16)
            sp.wait_ge(sem("w1g_split"), 1)
            sp.dma_start(lb12[:], ins["L0_ffn_ln_b"].partition_broadcast(12)).then_inc(sem("lb_in"), 16)
            sp.wait_ge(sem("gram_tr"), E)
            sp.wait_ge(sem("w1g_mult"), DC)
            for m in range(3):
                sp.wait_ge(sem(f"h0_stored{m}"), 16 * len(range(m, NT, 3)))
            for i in range(NT):
                if i >= 2:
                    sp.wait_ge(sem("h1"), i - 1)
                sp.dma_start(h0r[:, i % 2, :], h0d[i]).then_inc(sem(f"h0_back{i % 2}"), 16)
                store(sp, i - 6)
            for i in range(NT - 6, NT):
                store(sp, i)
            for k in range(4):
                sp.wait_ge(sem(f"out_stored{k}"), 16 * len(range(k, NT, 4)))

        @block.gpsimd
        def _(pool):
            pool.memset(ident[:], 0.0).then_inc(sem("ident0"), 1)
            pool.wait_ge(sem("ident0"), 1)
            pool.affine_select(out=ident[:], in_=ident[:], compare_op=ALU.not_equal, fill=1.0, base=0,
                               pattern=[[-1, P]], channel_multiplier=1).then_inc(sem("ident"), 1)
            pool.iota(rowid[:], pattern=[[0, 1]], base=0, channel_multiplier=1,
                      allow_small_or_imprecise_dtypes=True).then_inc(sem("consts"), 1)
            pool.iota(tf[:, 7, :], pattern=[[1, LT]], base=0, channel_multiplier=0,
                      allow_small_or_imprecise_dtypes=True).then_inc(sem("consts"), 1)
            pool.memset(zrow[:], 0.0).then_inc(sem("zrow"), 1)
            pool.memset(epsc[:], EPS).then_inc(sem("consts"), 1)
            pool.memset(onec[:], 1.0).then_inc(sem("consts"), 1)
            pool.iota(kio[:], pattern=[[-1, L]], base=L - 1, channel_multiplier=0,
                      allow_small_or_imprecise_dtypes=True).then_inc(sem("consts"), 1)
            pool.iota(eid[:], pattern=[[1, E]], base=0, channel_multiplier=0,
                      allow_small_or_imprecise_dtypes=True).then_inc(sem("consts"), 1)
            pool.memset(m12[:], 0.0).then_inc(sem("m12"), 1)
            for n in range(3):
                pool.wait_ge(sem("m12"), n + 1)
                pool.affine_select(out=m12[:], in_=m12[:], compare_op=ALU.not_equal, fill=1.0, base=-E * n,
                                   pattern=[[-1, E]], channel_multiplier=1).then_inc(sem("m12"), 1)
            pool.memset(mA[:], 1.0).then_inc(sem("mAB"), 1)
            pool.memset(mB[:], 0.0).then_inc(sem("mAB"), 1)
            pool.wait_ge(sem("mAB"), 2)
            pool.affine_select(out=mA[:], in_=mA[:], compare_op=ALU.is_ge, fill=0.0, base=2 * E - 1,
                               pattern=[[0, 1]], channel_multiplier=-1).then_inc(sem("mAB"), 1)
            pool.affine_select(out=mB[:], in_=mB[:], compare_op=ALU.is_ge, fill=1.0, base=2 * E - 1,
                               pattern=[[0, 1]], channel_multiplier=-1).then_inc(sem("mAB"), 1)
            pool.wait_ge(sem("adt"), 1)
            pool.wait_ge(sem("consts"), 6)
            for m in range(3):
                pool.wait_ge(sem(f"h0_stored{m}"), 16 * len(range(m, NT, 3)))
            pool.wait_ge(sem("zrow_stored"), 64)
            for j in range(HC):
                pool.tensor_tensor(Eb[:, j], adt[:, j].rearrange("p (o s) -> p o s", o=1).broadcast_to([P, L, S]),
                                   kio[:].rearrange("p (k o) -> p k o", o=1).broadcast_to([P, L, S]),
                                   ALU.mult).then_inc(sem("exponent"), 1)
            for j in range(HC):
                pool.wait_ge(sem("conv"), j + 1)
                mid = ur[:, j % 2, B:B + N]
                pool.tensor_tensor(mid, mid, hb[:, j % 2, :], ALU.subtract).then_inc(sem("u_minus_h"), 1)
                pool.wait_ge(sem("u_minus_h"), j + 1)
                pool.wait_ge(sem("gate"), NB * (j + 1))
                pool.tensor_tensor(mid, mid, gb[j % 2][:], ALU.mult).then_inc(sem("gated"), 1)
            pool.wait_ge(sem("w1_centred"), E * DC)
            pool.wait_ge(sem("gfb_in"), 16)
            pool.wait_ge(sem("c_ps"), len(C_RING))
            for dc in range(DC):
                pool.tensor_tensor(w1p[:, :, dc, :], w1c[:, :, dc, :], gfb[:], ALU.mult).then_inc(sem("w1g_mult"), 1)
            pool.wait_ge(sem("w1g_mult"), DC)
            pool.memset(Bst[:].bitcast(F32), 0.0).then_inc(sem("std_zero"), 1)
            pool.memset(stdT[:].bitcast(F32), 0.0).then_inc(sem("std_zero"), 1)
            for i in range(NT):
                pool.wait_ge(sem(f"h0_back{i % 2}"), 16 * (i // 2 + 1))
                pool.wait_ge(sem("nmr0"), 1)
                if i >= 2:
                    pool.wait_ge(sem("r1"), i - 1)
                pool.tensor_scalar(xb[:, i % 2, :], h0r[:, i % 2, :], rs0[:, i:i + 1], nmr0[:, i:i + 1],
                                   ALU.mult, ALU.add).then_inc(sem("xb0"), 1)
                pool.wait_ge(sem("xb0"), i + 1)
                pool.wait_ge(sem("rows_in"), 80)
                pool.tensor_tensor(xb[:, i % 2, :], xb[:, i % 2, :], bout_b[:], ALU.add).then_inc(sem("xb"), 1)
                pool.tensor_tensor(h0r[:, i % 2, :], h0r[:, i % 2, :], lnb_b[:], ALU.add).then_inc(sem("h0b"), 1)
                if i >= 2:
                    residual(pool, i - 2)
            residual(pool, NT - 2)
            residual(pool, NT - 1)

        @block.tensor
        def _(pe):
            pe.wait_ge(sem("ident"), 1)
            for step in A_STEPS:
                if step[0] == "ring":
                    q = step[1]
                    kind, *rest = A_RING[q]
                    if q >= 4:
                        who, n = a_read(q - 4)
                        pe.wait_ge(sem(f"a_read_{who}"), n)
                    ps = bank[q % 4]
                    if kind == "vec":
                        pe.wait_ge(sem("vecs_in"), 16 * len(VECS))
                        mm = pe.transpose(ps[:, 0:NV], vec_rows[0:NV, :], ident[0:NV, 0:NV])
                    elif kind == "pos":
                        pe.wait_ge(sem("pos_spread"), 2)
                        k = rest[0]
                        mm = pe.matmul(ps[0:LT + 2, :], ones_b[:, 0:LT + 2],
                                       posD[:].rearrange("p j b -> p (j b)")[:, k * 512:(k + 1) * 512],
                                       start=True, stop=True)
                    elif kind == "wp":
                        pe.wait_ge(sem("wp_in"), 16)
                        for c in range(rest[0], rest[0] + 2):
                            for eh in range(DC):
                                mm = pe.transpose(ps[:, (c % 2) * D + eh * P:(c % 2) * D + (eh + 1) * P],
                                                  Wpr[:, eh, c * P:(c + 1) * P], ident[:])
                    elif kind == "w":
                        w, dc = rest
                        pe.wait_ge(sem(f"w_in{w}"), 16)
                        for j in range(HC):
                            mm = pe.transpose(ps[:, j * P:(j + 1) * P], Wr[w][:, j, dc * P:(dc + 1) * P], ident[:])
                    else:
                        half, g, wp = rest
                        pe.wait_ge(sem(f"img_in{g}{wp // 2}"), 32)
                        for kk in range(KT):
                            c0 = (half * KT + kk) * P
                            mm = pe.transpose(ps[:, kk * ROWS:(kk + 1) * ROWS], XI[:, g, wp, c0:c0 + P],
                                              ident[0:ROWS, 0:ROWS])
                    mm.then_inc(sem("a_ps"), 1)
                elif step[0] == "a1":
                    i = step[1]
                    m = TILE_ORDER.index(i)
                    ps = bank[4 + m % 2][:, 0:D]
                    if m >= 2:
                        pe.wait_ge(sem("h0_copied"), m - 1)
                    if i >= NTI:
                        pe.wait_ge(sem("onehot"), 2)
                        pe.wait_ge(sem("table_in"), 16)
                        mm = pe.matmul(ps, OH[:, (i - NTI) * P:(i - NTI + 1) * P], tabl[:], start=True, stop=True)
                    else:
                        pe.wait_ge(sem("posb"), 2)
                        who, n = a_read(len(A_RING) - 2)
                        pe.wait_ge(sem(f"a_read_{who}"), n)
                        who, n = a_read(len(A_RING) - 1)
                        pe.wait_ge(sem(f"a_read_{who}"), n)
                        for c in range(CK):
                            pe.matmul(ps, patchT[:, c, TPT * i:TPT * (i + 1), :].rearrange("p t b -> p (t b)"),
                                      WpT[:, c, :], start=(c == 0), stop=False)
                        mm = pe.matmul(ps, sel[:, TPT * i:TPT * (i + 1), :].rearrange("p t b -> p (t b)"), posb[:],
                                       start=False, stop=True)
                    mm.then_inc(sem("h0_ps"), 1)
                elif step[0] == "a4":
                    m = TILE_ORDER.index(step[1])
                    pe.wait_ge(sem("x"), m + 1)
                    if m >= 2:
                        pe.wait_ge(sem("xT"), m - 1)
                    for dc in range(DC):
                        mm = pe.transpose(bank[6 + m % 2][:, dc * P:(dc + 1) * P], xs[:, m % 2, dc * P:(dc + 1) * P],
                                          ident[:])
                    mm.then_inc(sem("xT_ps"), 1)

            for n, nb in enumerate(BLOCK_ORDER):
                n0, w = BLOCKS[nb]
                pe.wait_ge(sem("xT"), ready_tiles(nb))
                for j in range(HC):
                    q = n * HC + j
                    if q >= 4:
                        pe.wait_ge(sem("dt_read"), q - 3)
                    for dc in range(DC):
                        mm = split3(pe, bank[q % 4][:, 0:w], WT[0][0][:, dc, j * P:(j + 1) * P],
                                    WT[0][1][:, dc, j * P:(j + 1) * P], xT_hi[:, dc, n0:n0 + w],
                                    xT_lo[:, dc, n0:n0 + w], dc == 0, dc == DC - 1)
                    mm.then_inc(sem("dt_mm"), 1)
            pe.wait_ge(sem("dt_read"), HC * NB)

            ring = 0
            for step in C_STEPS:
                if step[0] == "proj":
                    j = step[1]
                    for nb, (n0, w) in enumerate(BLOCKS):
                        c = j * NB + nb
                        for wt, first, done, read in ((1, 0, "u_mm", "ur"), (2, 2, "g_mm", "gate")):
                            if c >= 2:
                                pe.wait_ge(sem(read), c - 1)
                            for dc in range(DC):
                                mm = split3(pe, bank[first + c % 2][:, 0:w], WT[wt][0][:, dc, j * P:(j + 1) * P],
                                            WT[wt][1][:, dc, j * P:(j + 1) * P], xT_hi[:, dc, n0:n0 + w],
                                            xT_lo[:, dc, n0:n0 + w], dc == 0, dc == DC - 1)
                            mm.then_inc(sem(done), 1)
                    continue
                count = 1 if step[0] == "kernels" else B // 4
                for k in range(count):
                    if ring >= 4:
                        who, n = c_read(ring - 4)
                        pe.wait_ge(sem(f"c_read_{who}"), n)
                    ps = bank[4 + ring % 4]
                    if step[0] == "kernels":
                        pe.wait_ge(sem("kernel_sum"), HC)
                        for j in range(HC):
                            mm = pe.transpose(ps[0:L, j * P:(j + 1) * P], Kk[:, j, :], ident[:])
                    else:
                        j = step[1]
                        pe.wait_ge(sem("mixed"), j + 1)
                        for b in range(4 * k, 4 * k + 4):
                            mm = pe.transpose(ps[0:L, (b % 4) * P:(b % 4 + 1) * P],
                                              hb[:, j % 2, :].rearrange("p (t b) -> p t b", b=B)[:, :, b], ident[:])
                    mm.then_inc(sem("c_ps"), 1)
                    ring += 1

            pe.wait_ge(sem("ur"), HC * NB)
            pe.wait_ge(sem("gate"), HC * NB)
            for q in (len(C_RING) - 2, len(C_RING) - 1):
                who, n = c_read(q)
                pe.wait_ge(sem(f"c_read_{who}"), n)
            for v in range(2 * QN):
                q = v // 2
                pe.wait_ge(sem(f"toep_in{q % 3}"), 16 * (q // 3 + 1))
                if v >= 4:
                    pe.wait_ge(sem("y_dve" if v % 2 else "y_act"), (v - 4) // 2 + 1)
                for k in range(4):
                    hq = 4 * v + k
                    for j in range(HC):
                        mm = pe.matmul(bank[v % 4][j * B:(j + 1) * B, k * L:(k + 1) * L], U2[:, j, hq, :],
                                       Tb[q % 3][:, :, j * QH + hq % QH], start=True, stop=True)
                mm.then_inc(sem("ssm_mm"), 1)

            for q, (kind, *rest) in enumerate(G_RING):
                if q >= 4:
                    who, n = g_read(q - 4)
                    pe.wait_ge(sem(f"g_read_{who}"), n)
                ps = bank[4 + q % 4]
                if kind == "wo":
                    pe.wait_ge(sem("wo_in"), 16)
                    for j in range(2):
                        for c in range(DC):
                            h0_ = (2 * rest[0] + j) * P
                            mm = pe.transpose(ps[:, j * D + c * P:j * D + (c + 1) * P], Wor[:, c, h0_:h0_ + P], ident[:])
                elif kind == "rw":
                    pe.wait_ge(sem("router_in"), 16)
                    for dc in range(DC):
                        mm = pe.transpose(ps[:, dc * E:(dc + 1) * E], rwt[:, dc * P:(dc + 1) * P], ident[0:E, 0:E])
                elif kind == "cbc":
                    pe.wait_ge(sem("rnb_spread"), DC)
                    pe.wait_ge(sem("rwT"), 1)
                    for dc in range(DC):
                        mm = pe.matmul(ps[:, 0:E], zjunk[:, dc * P:(dc + 1) * P], rwT[:, dc, :], start=(dc == 0),
                                       stop=(dc == DC - 1))
                elif kind == "w1T":
                    e, k = rest
                    pe.wait_ge(sem("w1_centred"), E * DC)
                    for hc in range(2):
                        for dc in range(DC):
                            c0 = (2 * k + hc) * P
                            mm = pe.transpose(ps[:, hc * D + dc * P:hc * D + (dc + 1) * P], w1c[:, e, dc, c0:c0 + P],
                                              ident[:])
                    if k == 1:
                        mm.then_inc(sem("gram_tr"), 1)
                        pe.wait_ge(sem("gram_tr"), e + 1)
                        mm = pe.nop()
                else:
                    e = rest[0]
                    pe.wait_ge(sem("w1T"), 2 * (e + 1))
                    for dc in range(DC):
                        for hc in range(HC):
                            mm = pe.matmul(ps[:, dc * D:(dc + 1) * D], w1cT[:, hc, dc * P:(dc + 1) * P], w1cT[:, hc, :],
                                           start=(hc == 0), stop=(hc == HC - 1))
                mm.then_inc(sem("g_ps"), 1)
            for q in range(len(G_RING) - 4, len(G_RING)):
                who, n = g_read(q)
                pe.wait_ge(sem(f"g_read_{who}"), n)

            aux = 0

            def aux_bank():
                nonlocal aux
                if aux >= 4:
                    who, n = aux_read(aux - 4)
                    pe.wait_ge(sem(f"aux_read_{who}"), n)
                aux += 1
                return bank[4 + (aux - 1) % 4]

            for kind, *rest in F_STEPS:
                i = rest[0]
                if kind == "yT":
                    ps = aux_bank()
                    if i == 0:
                        pe.wait_ge(sem("y_act"), QN)
                        pe.wait_ge(sem("y_dve"), QN)
                    for tt in range(TPT):
                        mm = pe.transpose(ps[:, tt * P:(tt + 1) * P], y[:, :, L - 1 - (TPT * i + tt)], ident[:])
                    mm.then_inc(sem("yT_ps"), 1)
                elif kind == "out":
                    ps = aux_bank()
                    pe.wait_ge(sem("yT"), i + 1)
                    for j in range(HC):
                        mm = pe.matmul(ps[:, 0:D], yT[:, i % 2, j, :], WoT[:, j, :], start=(j == 0), stop=(j == HC - 1))
                    mm.then_inc(sem("out_mm"), 1)
                elif kind == "x2T":
                    ps = aux_bank()
                    pe.wait_ge(sem("x2"), i + 1)
                    for dc in range(DC):
                        mm = pe.transpose(ps[:, dc * P:(dc + 1) * P], x2s[:, i % 2, dc * P:(dc + 1) * P], ident[:])
                    mm.then_inc(sem("x2T_ps"), 1)
                elif kind in ("z0", "z1"):
                    pe.wait_ge(sem("x2T"), i + 1)
                    tok_ = slice(i % 2 * P, (i % 2 + 1) * P)
                    hi, lo = x2T_hi[:, i // 2 % 2, :, tok_], x2T_lo[:, i // 2 % 2, :, tok_]
                    if kind == "z0":
                        ps = aux_bank()
                        pe.wait_ge(sem("router_split"), 2)
                        for dc in range(DC):
                            mm = split3(pe, ps[:, 0:E], hi[:, dc, :], lo[:, dc, :], rg_hi[:, dc, :], rg_lo[:, dc, :],
                                        dc == 0, dc == DC - 1)
                        mm.then_inc(sem("logit_mm"), 1)
                    ps = aux_bank()
                    cols = slice(0, 512) if kind == "z0" else slice(512, 1024)
                    for dc in range(DC):
                        mm = split3(pe, ps[:], hi[:, dc, :], lo[:, dc, :], G_hi[:, dc, cols], G_lo[:, dc, cols],
                                    dc == 0, dc == DC - 1)
                    mm.then_inc(sem("z_mm"), 1)
                elif kind == "stdT":
                    ps = aux_bank()
                    pe.wait_ge(sem("s3"), 3 * (i + 1))
                    mm = pe.transpose(ps[0:3 * E, 0:P], s3[:, i % 2].rearrange("p a e -> p (a e)").bitcast(F32), ident[:])
                    mm.then_inc(sem("stdT_ps"), 1)
                elif kind == "hid":
                    b, e, k = rest
                    q, w = hid_job(b, e, k), P * len(FB[b])
                    if q == 0:
                        pe.wait_ge(sem("w1g_split"), 2)
                        pe.wait_ge(sem("Bst"), 1)
                    if q >= 2:
                        pe.wait_ge(sem("hid_lo"), q - 1)
                    pe.wait_ge(sem("stdT"), FB[b][-1] + 1)
                    for hc in (2 * k, 2 * k + 1):
                        ps = bank[q % 2][:, (hc % 2) * 2 * P:(hc % 2) * 2 * P + w]
                        hs = slice(hc * P, (hc + 1) * P)
                        for dc in range(DC):
                            split3(pe, ps, w1g_hi[:, e, dc, hs], w1g_lo[:, e, dc, hs], x2T_hi[:, b % 2, dc, 0:w],
                                   x2T_lo[:, b % 2, dc, 0:w], dc == 0, False)
                        mm = pe.matmul(ps, Bst[:, e, hs], stdT[:, b % 2, 0:w], start=False, stop=True)
                    mm.then_inc(sem("hid_mm"), 1)
                elif kind == "w2":
                    b, e = rest
                    q = b * E + e
                    if q == 0:
                        pe.wait_ge(sem("w2_split"), 2)
                    if q >= 2:
                        pe.wait_ge(sem("combined"), q - 1)
                    pe.wait_ge(sem("hid_lo"), hid_job(b, e, 1) + 1)
                    for n in range(len(FB[b])):
                        ts = slice(n * P, (n + 1) * P)
                        for hc in range(HC):
                            mm = split3(pe, bank[2 + q % 2][:, n * D:(n + 1) * D], hid_hi[:, e % 2, hc, ts],
                                        hid_lo[:, e % 2, hc, ts], w2_hi[:, e, hc, :], w2_lo[:, e, hc, :],
                                        hc == 0, hc == HC - 1)
                    mm.then_inc(sem("w2_mm"), 1)

        @block.scalar
        def _(act):
            act.dma_start(Wpr[:], ins["L0_tok_W_proj"].rearrange("(c p) d -> p c d", p=P)).then_inc(sem("wp_in"), 16)
            act.dma_start(araw[:], state("L0_attn_A_raw")).then_inc(sem("araw_in"), 16)
            act.dma_start(posb[:], ins["L0_tok_pos_emb"]).then_inc(sem("bcs_in"), 16)
            act.dma_start(bpb[:], ins["L0_tok_b_proj"].partition_broadcast(LI)).then_inc(sem("bcs_in"), 16)
            for w in range(3):
                act.dma_start(Wr[w][:], w_dram[w]).then_inc(sem(f"w_in{w}"), 16)
            act.dma_start(bcs[:, 0], state("L0_attn_B_ssm")).then_inc(sem("bcs_in"), 16)
            act.dma_start(bcs[:, 1], state("L0_attn_C_ssm")).then_inc(sem("bcs_in"), 16)
            act.dma_start(cw[:], ins["L0_attn_conv_w"].rearrange("(c p) o k -> p c (o k)", p=P)).then_inc(sem("cw_in"), 16)
            for t, n in ((bout_b, "L0_attn_b_out"), (lng_b, "L0_attn_ln_g"), (lnb_b, "L0_attn_ln_b"),
                         (ong_b, "L0_ffn_on_g"), (onb_b, "L0_ffn_on_b")):
                act.dma_start(t[:], ins[n].partition_broadcast(P)).then_inc(sem("rows_in"), 16)

            def copy(o, i):
                return act.activation(o, i, ACT.Identity)

            act.preload_act_table_set("natural_log_exp_and_others")
            act.wait_ge(sem("a_capped"), 1)
            act.activation(atmp[:], atmp[:], ACT.Exp).then_inc(sem("a_exp"), 1)
            act.wait_ge(sem("a_exp"), 1)
            act.wait_ge(sem("consts"), 6)
            act.activation(atmp[:], atmp[:], ACT.Ln, bias=onec[:]).then_inc(sem("a_ln"), 1)
            for step in A_STEPS:
                if step[0] == "ring":
                    q = step[1]
                    kind, *rest = A_RING[q]
                    ps = bank[q % 4]
                    if kind == "wp":
                        act.wait_ge(sem("a_ps"), q + 1)
                        c = rest[0]
                        copy(WpT[:, c:c + 2, :].rearrange("p c e -> p (c e)"), ps[:]).then_inc(sem("a_read_act"), 1)
                    elif kind == "w":
                        w, dc = rest
                        act.wait_ge(sem("a_ps"), q + 1)
                        copy(WT[w][0][:, dc, :], ps[:]).then_inc(sem("w_hi"), 1)
                    elif kind == "img" and a_reader(q) == "act":
                        act.wait_ge(sem("a_ps"), q + 1)
                        copy(*patches(ps, *rest)).then_inc(sem("a_read_act"), 1)
                    continue
                kind, m = step[0], TILE_ORDER.index(step[1])
                i = step[1]
                if kind == "a1":
                    act.wait_ge(sem("h0_ps"), m + 1)
                    if m >= 3:
                        act.wait_ge(sem(f"h0_stored{m % 3}"), 16 * (m // 3))
                        act.wait_ge(sem("x"), m - 2)
                    copy(h0s[:, m % 3, :], bank[4 + m % 2][:, 0:D]).then_inc(sem("h0_copied"), 1)
                elif kind == "a3":
                    act.wait_ge(sem("mv0"), m + 1)
                    act.activation(sd0[:, i:i + 1], mv0[:, i, 1:2], ACT.Sqrt, bias=epsc[:]).then_inc(sem("sd0"), 1)
                elif kind == "a4":
                    act.wait_ge(sem("xT_ps"), m + 1)
                    copy(xT_hi[:, :, i * P:(i + 1) * P], bank[6 + m % 2][:, 0:D].rearrange("p (c n) -> p c n", c=DC)
                         ).then_inc(sem("xT_hi"), 1)
            act.preload_act_table_set("natural_log_exp_and_others")
            for q in range(HC * NB):
                w = BLOCKS[BLOCK_ORDER[q // HC]][1]
                act.wait_ge(sem("dt_capped"), q + 1)
                act.activation(spt[:, q % 4, 0:w], spt[:, q % 4, 0:w], ACT.Exp).then_inc(sem("dt_exp"), 1)
                if q >= 1:
                    log1p(act, q - 1)
            log1p(act, HC * NB - 1)
            for step in C_STEPS:
                if step[0] == "proj":
                    j = step[1]
                    if j == 0:
                        act.wait_ge(sem("ur_pads"), 2)
                    for nb, (n0, w) in enumerate(BLOCKS):
                        c = j * NB + nb
                        act.wait_ge(sem("u_mm"), c + 1)
                        if j >= 2:
                            act.wait_ge(sem("mixed"), j - 1)
                        copy_b(act, ur[:, j % 2, B + n0:B + n0 + w], bank[c % 2][:, 0:w], vec[:, bx0 + j:bx0 + j + 1]
                               ).then_inc(sem("ur"), 1)
                        act.wait_ge(sem("g_mm"), c + 1)
                        if j >= 2:
                            act.wait_ge(sem("gated"), j - 1)
                        if j == 1:
                            act.wait_ge(sem("zrow_stored"), 64)
                            act.wait_ge(sem("h0_stored0"), 16 * len(range(0, NT, 3)))
                            act.wait_ge(sem("h0_stored1"), 16 * len(range(1, NT, 3)))
                            act.wait_ge(sem("h0_stored2"), 16 * len(range(2, NT, 3)))
                        act.activation(gb[j % 2][:, n0:n0 + w], bank[2 + c % 2][:, 0:w], ACT.Sigmoid,
                                       bias=vec[:, bg0 + j:bg0 + j + 1]).then_inc(sem("gate"), 1)
                    act.wait_ge(sem("ur"), NB * (j + 1))
                    act.wait_ge(sem("cw_in"), 16)
                    if j >= 2:
                        act.wait_ge(sem("c_ps"), 1 + max(q for q, r in enumerate(C_RING) if r[0:2] == ("uT", j - 2)))
                    act.activation(hb[:, j % 2, :], ur[:, j % 2, B:B + N], ACT.Identity, scale=cw[:, j, 1:2],
                                   bias=vec[:, cb0 + j:cb0 + j + 1]).then_inc(sem("h_init"), 1)
                elif step[0] == "kernels":
                    pass
                else:
                    turned(act, step[1], "act")
                if step == ("proj", 0):
                    act.wait_ge(sem("adt"), 1)
                    act.activation(wmix[:], adt[:], ACT.Exp).then_inc(sem("a_d"), 1)
                    for j in range(HC):
                        act.wait_ge(sem("exponent"), j + 1)
                        act.activation(Eb[:, j], Eb[:, j], ACT.Exp).then_inc(sem("powers"), 1)
            for v in range(0, 2 * QN, 2):
                act.wait_ge(sem("ssm_mm"), v + 1)
                copy(y[:, 4 * v:4 * v + 4, :].rearrange("p k t -> p (k t)"), bank[v % 4][:, 0:4 * L]).then_inc(
                    sem("y_act"), 1)
                if v in (16, 18):
                    dc = (v - 16) // 2
                    act.wait_ge(sem("w1g_mult"), dc + 1)
                    copy(w1g_hi[:, :, dc, :], w1p[:, :, dc, :]).then_inc(sem("w1g_hi"), 1)
            for q, (kind, *rest) in enumerate(G_RING):
                ps = bank[4 + q % 4]
                if kind == "wo":
                    act.wait_ge(sem("g_ps"), q + 1)
                    j = 2 * rest[0]
                    copy(WoT[:, j:j + 2, :].rearrange("p j d -> p (j d)"), ps[:]).then_inc(sem("g_read_act"), 1)
                elif kind == "w1T":
                    e, k = rest
                    act.wait_ge(sem("g_ps"), q + 1)
                    if e >= 1:
                        act.wait_ge(sem("g_ps"), q - k)
                    copy(w1cT[:, 2 * k:2 * k + 2, :].rearrange("p j d -> p (j d)"), ps[:]).then_inc(sem("w1T"), 1)
                    act.wait_ge(sem("w1T"), 2 * e + k + 1)
                    act.sem_inc(sem("g_read_act"), 1)
                elif kind == "gram":
                    e = rest[0]
                    act.wait_ge(sem("g_ps"), q + 1)
                    copy(G_hi[:, :, e * D:(e + 1) * D], ps[:].rearrange("p (c d) -> p c d", c=DC)).then_inc(sem("G_hi"), 1)
                if kind == "gram" and rest[0] == 0:
                    act.wait_ge(sem("w2_in"), 16)
                    copy(w2_hi[:], w2raw[:]).then_inc(sem("w2_hi"), 1)
            for kind, *rest in F_STEPS:
                i = rest[0]
                if kind == "yT":
                    act.wait_ge(sem("yT_ps"), i + 1)
                    act.wait_ge(sem("w1g_mult"), DC)
                    act.wait_ge(sem("gram_tr"), E)
                    if i >= 2:
                        act.wait_ge(sem("out_mm"), i - 1)
                    n = AUX.index((kind, i))
                    copy(yT[:, i % 2].rearrange("p j (t b) -> p j t b", b=B),
                         bank[4 + n % 4][:].rearrange("p (t j b) -> p j t b", j=HC, b=B)).then_inc(sem("yT"), 1)
                    act.wait_ge(sem("yT"), i + 1)
                    act.sem_inc(sem("aux_read_act"), 1)
                elif kind == "h1":
                    pass
                elif kind == "ln1":
                    act.wait_ge(sem("mv1"), i + 1)
                    act.activation(sd1[:, i:i + 1], mv1[:, i, 1:2], ACT.Sqrt, bias=epsc[:]).then_inc(sem("sd1"), 1)
                elif kind == "x2":
                    act.wait_ge(sem("mv2"), i + 1)
                    act.activation(sd2[:, i:i + 1], mv2[:, i, 1:2], ACT.Sqrt, bias=epsc[:]).then_inc(sem("sd2"), 1)
                    act.wait_ge(sem("v2n"), i + 1)
                    act.activation(rs2r[:, i:i + 1], v2n[:, i:i + 1], ACT.Sqrt, bias=epsc[:]).then_inc(sem("sdr"), 1)
                elif kind == "x2T":
                    act.wait_ge(sem("x2T_ps"), i + 1)
                    if i == 0:
                        act.wait_ge(sem("Bst"), 1)
                    n = AUX.index((kind, i))
                    copy(x2T_hi[:, i // 2 % 2, :, i % 2 * P:(i % 2 + 1) * P],
                         bank[4 + n % 4][:, 0:D].rearrange("p (c n) -> p c n", c=DC)).then_inc(sem("x2T_hi"), 1)
                elif kind == "std":
                    act.wait_ge(sem("varE"), E * (i + 1))
                    act.activation(stdE[:, i, :], varE[:, i, :], ACT.Sqrt, bias=epsc[:], scale=1.0 / HF).then_inc(
                        sem("stdE"), 1)
                elif kind == "stdT":
                    act.wait_ge(sem("stdT_ps"), i + 1)
                    act.wait_ge(sem("std_zero"), 2)
                    n = AUX.index((kind, i))
                    copy(stdT[0:3 * E, i // 2 % 2, i % 2 * P:(i % 2 + 1) * P], bank[4 + n % 4][0:3 * E, 0:P]).then_inc(
                        sem("stdT"), 1)
                    act.wait_ge(sem("stdT"), i + 1)
                    act.sem_inc(sem("aux_read_act"), 1)
                elif kind == "route1":
                    act.wait_ge(sem("logit_rel"), i + 1)
                    ts = slice(FB[i][0], FB[i][-1] + 1)
                    act.activation(gx[:, ts, :], gx[:, ts, :], ACT.Exp).then_inc(sem("gexp"), 1)
                elif kind == "hid":
                    b, e, k = rest
                    q, w = hid_job(b, e, k), P * len(FB[b])
                    act.wait_ge(sem("hid_mm"), q + 1)
                    if b * E + e >= 2:
                        act.wait_ge(sem("w2_mm"), b * E + e - 1)
                    act.activation(hid_hi[:, e % 2, 2 * k:2 * k + 2, 0:w],
                                   bank[q % 2][:].rearrange("p (c n) -> p c n", c=2)[:, :, 0:w], ACT.Relu).then_inc(
                                       sem("hid_hi"), 1)
                elif kind == "fin2":
                    for i in FB[rest[0]]:
                        act.wait_ge(sem("mv3"), i + 1)
                        act.activation(sd3[:, i:i + 1], mv3[:, i, 1:2], ACT.Sqrt, bias=epsc[:]).then_inc(sem("sd3"), 1)

        @block.vector
        def _(dve):
            linked = [0]

            def link(ins_):
                linked[0] += 1
                ins_.then_inc(sem("dve_link"), 1)
                dve.wait_ge(sem("dve_link"), linked[0])

            def signal(ins_, name, n):
                ins_.then_inc(sem(name), 1)
                dve.wait_ge(sem(name), n)

            dve.wait_ge(sem("tok_in"), 16)
            dve.wait_ge(sem("consts"), 6)
            jp = tf[:, 7, :]
            link(dve.tensor_copy(tf[:, 0, :], tok[:]))
            link(dve.tensor_scalar(tf[:, 1, :], tf[:, 0, :], 1.0, None, ALU.not_equal))
            link(dve.tensor_tensor_scan(tf[:, 2, :], tf[:, 1, :], tf[:, 1, :], 1.0, ALU.mult, ALU.mult))
            link(dve.scalar_tensor_tensor(tf[:, 3, :], tf[:, 0, :], 4.0, jp, ALU.is_equal, ALU.mult))
            link(dve.tensor_tensor_scan(tf[:, 4, :], tf[:, 3, :], tf[:, 3, :], 0.0, ALU.max, ALU.max))
            link(dve.tensor_tensor(tf[:, 5, :], jp, tf[:, 4, :], ALU.subtract))
            link(dve.scalar_tensor_tensor(tf[:, 6, :], tf[:, 5, :], 1.0, tf[:, 2, :], ALU.add, ALU.mult))
            link(dve.tensor_scalar(tf[:, 5, :], tf[:, 6, :], 1.0, None, ALU.add))
            dve.wait_ge(sem("ident"), 1)
            dve.tensor_tensor(posD[:], tf[:, 5, :].rearrange("p (j o) -> p j o", o=1).broadcast_to([B, LT, B]),
                              ident[0:B, 0:B].rearrange("p (o b) -> p o b", o=1).broadcast_to([B, LT, B]),
                              ALU.mult).then_inc(sem("pos_spread"), 1)
            dve.memset(ones_b[:], 1.0).then_inc(sem("pos_spread"), 1)
            dve.wait_ge(sem("araw_in"), 16)
            dve.tensor_scalar(atmp[:], araw[:], 40.0, None, ALU.min).then_inc(sem("a_capped"), 1)
            dve.wait_ge(sem("bcs_in"), 64)
            dve.tensor_tensor(posb[:], posb[:], bpb[:], ALU.add).then_inc(sem("posb"), 1)
            dve.tensor_copy(sel[:], ident[0:LI, 0:LI].rearrange("p (t o) -> p t o", o=1).broadcast_to([LI, LI, B])
                            ).then_inc(sem("posb"), 1)
            for step in A_STEPS:
                if step[0] == "ring":
                    q = step[1]
                    kind, *rest = A_RING[q]
                    ps = bank[q % 4]
                    if a_reader(q) != "dve":
                        continue
                    dve.wait_ge(sem("a_ps"), q + 1)
                    if kind == "vec":
                        dve.tensor_copy(vec[:, 0:NV], ps[:, 0:NV]).then_inc(sem("a_read_dve"), 1)
                    elif kind == "pos":
                        k = rest[0]
                        dve.wait_ge(sem("consts"), 6)
                        signal(dve.tensor_scalar(OH[:, k * 512:(k + 1) * 512], ps[0:LT + 2, :], rowid[0:LT + 2, :], None,
                                                 ALU.is_equal), "onehot", k + 1)
                        dve.sem_inc(sem("a_read_dve"), 1)
                    elif kind == "w":
                        w, dc = rest
                        dve.wait_ge(sem("w_hi"), w * DC + dc + 1)
                        dve.tensor_tensor(WT[w][1][:, dc, :], ps[:], WT[w][0][:, dc, :].bitcast(F32), ALU.subtract
                                          ).then_inc(sem("a_read_dve"), 1)
                    else:
                        dve.tensor_copy(*patches(ps, *rest)).then_inc(sem("a_read_dve"), 1)
                    continue
                kind, i = step
                m = TILE_ORDER.index(i)
                if kind == "a2":
                    dve.wait_ge(sem("h0_copied"), m + 1)
                    link(dve.bn_stats(bst[:], h0s[:, m % 3, :]))
                    signal(dve.bn_aggr(mv0[:, i, :], bst[:]), "mv0", m + 1)
                elif kind == "a3":
                    dve.wait_ge(sem("sd0"), m + 1)
                    link(dve.reciprocal(rs0[:, i:i + 1], sd0[:, i:i + 1]))
                    if m >= 2:
                        dve.wait_ge(sem("xT_ps"), m - 1)
                    dve.tensor_scalar(xs[:, m % 2, :], h0s[:, m % 3, :], mv0[:, i, 0:1], rs0[:, i:i + 1], ALU.subtract,
                                      ALU.mult).then_inc(sem("x"), 1)
                elif kind == "a4":
                    dve.wait_ge(sem("xT_hi"), m + 1)
                    dve.tensor_tensor(xT_lo[:, :, i * P:(i + 1) * P],
                                      bank[6 + m % 2][:, 0:D].rearrange("p (c n) -> p c n", c=DC),
                                      xT_hi[:, :, i * P:(i + 1) * P].bitcast(F32), ALU.subtract).then_inc(sem("xT"), 1)
            dve.wait_ge(sem("x"), NT)
            dve.scalar_tensor_tensor(nmr0[:], mv0[:, :, 0], -1.0, rs0[:], ALU.mult, ALU.mult).then_inc(sem("nmr0"), 1)
            dve.wait_ge(sem("a_ln"), 1)
            link(dve.tensor_tensor(amat[:], araw[:], atmp[:], ALU.max))
            link(dve.tensor_scalar(amat[:], amat[:], -1.0, None, ALU.mult))
            link(dve.tensor_scalar(winv[:], amat[:], 1e-6, None, ALU.add))
            link(dve.reciprocal(winv[:], winv[:]))
            dve.wait_ge(sem("xT_ps"), NT)
            for q in range(HC * NB + 2):
                if q < HC * NB:
                    w, j = BLOCKS[BLOCK_ORDER[q // HC]][1], q % HC
                    dve.wait_ge(sem("dt_mm"), q + 1)
                    dve.tensor_scalar(spt[:, q % 4, 0:w], bank[q % 4][:, 0:w], vec[:, bdt0 + j:bdt0 + j + 1], 40.0,
                                      ALU.add, ALU.min).then_inc(sem("dt_capped"), 1)
                if q >= 2:
                    k = q - 2
                    w, j = BLOCKS[BLOCK_ORDER[k // HC]][1], k % HC
                    dve.wait_ge(sem("dt_ln"), k + 1)
                    if k >= 2:
                        dve.wait_ge(sem("dt_read"), k - 1)
                    dve.scalar_tensor_tensor(spj[:, k % 2, 0:w], bank[k % 4][:, 0:w], vec[:, bdt0 + j:bdt0 + j + 1],
                                             spt[:, k % 4, 0:w], ALU.add, ALU.max,
                                             accum_out=dts[:, j, k // HC:k // HC + 1]).then_inc(sem("dt_read"), 1)
            dve.wait_ge(sem("dt_read"), HC * NB)
            link(dve.reduce_sum(dt1[:], dts[:], AX))
            link(dve.tensor_scalar(dtc[:], dt1[:], 1.0 / N, 0.001, ALU.mult, ALU.max))
            link(dve.tensor_scalar(dt1[:], dtc[:], 2.0, None, ALU.min))
            dve.tensor_tensor(adt[:], amat[:], dt1[:].rearrange("p (c o) -> p c o", o=1).broadcast_to([P, HC, S]),
                              ALU.mult).then_inc(sem("adt"), 1)
            who, n = a_read(len(A_RING) - 2)
            dve.wait_ge(sem("a_ps"), len(A_RING))
            for k in range(2):
                dve.memset(ur[:, k].rearrange("p (a c) -> p a c", c=B)[:, ::N // B + 1, :], 0.0).then_inc(
                    sem("ur_pads"), 1)
            mixed = 0
            for step in C_STEPS:
                if step[0] == "proj":
                    j = step[1]
                    dve.wait_ge(sem("h_init"), j + 1)
                    u, h = ur[:, j % 2], hb[:, j % 2, :]
                    link(dve.scalar_tensor_tensor(h, u[:, 0:N], cw[:, j, 0:1], h, ALU.mult, ALU.add))
                    dve.scalar_tensor_tensor(h, u[:, 2 * B:2 * B + N], cw[:, j, 2:3], h, ALU.mult, ALU.add).then_inc(
                        sem("conv"), 1)
                elif step[0] == "turn":
                    turned(dve, step[1], "dve")
                else:
                    q = C_RING.index(("kT",))
                    dve.wait_ge(sem("c_ps"), q + 1)
                    dve.tensor_copy(kt[:].rearrange("k q j h -> k j q h"),
                                    bank[4 + q % 4][0:L, :].rearrange("k (j q h) -> k j q h", j=HC, h=QH)).then_inc(
                                        sem("kt_ready"), 1)
                    dve.wait_ge(sem("kt_ready"), 1)
                    dve.sem_inc(sem("c_read_dve"), 1)
                if step == ("proj", 0):
                    dve.wait_ge(sem("a_d"), 1)
                    link(dve.scalar_tensor_tensor(wmix[:], wmix[:], 1.0, winv[:], ALU.subtract, ALU.mult))
                    link(dve.tensor_tensor(wmix[:], wmix[:], bcs[:, 0], ALU.mult))
                    link(dve.tensor_tensor(wmix[:], wmix[:], bcs[:, 1], ALU.mult))
                    for j in range(HC):
                        dve.wait_ge(sem("powers"), j + 1)
                        signal(dve.tensor_tensor(Eb[:, j], Eb[:, j],
                                                 wmix[:, j].rearrange("p (o s) -> p o s", o=1).broadcast_to([P, L, S]),
                                                 ALU.mult), "power_w", j + 1)
                        signal(dve.reduce_sum(Kk[:, j, :], Eb[:, j], AX), "kernel_sum", j + 1)
                if step in (("proj", 1), ("turn", 0), ("turn", 1), ("turn", 2)) :
                    j = {("proj", 1): 0, ("turn", 0): 1, ("turn", 1): 2, ("turn", 2): 3}[step]
                    mixed += 1
                    assert mixed == j + 1
                    dve.wait_ge(sem("gated"), j + 1)
                    h = hb[:, j % 2, :]
                    dve.tensor_tensor(h, h, ur[:, j % 2, B:B + N], ALU.add).then_inc(sem("mixed"), 1)
            for v in range(1, 2 * QN, 2):
                dve.wait_ge(sem("ssm_mm"), v + 1)
                dve.tensor_copy(y[:, 4 * v:4 * v + 4, :].rearrange("p k t -> p (k t)"), bank[v % 4][:, 0:4 * L]).then_inc(
                    sem("y_dve"), 1)
                if v == 7:
                    dve.wait_ge(sem("w1_in"), 16)
                    link(dve.reduce_sum(w1m[:], w1c[:].rearrange("p e c h -> p (e c) h"), AX))
                    link(dve.tensor_scalar(w1m[:], w1m[:], -1.0 / HF, None, ALU.mult))
                if v in (9, 11, 13, 15):
                    e = (v - 9) // 2
                    for dc in range(DC):
                        k = e * DC + dc
                        dve.tensor_scalar(w1c[:, e, dc, :], w1c[:, e, dc, :], w1m[:, k:k + 1], None, ALU.add).then_inc(
                            sem("w1_centred"), 1)
                if v in (23, 25):
                    dc = (v - 23) // 2
                    dve.wait_ge(sem("w1g_hi"), dc + 1)
                    dve.tensor_tensor(w1g_lo[:, :, dc, :], w1p[:, :, dc, :], w1g_hi[:, :, dc, :].bitcast(F32),
                                      ALU.subtract).then_inc(sem("w1g_split"), 1)
            for q, (kind, *rest) in enumerate(G_RING):
                ps = bank[4 + q % 4]
                if kind == "rw":
                    dve.wait_ge(sem("g_ps"), q + 1)
                    signal(dve.tensor_copy(rwT[:].rearrange("p c e -> p (c e)"), ps[:, 0:DC * E]), "rwT", 1)
                    dve.sem_inc(sem("g_read_dve"), 1)
                    for dc in range(DC):
                        dve.tensor_copy(zjunk[:, dc * P:(dc + 1) * P],
                                        vec[:, rnb0 + dc:rnb0 + dc + 1].broadcast_to([P, P])).then_inc(
                                            sem("rnb_spread"), 1)
                        link(dve.tensor_scalar(rg[:, dc, :], rwT[:, dc, :], vec[:, rng0 + dc:rng0 + dc + 1], None,
                                               ALU.mult))
                    signal(dve.tensor_copy(rg_hi[:], rg[:]), "router_split", 1)
                    dve.tensor_tensor(rg_lo[:], rg[:], rg_hi[:].bitcast(F32), ALU.subtract).then_inc(
                        sem("router_split"), 1)
                elif kind == "cbc":
                    dve.wait_ge(sem("g_ps"), q + 1)
                    dve.tensor_copy(cbc[:], ps[:, 0:E]).then_inc(sem("g_read_dve"), 1)
                elif kind == "gram":
                    e = rest[0]
                    dve.wait_ge(sem("G_hi"), e + 1)
                    dve.tensor_tensor(G_lo[:, :, e * D:(e + 1) * D], ps[:].rearrange("p (c d) -> p c d", c=DC),
                                      G_hi[:, :, e * D:(e + 1) * D].bitcast(F32), ALU.subtract).then_inc(
                                          sem("g_read_dve"), 1)
                    if e == 0:
                        dve.wait_ge(sem("lb_in"), 16)
                        dve.wait_ge(sem("std_zero"), 2)
                        dve.wait_ge(sem("mAB"), 4)
                        dve.wait_ge(sem("m12"), 4)
                        b12 = Bst[0:12]
                        link(dve.tensor_copy(b12, lb12[:]))
                        link(dve.tensor_tensor(lb12[:], lb12[:], b12.bitcast(F32), ALU.subtract))
                        link(dve.tensor_scalar(lb12[:], lb12[:], mB[:], None, ALU.mult))
                        link(dve.scalar_tensor_tensor(b12.rearrange("p e h -> p (e h)"),
                                                      b12.bitcast(F32).rearrange("p e h -> p (e h)"), mA[:],
                                                      lb12[:].rearrange("p e h -> p (e h)"), ALU.mult, ALU.add))
                        for k in range(E):
                            last = dve.tensor_scalar(b12[:, k, :], b12[:, k, :].bitcast(F32), m12[:, k:k + 1], None,
                                                     ALU.mult)
                            if k < E - 1:
                                link(last)
                        last.then_inc(sem("Bst"), 1)
                    if e == 1:
                        dve.wait_ge(sem("w2_hi"), 1)
                        for k in range(2):
                            es = slice(2 * k, 2 * k + 2)
                            dve.tensor_tensor(w2_lo[:, es], w2raw[:, es], w2_hi[:, es].bitcast(F32), ALU.subtract
                                              ).then_inc(sem("w2_split"), 1)
            for kind, *rest in F_STEPS:
                i = rest[0]
                if kind == "out":
                    n = AUX.index((kind, i))
                    dve.wait_ge(sem("out_mm"), i + 1)
                    dve.wait_ge(sem("xb"), i + 1)
                    signal(dve.tensor_tensor(r1[:, i % 2, :], bank[4 + n % 4][:, 0:D], xb[:, i % 2, :], ALU.add), "r1", i + 1)
                    dve.sem_inc(sem("aux_read_dve"), 1)
                    link(dve.bn_stats(bst1[:], r1[:, i % 2, :]))
                    signal(dve.bn_aggr(mv1[:, i, :], bst1[:]), "mv1", i + 1)
                elif kind == "ln1":
                    dve.wait_ge(sem("sd1"), i + 1)
                    link(dve.reciprocal(rs1[:, i:i + 1], sd1[:, i:i + 1]))
                    r = r1[:, i % 2, :]
                    link(dve.tensor_scalar(r, r, mv1[:, i, 0:1], rs1[:, i:i + 1], ALU.subtract, ALU.mult))
                    link(dve.tensor_tensor(r, r, lng_b[:], ALU.mult))
                    dve.wait_ge(sem("h0b"), i + 1)
                    signal(dve.tensor_tensor(h1[:, i, :], r, h0r[:, i % 2, :], ALU.add), "h1", i + 1)
                elif kind == "h1":
                    link(dve.bn_stats(bst2[:], h1[:, i, :]))
                    signal(dve.bn_aggr(mv2[:, i, :], bst2[:]), "mv2", i + 1)
                elif kind == "x2":
                    dve.wait_ge(sem("sd2"), i + 1)
                    link(dve.reciprocal(rs2[:, i:i + 1], sd2[:, i:i + 1]))
                    link(dve.tensor_scalar(v2n[:, i:i + 1], mv2[:, i, 1:2], rs2[:, i:i + 1], rs2[:, i:i + 1], ALU.mult,
                                           ALU.mult))
                    dve.sem_inc(sem("v2n"), 1)
                    if i >= 2:
                        dve.wait_ge(sem("x2T_ps"), i - 1)
                        dve.wait_ge(sem("varE"), E * (i - 1))
                    dve.tensor_scalar(x2s[:, i % 2, :], h1[:, i, :], mv2[:, i, 0:1], rs2[:, i:i + 1], ALU.subtract,
                                      ALU.mult).then_inc(sem("x2"), 1)
                    dve.wait_ge(sem("sdr"), i + 1)
                    link(dve.reciprocal(rs2r[:, i:i + 1], rs2r[:, i:i + 1]))
                elif kind == "x2T":
                    n = AUX.index((kind, i))
                    ts = slice(i % 2 * P, (i % 2 + 1) * P)
                    dve.wait_ge(sem("x2T_hi"), i + 1)
                    signal(dve.tensor_tensor(x2T_lo[:, i // 2 % 2, :, ts],
                                             bank[4 + n % 4][:, 0:D].rearrange("p (c n) -> p c n", c=DC),
                                             x2T_hi[:, i // 2 % 2, :, ts].bitcast(F32), ALU.subtract), "x2T", i + 1)
                    dve.sem_inc(sem("aux_read_dve"), 1)
                elif kind in ("z0", "z1"):
                    if kind == "z0":
                        n = AUX.index(("lg", i))
                        dve.wait_ge(sem("logit_mm"), i + 1)
                        signal(dve.scalar_tensor_tensor(lg[:, i, :], bank[4 + n % 4][:, 0:E], rs2r[:, i:i + 1], cbc[:],
                                                        ALU.mult, ALU.add), "logits", i + 1)
                        dve.sem_inc(sem("aux_read_dve"), 1)
                    n = AUX.index((kind, i))
                    half = int(kind == "z1")
                    dve.wait_ge(sem("z_mm"), z_count(kind, i))
                    for k in range(2):
                        e = 2 * half + k
                        signal(dve.tensor_tensor_reduce(zjunk[:], bank[4 + n % 4][:, k * D:(k + 1) * D], x2s[:, i % 2, :],
                                                        1.0, 0.0, ALU.mult, ALU.add, varE[:, i, e:e + 1]),
                               "varE", var_count(kind, i) - 1 + k)
                    dve.sem_inc(sem("aux_read_dve"), 1)
                elif kind == "std":
                    dve.wait_ge(sem("stdE"), i + 1)
                    dve.reciprocal(rstE[:, i, :], stdE[:, i, :]).then_inc(sem("rstE"), 1)
                    if i >= 2:
                        dve.wait_ge(sem("stdT_ps"), i - 1)
                    s = s3[:, i % 2]
                    signal(dve.tensor_copy(s[:, 0, :], stdE[:, i, :]), "s3", 3 * i + 1)
                    dve.tensor_tensor(s[:, 1, :], stdE[:, i, :], s[:, 0, :].bitcast(F32), ALU.subtract).then_inc(
                        sem("s3"), 1)
                    dve.tensor_copy(s[:, 2, :], s[:, 0, :].bitcast(F32)).then_inc(sem("s3"), 1)
                elif kind == "route1":
                    t0, t1 = FB[i][0], FB[i][-1] + 1
                    ts, w = slice(t0, t1), t1 - t0
                    dve.wait_ge(sem("logits"), t1)
                    link(dve.tensor_reduce(rsum[:, ts], lg[:, ts, :], AX, ALU.max))
                    dve.tensor_tensor(gx[:, ts, :], lg[:, ts, :], spread(rsum[:, ts], w), ALU.subtract).then_inc(
                        sem("logit_rel"), 1)
                elif kind == "route2":
                    t0, t1 = FB[i][0], FB[i][-1] + 1
                    ts, w = slice(t0, t1), t1 - t0
                    dve.wait_ge(sem("gexp"), i + 1)
                    g, rk, cp = gx[:, ts, :], rank[:, ts, :], cmp[:, ts, :]
                    link(dve.reduce_sum(rsum[:, ts], g, AX))
                    link(dve.reciprocal(rsum[:, ts], rsum[:, ts]))
                    link(dve.tensor_tensor(g, g, spread(rsum[:, ts], w), ALU.mult))
                    dve.wait_ge(sem("consts"), 6)
                    link(dve.tensor_copy(rk, eid[:].rearrange("p (o e) -> p o e", o=1).broadcast_to([P, w, E])))
                    for d in range(1, E):
                        link(dve.tensor_tensor(cp[:, :, 0:E - d], g[:, :, d:E], g[:, :, 0:E - d], ALU.is_gt))
                        link(dve.tensor_tensor(rk[:, :, 0:E - d], rk[:, :, 0:E - d], cp[:, :, 0:E - d], ALU.add))
                        link(dve.tensor_tensor(rk[:, :, d:E], rk[:, :, d:E], cp[:, :, 0:E - d], ALU.subtract))
                    link(dve.scalar_tensor_tensor(cp, rk, 2.0, g, ALU.is_lt, ALU.mult))
                    link(dve.reduce_sum(rsum[:, ts], cp, AX))
                    link(dve.tensor_scalar(rsum[:, ts], rsum[:, ts], 1e-8, None, ALU.add))
                    link(dve.reciprocal(rsum[:, ts], rsum[:, ts]))
                    link(dve.tensor_tensor(cp, cp, spread(rsum[:, ts], w), ALU.mult))
                    dve.wait_ge(sem("rstE"), t1)
                    signal(dve.tensor_tensor(wE[:, ts, :], cp, rstE[:, ts, :], ALU.mult), "wE", i + 1)
                elif kind == "hid":
                    b, e, k = rest
                    q, w = hid_job(b, e, k), P * len(FB[b])
                    dve.wait_ge(sem("hid_hi"), q + 1)
                    hs = slice(2 * k, 2 * k + 2)
                    dve.scalar_tensor_tensor(hid_lo[:, e % 2, hs, 0:w],
                                             bank[q % 2][:].rearrange("p (c n) -> p c n", c=2)[:, :, 0:w], 0.0,
                                             hid_hi[:, e % 2, hs, 0:w].bitcast(F32), ALU.max, ALU.subtract).then_inc(
                                                 sem("hid_lo"), 1)
                elif kind == "w2":
                    b, e = rest
                    q = b * E + e
                    dve.wait_ge(sem("w2_mm"), q + 1)
                    if e:
                        dve.wait_ge(sem("combined"), q)
                    for n, i in enumerate(FB[b]):
                        a, ps = acc[:, b % 2, n, :], bank[2 + q % 2][:, n * D:(n + 1) * D]
                        if e == 0:
                            if i >= 4:
                                dve.wait_ge(sem(f"out_stored{i % 4}"), 16 * (i // 4))
                            last = dve.tensor_scalar(a, ps, wE[:, i, 0:1], None, ALU.mult)
                        else:
                            last = dve.scalar_tensor_tensor(a, ps, wE[:, i, e:e + 1], a, ALU.mult, ALU.add)
                    last.then_inc(sem("combined"), 1)
                elif kind == "fin1":
                    dve.wait_ge(sem("combined"), E * (i + 1))
                    for n, t in enumerate(FB[i]):
                        link(dve.bn_stats(bst3[:], acc[:, i % 2, n, :]))
                        signal(dve.bn_aggr(mv3[:, t, :], bst3[:]), "mv3", t + 1)
                elif kind == "fin2":
                    for n, t in enumerate(FB[i]):
                        a = acc[:, i % 2, n, :]
                        dve.wait_ge(sem("sd3"), t + 1)
                        link(dve.reciprocal(rs3[:, t:t + 1], sd3[:, t:t + 1]))
                        link(dve.tensor_scalar(a, a, mv3[:, t, 0:1], rs3[:, t:t + 1], ALU.subtract, ALU.mult))
                        link(dve.tensor_tensor(a, a, ong_b[:], ALU.mult))
                        dve.wait_ge(sem("h1b"), t + 1)
                        dve.tensor_tensor(a, a, h1[:, t, :], ALU.add).then_inc(sem("result"), 1)



def kernel(**inputs):
    import concourse.bacc as _bacc
    from concourse.bass_utils import run_bass_kernel_spmd as _run
    import numpy as _np

    nc = _bacc.Bacc("TRN2", target_bir_lowering=False, num_devices=1)
    arrays, ins = {}, {}
    for name, value in inputs.items():
        a = _np.ascontiguousarray(value)
        arrays[f"in_{name}_dram"] = a
        ins[name] = nc.dram_tensor(f"in_{name}_dram", a.shape, mybir.dt.from_np(a.dtype), kind="ExternalInput").ap()
    batch, seq = inputs["x"].shape[0], 36 + inputs["x_txt"].shape[1]
    out = nc.dram_tensor("out_0_dram", (batch, seq, inputs["L0_tok_W_proj"].shape[0]), F32, kind="ExternalOutput").ap()
    build_kernel(nc, ins, out)
    r = _run(nc, [arrays], core_ids=[0])
    return r.results[0]["out_0_dram"]
```

```python
from contextlib import ExitStack

import concourse.bass as bass
from concourse import mybir

F32 = mybir.dt.float32
F32R = mybir.dt.float32r
I32 = mybir.dt.int32
ALU = mybir.AluOpType
ACT = mybir.ActivationFunctionType
AX = mybir.AxisListType.X
P = 128


def build_kernel(nc, ins, out):
    B, IMG, _, CH = ins["x"].shape
    LT = ins["x_txt"].shape[1]
    D, PD = ins["L0_tok_W_proj"].shape
    PS = 16
    HP = IMG // PS
    LI = HP * HP
    L = LI + LT
    H, S = ins["L0_attn_A_raw"].shape
    E, _, HF = ins["L0_ffn_w1"].shape
    N = L * B
    NT = N // P
    TPT = P // B
    NTI = LI // TPT
    DC, HC = D // P, H // P
    EPS = 1e-5
    BLOCKS = [(n, min(512, N - n)) for n in range(0, N, 512)]
    NB = len(BLOCKS)
    GB = B // 2
    ROWS = GB * HP
    CK = PD // P
    KT = CK // 2
    PWC = PS * CH
    QN, QH = 16, H // HC // 16
    QC = QH * HC

    stack = ExitStack()
    with stack:
        def sb(name, shape, dt=F32):
            return stack.enter_context(nc.sbuf_tensor(name, shape, dt))

        sems = {}

        def sem(name):
            if name not in sems:
                sems[name] = stack.enter_context(nc.semaphore(name))
            return sems[name]

        ident = sb("ident", [P, P])
        vec_rows = sb("vec_rows", [52, P])
        vec = sb("vec", [P, 52])
        cw = sb("cw", [P, HC, 3])
        c1 = sb("c1", [P, HC])
        araw = sb("araw", [P, HC, S])
        bcs = sb("bcs", [P, 2, HC, S])
        amat = sb("amat", [P, HC, S])
        atmp = sb("atmp", [P, HC, S])
        adt = sb("adt", [P, HC, S])
        wmix = sb("wmix", [P, HC, S])
        winv = sb("winv", [P, HC, S])
        kio = sb("kio", [P, L])
        rowid = sb("rowid", [P, 1])
        mv0 = sb("mv0", [P, NT, 2])
        sd0 = sb("sd0", [P, NT])
        rs0 = sb("rs0", [P, NT])
        nmr0 = sb("nmr0", [P, NT])
        bst = sb("bst", [P, 6])
        bst1 = sb("bst1", [P, 2, 6])
        bst2 = sb("bst2", [P, 2, 6])
        bst3 = sb("bst3", [P, 2, 6])
        mv1 = sb("mv1", [P, NT, 2])
        sd1 = sb("sd1", [P, NT])
        rs1 = sb("rs1", [P, NT])
        mv2 = sb("mv2", [P, NT, 2])
        sd2 = sb("sd2", [P, NT])
        rs2 = sb("rs2", [P, NT])
        v2n = sb("v2n", [P, NT])
        rs2r = sb("rs2r", [P, NT])
        ones_b = sb("ones_b", [B, LT + 2])
        mv3 = sb("mv3", [P, NT, 2])
        sd3 = sb("sd3", [P, NT])
        rs3 = sb("rs3", [P, NT])
        epsc = sb("epsc", [P, 1])
        onec = sb("onec", [P, 1])
        dts = sb("dts", [P, HC, NB])
        dt1 = sb("dt1", [P, HC])
        dtc = sb("dtc", [P, HC])
        rwT = sb("rwT", [P, DC, E])
        rg = sb("rg", [P, DC, E])
        rg_hi = sb("rg_hi", [P, DC, E], F32R)
        rg_lo = sb("rg_lo", [P, DC, E], F32R)
        cbc = sb("cbc", [P, E])
        bout_b = sb("bout_b", [P, D])
        lng_b = sb("lng_b", [P, D])
        lnb_b = sb("lnb_b", [P, D])
        ong_b = sb("ong_b", [P, D])
        onb_b = sb("onb_b", [P, D])
        varE = sb("varE", [P, NT, E])
        stdE = sb("stdE", [P, NT, E])
        s3 = sb("s3", [P, 2, 3, E], F32R)
        lg = sb("lg", [P, NT, E])
        gx = sb("gx", [P, NT, E])
        rank = sb("rank", [P, NT, E])
        top = sb("top", [P, NT, E])
        pair = sb("pair", [P, 2, 6])
        rsum = sb("rsum", [P, NT])
        wE = sb("wE", [P, NT, E])
        eid = sb("eid", [P, E])
        m12 = sb("m12", [12, E])
        mA = sb("mA", [12, 1])
        mB = sb("mB", [12, 1])
        w1m = sb("w1m", [P, E * DC])

        base = (nc.sbuf_base + 63) // 64 * 64

        def at(name, shape, offset, dt=F32):
            return nc.alloc_sbuf_tensor_at(name, shape, dt, offset=offset)

        def size(*shape):
            n = 4
            for s in shape:
                n *= s
            return (n + 63) // 64 * 64

        def place(start, end, *wanted):
            got = []
            for name, shape, *dt in wanted:
                got.append(at(name, shape, start, *dt))
                start += size(*shape[1:])
            assert start <= end, (wanted[-1][0], start, end)
            return got

        R1 = base
        R2 = R1 + 2 * size(DC, N)
        R3 = R2 + 6 * size(DC, H)
        R4 = R3 + size(5 * N + 4 * B)
        R5 = R4 + size(H * B)
        R6 = R5 + 3 * size(L * QC)
        TOP = nc.sbuf_usable_end

        xT_hi, xT_lo = place(R1, R2, ("xT_hi", [P, DC, N], F32R), ("xT_lo", [P, DC, N], F32R))
        y = at("y", [P, H // HC, L], R1)
        WT = place(R2, R3, *[(f"WT{w}_{v}", [P, DC, H], F32R) for w in ("dt", "x", "g") for v in ("hi", "lo")])
        WT = [WT[0:2], WT[2:4], WT[4:6]]
        w1c, gfb = place(R2, R3, ("w1c", [P, E, DC, HF]), ("gfb", [P, E, HF]))
        h0r, xb, r1, x2s, yT, acc = place(R2, R2 + size(E, DC, HF), ("h0r", [P, 2, D]), ("xb", [P, 2, D]),
                                          ("r1", [P, 2, D]), ("x2s", [P, 2, D]), ("yT", [P, 2, HC, P]), ("acc", [P, 2, 2, D]))
        (w1p,) = place(R3 + size(E, DC, HF), R4, ("w1p", [P, E, DC, HF]))
        (Bst,) = place(R2 + size(E, DC, HF), R3, ("Bst", [P, E, HF], F32R))
        (XI,) = place(R3, R4, ("XI", [ROWS, 2, HP, PD]))
        ur, hb, gb0 = place(R3, R4, ("ur", [P, 2, N + 2 * B]), ("hb", [P, 2, N]), ("gb0", [P, N]))
        w1g_hi, w1g_lo, x2T_hi, x2T_lo, stdT = place(
            R3, R4, ("w1g_hi", [P, E, DC, HF], F32R), ("w1g_lo", [P, E, DC, HF], F32R),
            ("x2T_hi", [P, 2, DC, 2 * P], F32R), ("x2T_lo", [P, 2, DC, 2 * P], F32R), ("stdT", [P, 2, 2 * P], F32R))
        patchT, WpT, Wpr, Wr0, Wr1, Wr2, posD = place(
            R4, R5, ("patchT", [P, CK, LI, B]), ("WpT", [P, CK, D]), ("Wpr", [P, DC, PD]), ("Wr0", [P, HC, D]),
            ("Wr1", [P, HC, D]), ("Wr2", [P, HC, D]), ("posD", [B, LT, B]))
        Wr = [Wr0, Wr1, Wr2]
        spt, spj = place(R4, R5, ("spt", [P, 4, 512]), ("spj", [P, 2, 512]))
        (U2,) = place(R4, R5, ("U2", [L, HC, H // HC, B]))
        w2_hi, w2_lo, hid_hi, hid_lo, G_hi, G_lo = place(
            R4, R5, ("w2_hi", [P, E, HC, D], F32R), ("w2_lo", [P, E, HC, D], F32R),
            ("hid_hi", [P, 2, HC, 2 * P], F32R), ("hid_lo", [P, 2, HC, 2 * P], F32R),
            ("G_hi", [P, DC, E * D], F32R), ("G_lo", [P, DC, E * D], F32R))
        _, w2raw, Wor, _, _ = place(R4, R5, ("_w2", [P, E, HC, D]), ("w2raw", [P, E, HC, D]), ("Wor", [P, DC, H]),
                                    ("_h", [P, HC, 2 * P]), ("_h2", [P, HC, 2 * P]))
        OH, tabl, posb, bpb, sel, h0s, xs, tok, tf, zrow = place(
            R5, R6, ("OH", [LT + 2, LT * B]), ("tabl", [LT + 2, D]), ("posb", [LI, D]), ("bpb", [LI, D]),
            ("sel", [LI, LI, B]), ("h0s", [P, 3, D]), ("xs", [P, 2, D]), ("tok", [B, LT], I32), ("tf", [B, 8, LT]),
            ("zrow", [QN, (L - 1) * QC // 4]))
        Eb, gb1 = place(R5, R6, ("Eb", [P, HC, L, S]), ("gb1", [P, N]))
        gb = [gb0, gb1]
        Tb = place(R5, R6, *[(f"Tb{i}", [L, L, QC]) for i in range(3)])
        h1, WoT, w1cT = place(R5, R6, ("h1", [P, NT, D]), ("WoT", [P, HC, D]), ("w1cT", [P, HC, D]))
        zjunk, rwt = place(R6, TOP, ("zjunk", [P, 2, D]), ("rwt", [E, D]))
        (Kk,) = place(R6, TOP, ("Kk", [P, HC, L]))
        (kt,) = place(R6, TOP, ("kt", [L, QN, HC, QH]))
        (lb12,) = place(R3 + size(E, DC, HF) * 2, R4, ("lb12", [12, E, HF]))

        h0d = nc.dram_tensor("h0_spill", [NT, P, D], F32).ap()
        kpd = nc.dram_tensor("ssm_kernels", [QN, 2 * L - 1, QC], F32).ap()
        bank = [stack.enter_context(nc.psum_tensor(f"bank{i}", [P, 512], F32)) for i in range(8)]

        x = ins["x"]
        img = x.rearrange("(g b) (hp py) w c -> g (b hp) py (w c)", g=2, py=PS)
        w_dram = [ins[n].rearrange("(c p) d -> p c d", p=P) for n in ("L0_attn_W_dt", "L0_attn_W_x", "L0_attn_W_g")]

        def rows(name):
            a = ins[name]
            while len(a.shape) > 1:
                a = a.rearrange("a b -> (a b)")
            return a.rearrange("(r p) -> r p", p=P)

        def vecs(name):
            first = 0
            for n in VECS:
                count = rows(n).shape[0]
                if n == name:
                    return first, count
                first += count

        VECS = ["L0_attn_b_x", "L0_attn_b_g", "L0_attn_b_dt", "L0_attn_conv_b", "L0_ffn_rn_g", "L0_ffn_rn_b"]
        NV = sum(rows(n).shape[0] for n in VECS)
        bx0, bg0, bdt0, cb0, rng0, rnb0 = (vecs(n)[0] for n in VECS)
        state = lambda n: ins[n].rearrange("(c p) s -> p c s", p=P)

        TILE_ORDER = list(range(NTI, NT)) + [NTI - 1] + list(range(NTI - 1))
        BLOCK_ORDER = [3, 4, 2, 0, 1]

        def ready_tiles(nb):
            t0, t1 = BLOCKS[nb][0] // P, (BLOCKS[nb][0] + BLOCKS[nb][1]) // P
            return 1 + max(TILE_ORDER.index(t) for t in range(t0, t1))

        PREP = ([("vec",), ("pos", 0), ("pos", 1)] + [("wp", c) for c in range(0, CK, 2)]
                + [("w", w, dc) for w in range(3) for dc in range(DC)])
        IMAGES = [("img", half, g, wp) for g in range(2) for wp in range(HP) for half in range(2)]
        A_RING = PREP + IMAGES

        def a_reader(q):
            kind = A_RING[q][0]
            if kind == "img":
                return "act" if q % 2 else "dve"
            return "act" if kind == "wp" else "dve"

        def a_read(q):
            who = a_reader(q)
            return who, sum(a_reader(k) == who for k in range(q + 1))

        def wavefront(tiles, stages):
            return [(s, tiles[k - n]) for k in range(len(tiles) + len(stages) - 1)
                    for n, s in reversed(list(enumerate(stages))) if 0 <= k - n < len(tiles)]

        A_STEPS = ([("ring", q) for q in range(len(PREP))] + wavefront(TILE_ORDER[:8], ["a1", "a2", "a3", "a4"])
                   + [("ring", q) for q in range(len(PREP), len(A_RING))]
                   + wavefront(TILE_ORDER[8:], ["a1", "a2", "a3", "a4"]))

        FB = [list(range(i, min(i + 2, NT))) for i in range(0, NT, 2)]
        PAIR0 = {1: 0, 2: 3, 3: 5}
        EXPERTS = [("hid", 0, 0), ("hid", 0, 1), ("hid", 1, 0), ("hid", 1, 1), ("w2", 0), ("hid", 2, 0), ("hid", 2, 1),
                   ("w2", 1), ("hid", 3, 0), ("hid", 3, 1), ("w2", 2), ("w2", 3)]
        BESIDE = [["x2"], [], ["x2T0", "x2T1"], ["z00"], ["z10", "z01"], ["z11", "std"],
                  ["stdT0", "stdT1"], ["+yT0", "+yT1"], ["+out0", "+out1"], ["+ln1"], ["route1", "+h1"], ["route2"]]

        def beside(b, n):
            got = []
            for s in BESIDE[n]:
                nb = b + 1 + s.startswith("+")
                s = s.lstrip("+")
                if not 0 <= nb < len(FB):
                    continue
                if s[:-1] in ("yT", "out", "x2T", "z0", "z1", "stdT"):
                    if int(s[-1]) < len(FB[nb]):
                        got.append((s[:-1], FB[nb][int(s[-1])]))
                else:
                    got.append((s, nb))
            return got

        F_STEPS = []
        for b in range(-2, len(FB)):
            for n, (kind, *rest) in enumerate(EXPERTS):
                if b >= 0:
                    F_STEPS.append((kind, b, *rest))
                F_STEPS += beside(b, n)
                if n < 2 and b >= 1:
                    F_STEPS.append((f"fin{n + 1}", b - 1))
                if n == 2 and b >= 0:
                    F_STEPS.append(("route3", b))
        F_STEPS += [("fin1", len(FB) - 1), ("fin2", len(FB) - 1)]
        AUX = [s for s in F_STEPS if s[0] in ("yT", "out", "x2T", "z0", "z1", "stdT")]
        C_STEPS = [("proj", 0), ("proj", 1), ("turn", 0), ("proj", 2), ("turn", 1), ("proj", 3), ("kernels",), ("turn", 2),
                   ("turn", 3)]

        KERNEL_SUMS = [(2, 3), (2, 4), (3, 1), (3, 3)]

        def reached(nb, lag):
            n0, w = BLOCKS[nb]
            return max(0, n0 - lag * B), (N if nb == NB - 1 else n0 + w - lag * B)

        C_RING = []
        for step in C_STEPS:
            if step[0] == "kernels":
                C_RING.append(("kT",))
            if step[0] == "turn":
                C_RING += [("uT", step[1], k) for k in range(B // 4)]

        def c_reader(q):
            if C_RING[q][0] != "uT":
                return "dve"
            _, j, k = C_RING[q]
            return "act" if (k < 3, True, k < 3 or k % 2, k % 2 == 0)[j] else "dve"

        def c_read(q):
            who = c_reader(q)
            return who, sum(c_reader(k) == who for k in range(q + 1))

        G_RING = [("wo", 0), ("wo", 1), ("rw",), ("cbc",)] + [
            j for e in range(E) for j in (("w1T", e, 0), ("w1T", e, 1), ("gram", e))]

        GRAM = [(0, 0, 1.0), (1, 0, 2.0), (1, P, 1.0)]

        def g_read(q):
            who = {"wo": "act", "w1T": "act", "rw": "dve", "cbc": "dve", "gram": "dve"}
            return who[G_RING[q][0]], sum(who[j[0]] == who[G_RING[q][0]] for j in G_RING[:q + 1])

        AUX_READ = {"yT": "aux_read_act", "stdT": "aux_read_act", "out": "aux_read_dve", "x2T": "logits",
                    "z0": "aux_read_dve", "z1": "aux_read_dve"}

        def aux_read(q):
            name = AUX_READ[AUX[q][0]]
            return name, sum(AUX_READ[j[0]] == name for j in AUX[:q + 1])

        def hid_job(b, e, k):
            return (b * E + e) * 2 + k

        def store(eng, i):
            if i < 0:
                return
            eng.wait_ge(sem("result"), i + 1)
            src = acc[:, i // 2 % 2, i % 2, :]
            eng.dma_start(out[:, TPT * i:TPT * (i + 1), :].rearrange("b t d -> t b d"), src).then_inc(
                sem(f"out_stored{i % 4}"), 16)

        def split3(pe, out_ap, a_hi, a_lo, b_hi, b_lo, start, stop):
            pe.matmul(out_ap, a_hi, b_hi, start=start, stop=False)
            pe.matmul(out_ap, a_hi, b_lo, start=False, stop=False)
            return pe.matmul(out_ap, a_lo, b_hi, start=False, stop=stop)

        def copy_b(act, o, i, bias):
            return act.activation(o, i, ACT.Identity, bias=bias)

        def log1p(act, q):
            w = BLOCKS[BLOCK_ORDER[q // HC]][1]
            act.wait_ge(sem("dt_exp"), q + 1)
            act.activation(spt[:, q % 4, 0:w], spt[:, q % 4, 0:w], ACT.Ln, bias=onec[:]).then_inc(sem("dt_ln"), 1)

        def patches(ps, half, g, wp):
            dst = patchT[:].rearrange("p c (hp wp) b -> p c hp wp b", wp=HP)[
                :, half * KT:(half + 1) * KT, :, wp, g * GB:(g + 1) * GB]
            return dst, ps[:, 0:KT * ROWS].rearrange("p (k b hp) -> p k hp b", k=KT, hp=HP)

        def turned(eng, j, who):
            for k in range(B // 4):
                q = C_RING.index(("uT", j, k))
                if c_reader(q) != who:
                    continue
                eng.wait_ge(sem("c_ps"), q + 1)
                dst = U2[:, j, :, 4 * k:4 * k + 4]
                src = bank[4 + q % 4][0:L, :].rearrange("p (b h) -> p h b", b=4)
                ins_ = (eng.activation(dst, src, ACT.Identity) if who == "act" else eng.tensor_copy(dst, src))
                ins_.then_inc(sem(f"c_read_{who}"), 1)

        Z_ORDER = [s for s in F_STEPS if s[0] in ("z0", "z1")]

        def z_count(kind, i):
            return Z_ORDER.index((kind, i)) + 1

        def var_count(kind, i):
            return 2 * z_count(kind, i)

        def spread(a, w):
            return a.rearrange("p (t o) -> p t o", o=1).broadcast_to([P, w, E])
        block = stack.enter_context(nc.Block())

        @block.sync
        def _(sp):
            sp.dma_start(tok[:], ins["x_txt"]).then_inc(sem("tok_in"), 16)
            at_row = 0
            for n in VECS:
                a = rows(n)
                sp.dma_start(vec_rows[at_row:at_row + a.shape[0], :], a).then_inc(sem("vecs_in"), 16)
                at_row += a.shape[0]
            sp.wait_ge(sem("zrow"), 1)
            for k in range(4):
                part = (L - 1) * QC // 4
                sp.dma_start(kpd.rearrange("q k c -> q (k c)")[:, L * QC + k * part:L * QC + (k + 1) * part], zrow[:]).then_inc(
                    sem("zrow_stored"), 16)
            sp.dma_start(tabl[:], ins["L0_txt_weights"][0:LT + 2, :]).then_inc(sem("table_in"), 16)
            for g in range(2):
                for wp in range(HP):
                    sp.dma_start(XI[:, g, wp].rearrange("p (y k) -> p y k", k=PWC),
                                 img[g][:, :, wp * PWC:(wp + 1) * PWC]).then_inc(sem(f"img_in{g}{wp // 2}"), 16)
            for m, i in enumerate(TILE_ORDER):
                sp.wait_ge(sem("h0_copied"), m + 1)
                sp.dma_start(h0d[i], h0s[:, m % 3, :]).then_inc(sem(f"h0_stored{m % 3}"), 16)
            sp.wait_ge(sem("kt_ready"), 1)
            sp.wait_ge(sem("zrow_stored"), 64)
            sp.dma_start(kpd[:, 0:L, :].rearrange("q k c -> k q c"),
                         kt[:].rearrange("k q j h -> k q (j h)")).then_inc(sem("kernels_stored"), 16)
            sp.wait_ge(sem("kernels_stored"), 16)
            sp.dma_start(rwt[:], ins["L0_ffn_router_w"]).then_inc(sem("router_in"), 16)
            for q in range(QN):
                if q == 0:
                    sp.wait_ge(sem("kernel_sum"), HC)
                if q == 2:
                    sp.wait_ge(sem("gated"), HC * NB)
                if q >= 3:
                    sp.wait_ge(sem("ssm_mm"), 2 * (q - 2))
                src = bass.AP(kpd.tensor, kpd.offset + q * (2 * L - 1) * QC, [[QC, L], [1, L * QC]])
                sp.dma_start(Tb[q % 3][:].rearrange("s t c -> s (t c)"), src).then_inc(sem(f"toep_in{q % 3}"), 16)
                if q == 2:
                    sp.wait_ge(sem("g_mm"), HC * NB)
                if 2 <= q < 2 + E:
                    sp.dma_start(w1c[:, q - 2], ins["L0_ffn_w1"][q - 2].rearrange("(c p) h -> p c h", p=P)).then_inc(
                        sem("w1_in"), 16)
                if q == 2 + E:
                    sp.dma_start(gfb[:], ins["L0_ffn_ln_g"].partition_broadcast(P)).then_inc(sem("gfb_in"), 16)
            sp.wait_ge(sem("ssm_mm"), 2 * QN)
            sp.dma_start(Wor[:], ins["L0_attn_W_out"].rearrange("(c p) h -> p c h", p=P)).then_inc(sem("wo_in"), 16)
            sp.dma_start(w2raw[:], ins["L0_ffn_w2"].rearrange("e (c p) d -> p e c d", p=P)).then_inc(sem("w2_in"), 16)
            sp.wait_ge(sem("w1g_split"), 1)
            sp.dma_start(lb12[:], ins["L0_ffn_ln_b"].partition_broadcast(12)).then_inc(sem("lb_in"), 16)
            sp.wait_ge(sem("gram_tr"), E)
            sp.wait_ge(sem("w1g_mult"), DC)
            for m in range(3):
                sp.wait_ge(sem(f"h0_stored{m}"), 16 * len(range(m, NT, 3)))
            for i in range(NT):
                if i >= 2:
                    sp.wait_ge(sem("h1"), i - 1)
                sp.dma_start(h0r[:, i % 2, :], h0d[i]).then_inc(sem(f"h0_back{i % 2}"), 16)
                store(sp, i - 6)
            for i in range(NT - 6, NT):
                store(sp, i)
            for k in range(4):
                sp.wait_ge(sem(f"out_stored{k}"), 16 * len(range(k, NT, 4)))

        @block.gpsimd
        def _(pool):
            pool.memset(ident[:], 0.0).then_inc(sem("ident0"), 1)
            pool.wait_ge(sem("ident0"), 1)
            pool.affine_select(out=ident[:], in_=ident[:], compare_op=ALU.not_equal, fill=1.0, base=0,
                               pattern=[[-1, P]], channel_multiplier=1).then_inc(sem("ident"), 1)
            pool.iota(rowid[:], pattern=[[0, 1]], base=0, channel_multiplier=1,
                      allow_small_or_imprecise_dtypes=True).then_inc(sem("consts"), 1)
            pool.iota(tf[:, 7, :], pattern=[[1, LT]], base=0, channel_multiplier=0,
                      allow_small_or_imprecise_dtypes=True).then_inc(sem("consts"), 1)
            pool.memset(zrow[:], 0.0).then_inc(sem("zrow"), 1)
            pool.memset(epsc[:], EPS).then_inc(sem("consts"), 1)
            pool.memset(onec[:], 1.0).then_inc(sem("consts"), 1)
            pool.iota(kio[:], pattern=[[-1, L]], base=L - 1, channel_multiplier=0,
                      allow_small_or_imprecise_dtypes=True).then_inc(sem("consts"), 1)
            pool.iota(eid[:], pattern=[[1, E]], base=0, channel_multiplier=0,
                      allow_small_or_imprecise_dtypes=True).then_inc(sem("consts"), 1)
            pool.memset(m12[:], 0.0).then_inc(sem("m12"), 1)
            for n in range(3):
                pool.wait_ge(sem("m12"), n + 1)
                pool.affine_select(out=m12[:], in_=m12[:], compare_op=ALU.not_equal, fill=1.0, base=-E * n,
                                   pattern=[[-1, E]], channel_multiplier=1).then_inc(sem("m12"), 1)
            pool.memset(mA[:], 1.0).then_inc(sem("mAB"), 1)
            pool.memset(mB[:], 0.0).then_inc(sem("mAB"), 1)
            pool.wait_ge(sem("mAB"), 2)
            pool.affine_select(out=mA[:], in_=mA[:], compare_op=ALU.is_ge, fill=0.0, base=2 * E - 1,
                               pattern=[[0, 1]], channel_multiplier=-1).then_inc(sem("mAB"), 1)
            pool.affine_select(out=mB[:], in_=mB[:], compare_op=ALU.is_ge, fill=1.0, base=2 * E - 1,
                               pattern=[[0, 1]], channel_multiplier=-1).then_inc(sem("mAB"), 1)
            pool.wait_ge(sem("adt"), 1)
            pool.wait_ge(sem("consts"), 6)
            for m in range(3):
                pool.wait_ge(sem(f"h0_stored{m}"), 16 * len(range(m, NT, 3)))
            pool.wait_ge(sem("zrow_stored"), 64)
            for j in range(HC):
                pool.tensor_tensor(Eb[:, j], adt[:, j].rearrange("p (o s) -> p o s", o=1).broadcast_to([P, L, S]),
                                   kio[:].rearrange("p (k o) -> p k o", o=1).broadcast_to([P, L, S]),
                                   ALU.mult).then_inc(sem("exponent"), 1)
            for c in range(HC * NB):
                j, (a, b) = c // NB, reached(c % NB, 2)
                pool.wait_ge(sem("conv"), c + 1)
                mid = ur[:, j % 2, B + a:B + b]
                pool.tensor_tensor(mid, mid, hb[:, j % 2, a:b], ALU.subtract).then_inc(sem("u_minus_h"), 1)
                pool.wait_ge(sem("u_minus_h"), c + 1)
                pool.wait_ge(sem("gate"), c + 1)
                pool.tensor_tensor(mid, mid, gb[j % 2][:, a:b], ALU.mult).then_inc(sem("gated"), 1)
            pool.wait_ge(sem("w1_centred"), E * DC)
            pool.wait_ge(sem("gfb_in"), 16)
            pool.wait_ge(sem("c_ps"), len(C_RING))
            for dc in range(DC):
                pool.tensor_tensor(w1p[:, :, dc, :], w1c[:, :, dc, :], gfb[:], ALU.mult).then_inc(sem("w1g_mult"), 1)
            pool.wait_ge(sem("w1g_mult"), DC)
            pool.memset(Bst[:].bitcast(F32), 0.0).then_inc(sem("std_zero"), 1)
            pool.memset(stdT[:].bitcast(F32), 0.0).then_inc(sem("std_zero"), 1)
            linked = [0]

            def link(ins_):
                linked[0] += 1
                ins_.then_inc(sem("pool_link"), 1)
                pool.wait_ge(sem("pool_link"), linked[0])

            def row_inputs(i):
                pool.wait_ge(sem(f"h0_back{i % 2}"), 16 * (i // 2 + 1))
                pool.wait_ge(sem("nmr0"), 1)
                if i >= 2:
                    pool.wait_ge(sem("r1"), i - 1)
                pool.tensor_scalar(xb[:, i % 2, :], h0r[:, i % 2, :], rs0[:, i:i + 1], nmr0[:, i:i + 1],
                                   ALU.mult, ALU.add).then_inc(sem("xb0"), 1)
                pool.wait_ge(sem("xb0"), i + 1)
                pool.wait_ge(sem("rows_in"), 80)
                pool.tensor_tensor(xb[:, i % 2, :], xb[:, i % 2, :], bout_b[:], ALU.add).then_inc(sem("xb"), 1)
                pool.tensor_tensor(h0r[:, i % 2, :], h0r[:, i % 2, :], lnb_b[:], ALU.add).then_inc(sem("h0b"), 1)

            row_inputs(0)
            for kind, *rest in F_STEPS:
                i = rest[0]
                if kind == "out" and i + 1 < NT:
                    row_inputs(i + 1)
                elif kind == "x2T":
                    pool.wait_ge(sem("x2"), i + 1)
                    pool.tensor_tensor(h1[:, i, :], h1[:, i, :], onb_b[:], ALU.add).then_inc(sem("h1b"), 1)
                elif kind == "route2":
                    t0, t1 = FB[i][0], FB[i][-1] + 1
                    ts, w = slice(t0, t1), t1 - t0
                    pool.wait_ge(sem("gexp"), i + 1)
                    g, rk, cp, pr = gx[:, ts, :], rank[:, ts, :], top[:, ts, :], pair[:, 0:w, :]
                    for d in range(1, E):
                        o = PAIR0[d]
                        pool.tensor_tensor(pr[:, :, o:o + E - d], g[:, :, d:E], g[:, :, 0:E - d], ALU.subtract).then_inc(
                            sem("pair"), 1)
                    pool.wait_ge(sem("pair"), 3 * (i + 1))
                    link(pool.tensor_scalar(pr, pr, 0.0, None, ALU.is_gt))
                    before = eid[:].rearrange("p (o e) -> p o e", o=1).broadcast_to([P, w, E])
                    link(pool.tensor_tensor(rk[:, :, 0:E - 1], before[:, :, 0:E - 1], pr[:, :, 0:E - 1], ALU.add))
                    link(pool.tensor_copy(rk[:, :, E - 1:E], before[:, :, E - 1:E]))
                    link(pool.tensor_tensor(rk[:, :, 1:E], rk[:, :, 1:E], pr[:, :, 0:E - 1], ALU.subtract))
                    for d in range(2, E):
                        o = PAIR0[d]
                        link(pool.tensor_tensor(rk[:, :, 0:E - d], rk[:, :, 0:E - d], pr[:, :, o:o + E - d], ALU.add))
                        link(pool.tensor_tensor(rk[:, :, d:E], rk[:, :, d:E], pr[:, :, o:o + E - d], ALU.subtract))
                    link(pool.tensor_scalar(cp, rk, 2.0, None, ALU.is_lt))
                    link(pool.tensor_tensor(rk[:, :, 0:2], g[:, :, 0:2], g[:, :, 2:4], ALU.add))
                    link(pool.tensor_tensor(cp, cp, g, ALU.mult))
                    link(pool.tensor_tensor(rk[:, :, 2:4], cp[:, :, 0:2], cp[:, :, 2:4], ALU.add))
                    link(pool.tensor_tensor(pr[:, :, 0:2], rk[:, :, 0:E:2], rk[:, :, 1:E:2], ALU.add))
                    link(pool.tensor_scalar(pr[:, :, 2], pr[:, :, 0], 1e-8, None, ALU.mult))
                    link(pool.tensor_tensor(pr[:, :, 3], pr[:, :, 1], pr[:, :, 2], ALU.add))
                    pool.wait_ge(sem("stdE"), i + 1)
                    pool.tensor_tensor(rk, stdE[:, ts, :], pr[:, :, 3:4].broadcast_to([P, w, E]), ALU.mult).then_inc(
                        sem("top2"), 1)
                elif kind == "fin2":
                    for n, t in enumerate(FB[i]):
                        a = acc[:, i % 2, n, :]
                        pool.wait_ge(sem("fin_norm"), t + 1)
                        link(pool.tensor_tensor(a, a, ong_b[:], ALU.mult))
                        pool.wait_ge(sem("h1b"), t + 1)
                        pool.tensor_tensor(a, a, h1[:, t, :], ALU.add).then_inc(sem("result"), 1)

        @block.tensor
        def _(pe):
            pe.wait_ge(sem("ident"), 1)
            for step in A_STEPS:
                if step[0] == "ring":
                    q = step[1]
                    kind, *rest = A_RING[q]
                    if q >= 4:
                        who, n = a_read(q - 4)
                        pe.wait_ge(sem(f"a_read_{who}"), n)
                    ps = bank[q % 4]
                    if kind == "vec":
                        pe.wait_ge(sem("vecs_in"), 16 * len(VECS))
                        mm = pe.transpose(ps[:, 0:NV], vec_rows[0:NV, :], ident[0:NV, 0:NV])
                    elif kind == "pos":
                        pe.wait_ge(sem("pos_spread"), 2)
                        k = rest[0]
                        mm = pe.matmul(ps[0:LT + 2, :], ones_b[:, 0:LT + 2],
                                       posD[:].rearrange("p j b -> p (j b)")[:, k * 512:(k + 1) * 512],
                                       start=True, stop=True)
                    elif kind == "wp":
                        pe.wait_ge(sem("wp_in"), 16)
                        for c in range(rest[0], rest[0] + 2):
                            for eh in range(DC):
                                mm = pe.transpose(ps[:, (c % 2) * D + eh * P:(c % 2) * D + (eh + 1) * P],
                                                  Wpr[:, eh, c * P:(c + 1) * P], ident[:])
                    elif kind == "w":
                        w, dc = rest
                        pe.wait_ge(sem(f"w_in{w}"), 16)
                        for j in range(HC):
                            mm = pe.transpose(ps[:, j * P:(j + 1) * P], Wr[w][:, j, dc * P:(dc + 1) * P], ident[:])
                    else:
                        half, g, wp = rest
                        pe.wait_ge(sem(f"img_in{g}{wp // 2}"), 32)
                        for kk in range(KT):
                            c0 = (half * KT + kk) * P
                            mm = pe.transpose(ps[:, kk * ROWS:(kk + 1) * ROWS], XI[:, g, wp, c0:c0 + P],
                                              ident[0:ROWS, 0:ROWS])
                    mm.then_inc(sem("a_ps"), 1)
                elif step[0] == "a1":
                    i = step[1]
                    m = TILE_ORDER.index(i)
                    ps = bank[4 + m % 2][:, 0:D]
                    if m >= 2:
                        pe.wait_ge(sem("h0_copied"), m - 1)
                    if i >= NTI:
                        pe.wait_ge(sem("onehot"), 2)
                        pe.wait_ge(sem("table_in"), 16)
                        mm = pe.matmul(ps, OH[:, (i - NTI) * P:(i - NTI + 1) * P], tabl[:], start=True, stop=True)
                    else:
                        pe.wait_ge(sem("posb"), 2)
                        who, n = a_read(len(A_RING) - 2)
                        pe.wait_ge(sem(f"a_read_{who}"), n)
                        who, n = a_read(len(A_RING) - 1)
                        pe.wait_ge(sem(f"a_read_{who}"), n)
                        for c in range(CK):
                            pe.matmul(ps, patchT[:, c, TPT * i:TPT * (i + 1), :].rearrange("p t b -> p (t b)"),
                                      WpT[:, c, :], start=(c == 0), stop=False)
                        mm = pe.matmul(ps, sel[:, TPT * i:TPT * (i + 1), :].rearrange("p t b -> p (t b)"), posb[:],
                                       start=False, stop=True)
                    mm.then_inc(sem("h0_ps"), 1)
                elif step[0] == "a4":
                    m = TILE_ORDER.index(step[1])
                    pe.wait_ge(sem("x"), m + 1)
                    if m >= 2:
                        pe.wait_ge(sem("xT"), m - 1)
                    for dc in range(DC):
                        mm = pe.transpose(bank[6 + m % 2][:, dc * P:(dc + 1) * P], xs[:, m % 2, dc * P:(dc + 1) * P],
                                          ident[:])
                    mm.then_inc(sem("xT_ps"), 1)

            for n, nb in enumerate(BLOCK_ORDER):
                n0, w = BLOCKS[nb]
                pe.wait_ge(sem("xT"), ready_tiles(nb))
                for j in range(HC):
                    q = n * HC + j
                    if q >= 4:
                        pe.wait_ge(sem("dt_read"), q - 3)
                    for dc in range(DC):
                        mm = split3(pe, bank[q % 4][:, 0:w], WT[0][0][:, dc, j * P:(j + 1) * P],
                                    WT[0][1][:, dc, j * P:(j + 1) * P], xT_hi[:, dc, n0:n0 + w],
                                    xT_lo[:, dc, n0:n0 + w], dc == 0, dc == DC - 1)
                    mm.then_inc(sem("dt_mm"), 1)
            pe.wait_ge(sem("dt_read"), HC * NB)

            ring = 0
            for step in C_STEPS:
                if step[0] == "proj":
                    j = step[1]
                    for nb, (n0, w) in enumerate(BLOCKS):
                        c = j * NB + nb
                        for wt, first, done, read in ((1, 0, "u_mm", "ur"), (2, 2, "g_mm", "gate")):
                            if c >= 2:
                                pe.wait_ge(sem(read), c - 1)
                            for dc in range(DC):
                                mm = split3(pe, bank[first + c % 2][:, 0:w], WT[wt][0][:, dc, j * P:(j + 1) * P],
                                            WT[wt][1][:, dc, j * P:(j + 1) * P], xT_hi[:, dc, n0:n0 + w],
                                            xT_lo[:, dc, n0:n0 + w], dc == 0, dc == DC - 1)
                            mm.then_inc(sem(done), 1)
                    continue
                count = 1 if step[0] == "kernels" else B // 4
                for k in range(count):
                    if ring >= 4:
                        who, n = c_read(ring - 4)
                        pe.wait_ge(sem(f"c_read_{who}"), n)
                    ps = bank[4 + ring % 4]
                    if step[0] == "kernels":
                        pe.wait_ge(sem("kernel_sum"), HC)
                        for j in range(HC):
                            mm = pe.transpose(ps[0:L, j * P:(j + 1) * P], Kk[:, j, :], ident[:])
                    else:
                        j = step[1]
                        pe.wait_ge(sem("mixed"), NB * (j + 1))
                        for b in range(4 * k, 4 * k + 4):
                            mm = pe.transpose(ps[0:L, (b % 4) * P:(b % 4 + 1) * P],
                                              hb[:, j % 2, :].rearrange("p (t b) -> p t b", b=B)[:, :, b], ident[:])
                    mm.then_inc(sem("c_ps"), 1)
                    ring += 1

            pe.wait_ge(sem("ur"), HC * NB)
            pe.wait_ge(sem("gate"), HC * NB)
            for q in (len(C_RING) - 2, len(C_RING) - 1):
                who, n = c_read(q)
                pe.wait_ge(sem(f"c_read_{who}"), n)
            for v in range(2 * QN):
                q = v // 2
                pe.wait_ge(sem(f"toep_in{q % 3}"), 16 * (q // 3 + 1))
                if v >= 4:
                    pe.wait_ge(sem("y_dve" if v % 2 else "y_act"), (v - 4) // 2 + 1)
                for k in range(4):
                    hq = 4 * v + k
                    for j in range(HC):
                        mm = pe.matmul(bank[v % 4][j * B:(j + 1) * B, k * L:(k + 1) * L], U2[:, j, hq, :],
                                       Tb[q % 3][:, :, j * QH + hq % QH], start=True, stop=True)
                mm.then_inc(sem("ssm_mm"), 1)

            for q, (kind, *rest) in enumerate(G_RING):
                if q >= 4:
                    who, n = g_read(q - 4)
                    pe.wait_ge(sem(f"g_read_{who}"), n)
                ps = bank[4 + q % 4]
                if kind == "wo":
                    pe.wait_ge(sem("wo_in"), 16)
                    for j in range(2):
                        for c in range(DC):
                            h0_ = (2 * rest[0] + j) * P
                            mm = pe.transpose(ps[:, j * D + c * P:j * D + (c + 1) * P], Wor[:, c, h0_:h0_ + P], ident[:])
                elif kind == "rw":
                    pe.wait_ge(sem("router_in"), 16)
                    for dc in range(DC):
                        mm = pe.transpose(ps[:, dc * E:(dc + 1) * E], rwt[:, dc * P:(dc + 1) * P], ident[0:E, 0:E])
                elif kind == "cbc":
                    pe.wait_ge(sem("rnb_spread"), DC)
                    pe.wait_ge(sem("rwT"), 1)
                    for dc in range(DC):
                        mm = pe.matmul(ps[:, 0:E], zjunk[:, 0, dc * P:(dc + 1) * P], rwT[:, dc, :], start=(dc == 0),
                                       stop=(dc == DC - 1))
                elif kind == "w1T":
                    e, k = rest
                    pe.wait_ge(sem("w1_centred"), E * DC)
                    for hc in range(2):
                        for dc in range(DC):
                            c0 = (2 * k + hc) * P
                            mm = pe.transpose(ps[:, hc * D + dc * P:hc * D + (dc + 1) * P], w1c[:, e, dc, c0:c0 + P],
                                              ident[:])
                    if k == 1:
                        mm.then_inc(sem("gram_tr"), 1)
                        pe.wait_ge(sem("gram_tr"), e + 1)
                        mm = pe.nop()
                else:
                    e = rest[0]
                    pe.wait_ge(sem("w1T"), 2 * (e + 1))
                    for dc in range(DC):
                        w = (dc + 1) * P
                        for hc in range(HC):
                            mm = pe.matmul(ps[:, dc * D:dc * D + w], w1cT[:, hc, dc * P:(dc + 1) * P],
                                           w1cT[:, hc, 0:w], start=(hc == 0), stop=(hc == HC - 1))
                mm.then_inc(sem("g_ps"), 1)
            for q in range(len(G_RING) - 4, len(G_RING)):
                who, n = g_read(q)
                pe.wait_ge(sem(f"g_read_{who}"), n)

            aux = 0

            def aux_bank():
                nonlocal aux
                if aux >= 4:
                    name, n = aux_read(aux - 4)
                    pe.wait_ge(sem(name), n)
                aux += 1
                return bank[4 + (aux - 1) % 4]

            for kind, *rest in F_STEPS:
                i = rest[0]
                if kind == "yT":
                    ps = aux_bank()
                    if i == 0:
                        pe.wait_ge(sem("y_act"), QN)
                        pe.wait_ge(sem("y_dve"), QN)
                    for tt in range(TPT):
                        mm = pe.transpose(ps[:, tt * P:(tt + 1) * P], y[:, :, L - 1 - (TPT * i + tt)], ident[:])
                    mm.then_inc(sem("yT_ps"), 1)
                elif kind == "out":
                    ps = aux_bank()
                    pe.wait_ge(sem("yT"), i + 1)
                    for j in range(HC):
                        mm = pe.matmul(ps[:, 0:D], yT[:, i % 2, j, :], WoT[:, j, :], start=(j == 0), stop=(j == HC - 1))
                    mm.then_inc(sem("out_mm"), 1)
                elif kind == "x2T":
                    ps = aux_bank()
                    pe.wait_ge(sem("x2"), i + 1)
                    for dc in range(DC):
                        mm = pe.transpose(ps[:, dc * P:(dc + 1) * P], x2s[:, i % 2, dc * P:(dc + 1) * P], ident[:])
                    mm.then_inc(sem("x2T_ps"), 1)
                elif kind in ("z0", "z1"):
                    pe.wait_ge(sem("x2T"), i + 1)
                    tok_ = slice(i % 2 * P, (i % 2 + 1) * P)
                    hi, lo = x2T_hi[:, i // 2 % 2, :, tok_], x2T_lo[:, i // 2 % 2, :, tok_]
                    ps = aux_bank()
                    pl = bank[4 + AUX.index(("x2T", i)) % 4][:, D:D + E]
                    if kind == "z0":
                        pe.wait_ge(sem("router_split"), 2)
                    cols = slice(0, 512) if kind == "z0" else slice(512, 1024)
                    own = lambda a: a.rearrange("p (e k d) -> p e k d", e=2, k=DC)[:, :, 0, :]
                    for dc in (1, 0):
                        o, g_hi, g_lo = ps[:], G_hi[:, dc, cols], G_lo[:, dc, cols]
                        if dc == 0:
                            o, g_hi, g_lo = own(o), own(g_hi), own(g_lo)
                        for n, (a, g, r) in enumerate(((hi, g_hi, rg_hi), (hi, g_lo, rg_lo), (lo, g_hi, rg_hi))):
                            first, final = dc == 1 and n == 0, dc == 0 and n == 2
                            if kind == "z0":
                                mm = pe.matmul(pl, a[:, dc, :], r[:, dc, :], start=first, stop=final)
                                if final:
                                    mm.then_inc(sem("logit_mm"), 1)
                            mm = pe.matmul(o, a[:, dc, :], g, start=first, stop=final)
                    mm.then_inc(sem("z_mm"), 1)
                elif kind == "stdT":
                    ps = aux_bank()
                    pe.wait_ge(sem("s3"), 3 * (i // 2 + 1))
                    mm = pe.transpose(ps[0:3 * E, 0:P], s3[:, i % 2].rearrange("p a e -> p (a e)").bitcast(F32), ident[:])
                    mm.then_inc(sem("stdT_ps"), 1)
                elif kind == "hid":
                    b, e, k = rest
                    q, w = hid_job(b, e, k), P * len(FB[b])
                    if q == 0:
                        pe.wait_ge(sem("w1g_split"), 2)
                        pe.wait_ge(sem("Bst"), 1)
                    if q >= 2:
                        pe.wait_ge(sem("hid_lo"), q - 1)
                    pe.wait_ge(sem("stdT"), FB[b][-1] + 1)
                    for hc in (2 * k, 2 * k + 1):
                        ps = bank[q % 2][:, (hc % 2) * 2 * P:(hc % 2) * 2 * P + w]
                        hs = slice(hc * P, (hc + 1) * P)
                        for dc in range(DC):
                            split3(pe, ps, w1g_hi[:, e, dc, hs], w1g_lo[:, e, dc, hs], x2T_hi[:, b % 2, dc, 0:w],
                                   x2T_lo[:, b % 2, dc, 0:w], dc == 0, False)
                        mm = pe.matmul(ps, Bst[:, e, hs], stdT[:, b % 2, 0:w], start=False, stop=True)
                    mm.then_inc(sem("hid_mm"), 1)
                elif kind == "w2":
                    b, e = rest
                    q = b * E + e
                    if q == 0:
                        pe.wait_ge(sem("w2_split"), 2)
                    if q >= 2:
                        pe.wait_ge(sem("combined"), q - 1)
                    pe.wait_ge(sem("hid_lo"), hid_job(b, e, 1) + 1)
                    for n in range(len(FB[b])):
                        ts = slice(n * P, (n + 1) * P)
                        for hc in range(HC):
                            mm = split3(pe, bank[2 + q % 2][:, n * D:(n + 1) * D], hid_hi[:, e % 2, hc, ts],
                                        hid_lo[:, e % 2, hc, ts], w2_hi[:, e, hc, :], w2_lo[:, e, hc, :],
                                        hc == 0, hc == HC - 1)
                    mm.then_inc(sem("w2_mm"), 1)

        @block.scalar
        def _(act):
            act.dma_start(Wpr[:], ins["L0_tok_W_proj"].rearrange("(c p) d -> p c d", p=P)).then_inc(sem("wp_in"), 16)
            act.dma_start(araw[:], state("L0_attn_A_raw")).then_inc(sem("araw_in"), 16)
            act.dma_start(posb[:], ins["L0_tok_pos_emb"]).then_inc(sem("bcs_in"), 16)
            act.dma_start(bpb[:], ins["L0_tok_b_proj"].partition_broadcast(LI)).then_inc(sem("bcs_in"), 16)
            for w in range(3):
                act.dma_start(Wr[w][:], w_dram[w]).then_inc(sem(f"w_in{w}"), 16)
            act.dma_start(bcs[:, 0], state("L0_attn_B_ssm")).then_inc(sem("bcs_in"), 16)
            act.dma_start(bcs[:, 1], state("L0_attn_C_ssm")).then_inc(sem("bcs_in"), 16)
            act.dma_start(cw[:], ins["L0_attn_conv_w"].rearrange("(c p) o k -> p c (o k)", p=P)).then_inc(sem("cw_in"), 16)
            for t, n in ((bout_b, "L0_attn_b_out"), (lng_b, "L0_attn_ln_g"), (lnb_b, "L0_attn_ln_b"),
                         (ong_b, "L0_ffn_on_g"), (onb_b, "L0_ffn_on_b")):
                act.dma_start(t[:], ins[n].partition_broadcast(P)).then_inc(sem("rows_in"), 16)

            def copy(o, i):
                return act.activation(o, i, ACT.Identity)

            act.preload_act_table_set("natural_log_exp_and_others")
            act.wait_ge(sem("a_capped"), 1)
            act.activation(atmp[:], atmp[:], ACT.Exp).then_inc(sem("a_exp"), 1)
            act.wait_ge(sem("a_exp"), 1)
            act.wait_ge(sem("consts"), 6)
            act.activation(atmp[:], atmp[:], ACT.Ln, bias=onec[:]).then_inc(sem("a_ln"), 1)
            for step in A_STEPS:
                if step[0] == "ring":
                    q = step[1]
                    kind, *rest = A_RING[q]
                    ps = bank[q % 4]
                    if kind == "wp":
                        act.wait_ge(sem("a_ps"), q + 1)
                        c = rest[0]
                        copy(WpT[:, c:c + 2, :].rearrange("p c e -> p (c e)"), ps[:]).then_inc(sem("a_read_act"), 1)
                    elif kind == "w":
                        w, dc = rest
                        act.wait_ge(sem("a_ps"), q + 1)
                        copy(WT[w][0][:, dc, :], ps[:]).then_inc(sem("w_hi"), 1)
                    elif kind == "img" and a_reader(q) == "act":
                        act.wait_ge(sem("a_ps"), q + 1)
                        copy(*patches(ps, *rest)).then_inc(sem("a_read_act"), 1)
                    continue
                kind, m = step[0], TILE_ORDER.index(step[1])
                i = step[1]
                if kind == "a1":
                    act.wait_ge(sem("h0_ps"), m + 1)
                    if m >= 3:
                        act.wait_ge(sem(f"h0_stored{m % 3}"), 16 * (m // 3))
                        act.wait_ge(sem("x"), m - 2)
                    copy(h0s[:, m % 3, :], bank[4 + m % 2][:, 0:D]).then_inc(sem("h0_copied"), 1)
                elif kind == "a3":
                    act.wait_ge(sem("mv0"), m + 1)
                    act.activation(sd0[:, i:i + 1], mv0[:, i, 1:2], ACT.Sqrt, bias=epsc[:]).then_inc(sem("sd0"), 1)
                elif kind == "a4":
                    act.wait_ge(sem("xT_ps"), m + 1)
                    copy(xT_hi[:, :, i * P:(i + 1) * P], bank[6 + m % 2][:, 0:D].rearrange("p (c n) -> p c n", c=DC)
                         ).then_inc(sem("xT_hi"), 1)
            act.preload_act_table_set("natural_log_exp_and_others")
            for q in range(HC * NB):
                w = BLOCKS[BLOCK_ORDER[q // HC]][1]
                act.wait_ge(sem("dt_capped"), q + 1)
                act.activation(spt[:, q % 4, 0:w], spt[:, q % 4, 0:w], ACT.Exp).then_inc(sem("dt_exp"), 1)
                if q >= 1:
                    log1p(act, q - 1)
            log1p(act, HC * NB - 1)
            for step in C_STEPS:
                if step[0] == "proj":
                    j = step[1]
                    if j == 0:
                        act.wait_ge(sem("ur_pads"), 2)
                    for nb, (n0, w) in enumerate(BLOCKS):
                        c = j * NB + nb
                        act.wait_ge(sem("u_mm"), c + 1)
                        if j >= 2:
                            act.wait_ge(sem("mixed"), NB * (j - 1))
                        copy_b(act, ur[:, j % 2, B + n0:B + n0 + w], bank[c % 2][:, 0:w], vec[:, bx0 + j:bx0 + j + 1]
                               ).then_inc(sem("ur"), 1)
                        act.wait_ge(sem("g_mm"), c + 1)
                        if j >= 2:
                            act.wait_ge(sem("gated"), NB * (j - 1))
                        if j == 1:
                            act.wait_ge(sem("zrow_stored"), 64)
                            act.wait_ge(sem("h0_stored0"), 16 * len(range(0, NT, 3)))
                            act.wait_ge(sem("h0_stored1"), 16 * len(range(1, NT, 3)))
                            act.wait_ge(sem("h0_stored2"), 16 * len(range(2, NT, 3)))
                        act.activation(gb[j % 2][:, n0:n0 + w], bank[2 + c % 2][:, 0:w], ACT.Sigmoid,
                                       bias=vec[:, bg0 + j:bg0 + j + 1]).then_inc(sem("gate"), 1)
                        a, b = reached(nb, 1)
                        act.wait_ge(sem("ur"), c + 1)
                        act.wait_ge(sem("cw_in"), 16)
                        if j >= 2:
                            act.wait_ge(sem("c_ps"), 1 + max(q for q, r in enumerate(C_RING) if r[0:2] == ("uT", j - 2)))
                        act.activation(hb[:, j % 2, a:b], ur[:, j % 2, B + a:B + b], ACT.Identity, scale=cw[:, j, 1:2],
                                       bias=vec[:, cb0 + j:cb0 + j + 1]).then_inc(sem("h_init"), 1)
                elif step[0] == "turn":
                    turned(act, step[1], "act")
                if step == ("turn", 0):
                    act.wait_ge(sem("adt"), 1)
                    act.activation(wmix[:], adt[:], ACT.Exp).then_inc(sem("a_d"), 1)
                    for j in range(HC):
                        act.wait_ge(sem("exponent"), j + 1)
                        act.activation(Eb[:, j], Eb[:, j], ACT.Exp).then_inc(sem("powers"), 1)
            for v in range(0, 2 * QN, 2):
                act.wait_ge(sem("ssm_mm"), v + 1)
                copy(y[:, 4 * v:4 * v + 4, :].rearrange("p k t -> p (k t)"), bank[v % 4][:, 0:4 * L]).then_inc(
                    sem("y_act"), 1)
                if v in (16, 18):
                    dc = (v - 16) // 2
                    act.wait_ge(sem("w1g_mult"), dc + 1)
                    copy(w1g_hi[:, :, dc, :], w1p[:, :, dc, :]).then_inc(sem("w1g_hi"), 1)
            for q, (kind, *rest) in enumerate(G_RING):
                ps = bank[4 + q % 4]
                if kind == "wo":
                    act.wait_ge(sem("g_ps"), q + 1)
                    j = 2 * rest[0]
                    copy(WoT[:, j:j + 2, :].rearrange("p j d -> p (j d)"), ps[:]).then_inc(sem("g_read_act"), 1)
                elif kind == "w1T":
                    e, k = rest
                    act.wait_ge(sem("g_ps"), q + 1)
                    if e >= 1:
                        act.wait_ge(sem("g_ps"), q - k)
                    copy(w1cT[:, 2 * k:2 * k + 2, :].rearrange("p j d -> p (j d)"), ps[:]).then_inc(sem("w1T"), 1)
                    act.wait_ge(sem("w1T"), 2 * e + k + 1)
                    act.sem_inc(sem("g_read_act"), 1)
                elif kind == "gram":
                    e = rest[0]
                    act.wait_ge(sem("g_ps"), q + 1)
                    for dc, c0, times in GRAM:
                        act.activation(G_hi[:, dc, e * D + c0:e * D + c0 + P], ps[:, dc * D + c0:dc * D + c0 + P],
                                       ACT.Identity, scale=times).then_inc(sem("G_hi"), 1)
                if kind == "gram" and rest[0] == 0:
                    act.wait_ge(sem("w2_in"), 16)
                    copy(w2_hi[:], w2raw[:]).then_inc(sem("w2_hi"), 1)
            for kind, *rest in F_STEPS:
                i = rest[0]
                if kind == "yT":
                    act.wait_ge(sem("yT_ps"), i + 1)
                    act.wait_ge(sem("w1g_mult"), DC)
                    act.wait_ge(sem("gram_tr"), E)
                    if i >= 2:
                        act.wait_ge(sem("out_mm"), i - 1)
                    n = AUX.index((kind, i))
                    copy(yT[:, i % 2].rearrange("p j (t b) -> p j t b", b=B),
                         bank[4 + n % 4][:].rearrange("p (t j b) -> p j t b", j=HC, b=B)).then_inc(sem("yT"), 1)
                    act.wait_ge(sem("yT"), i + 1)
                    act.sem_inc(sem("aux_read_act"), 1)
                elif kind == "h1":
                    pass
                elif kind == "ln1":
                    ts = slice(FB[i][0], FB[i][-1] + 1)
                    act.wait_ge(sem("mv1"), ts.stop)
                    act.activation(sd1[:, ts], mv1[:, ts, 1], ACT.Sqrt, bias=epsc[:]).then_inc(sem("sd1"), 1)
                elif kind == "x2":
                    ts = slice(FB[i][0], FB[i][-1] + 1)
                    act.wait_ge(sem("mv2"), ts.stop)
                    act.activation(sd2[:, ts], mv2[:, ts, 1], ACT.Sqrt, bias=epsc[:]).then_inc(sem("sd2"), 1)
                elif kind == "x2T":
                    if i % 2 == 0:
                        ts = slice(i, FB[i // 2][-1] + 1)
                        act.wait_ge(sem("v2n"), i // 2 + 1)
                        act.activation(rs2r[:, ts], v2n[:, ts], ACT.Sqrt, bias=epsc[:]).then_inc(sem("sdr"), 1)
                    act.wait_ge(sem("x2T_ps"), i + 1)
                    if i == 0:
                        act.wait_ge(sem("Bst"), 1)
                    n = AUX.index((kind, i))
                    copy(x2T_hi[:, i // 2 % 2, :, i % 2 * P:(i % 2 + 1) * P],
                         bank[4 + n % 4][:, 0:D].rearrange("p (c n) -> p c n", c=DC)).then_inc(sem("x2T_hi"), 1)
                elif kind == "std":
                    ts = slice(FB[i][0], FB[i][-1] + 1)
                    act.wait_ge(sem("varE"), E * ts.stop)
                    act.activation(stdE[:, ts, :], varE[:, ts, :], ACT.Sqrt, bias=epsc[:], scale=1.0 / HF).then_inc(
                        sem("stdE"), 1)
                elif kind == "stdT":
                    act.wait_ge(sem("stdT_ps"), i + 1)
                    act.wait_ge(sem("std_zero"), 2)
                    n = AUX.index((kind, i))
                    copy(stdT[0:3 * E, i // 2 % 2, i % 2 * P:(i % 2 + 1) * P], bank[4 + n % 4][0:3 * E, 0:P]).then_inc(
                        sem("stdT"), 1)
                    act.wait_ge(sem("stdT"), i + 1)
                    act.sem_inc(sem("aux_read_act"), 1)
                elif kind == "route1":
                    act.wait_ge(sem("logit_rel"), i + 1)
                    ts = slice(FB[i][0], FB[i][-1] + 1)
                    act.activation(gx[:, ts, :], gx[:, ts, :], ACT.Exp).then_inc(sem("gexp"), 1)
                    act.preload_act_table_set("sqrt_and_others")
                elif kind == "hid":
                    b, e, k = rest
                    q, w = hid_job(b, e, k), P * len(FB[b])
                    act.wait_ge(sem("hid_mm"), q + 1)
                    if b * E + e >= 2:
                        act.wait_ge(sem("w2_mm"), b * E + e - 1)
                    act.activation(hid_hi[:, e % 2, 2 * k:2 * k + 2, 0:w],
                                   bank[q % 2][:].rearrange("p (c n) -> p c n", c=2)[:, :, 0:w], ACT.Relu).then_inc(
                                       sem("hid_hi"), 1)
                elif kind == "fin2":
                    ts = slice(FB[i][0], FB[i][-1] + 1)
                    act.wait_ge(sem("mv3"), ts.stop)
                    act.activation(sd3[:, ts], mv3[:, ts, 1], ACT.Sqrt, bias=epsc[:]).then_inc(sem("sd3"), 1)

        @block.vector
        def _(dve):
            linked = [0]

            def link(ins_):
                linked[0] += 1
                ins_.then_inc(sem("dve_link"), 1)
                dve.wait_ge(sem("dve_link"), linked[0])

            def mark(ins_):
                linked[0] += 1
                ins_.then_inc(sem("dve_link"), 1)
                return linked[0]

            def need(n):
                dve.wait_ge(sem("dve_link"), n)

            def signal(ins_, name, n):
                ins_.then_inc(sem(name), 1)
                dve.wait_ge(sem(name), n)

            dve.wait_ge(sem("tok_in"), 16)
            dve.wait_ge(sem("consts"), 6)
            jp = tf[:, 7, :]
            link(dve.tensor_copy(tf[:, 0, :], tok[:]))
            link(dve.tensor_scalar(tf[:, 1, :], tf[:, 0, :], 1.0, None, ALU.not_equal))
            link(dve.tensor_tensor_scan(tf[:, 2, :], tf[:, 1, :], tf[:, 1, :], 1.0, ALU.mult, ALU.mult))
            link(dve.scalar_tensor_tensor(tf[:, 3, :], tf[:, 0, :], 4.0, jp, ALU.is_equal, ALU.mult))
            link(dve.tensor_tensor_scan(tf[:, 4, :], tf[:, 3, :], tf[:, 3, :], 0.0, ALU.max, ALU.max))
            link(dve.tensor_tensor(tf[:, 5, :], jp, tf[:, 4, :], ALU.subtract))
            link(dve.scalar_tensor_tensor(tf[:, 6, :], tf[:, 5, :], 1.0, tf[:, 2, :], ALU.add, ALU.mult))
            link(dve.tensor_scalar(tf[:, 5, :], tf[:, 6, :], 1.0, None, ALU.add))
            dve.wait_ge(sem("ident"), 1)
            dve.tensor_tensor(posD[:], tf[:, 5, :].rearrange("p (j o) -> p j o", o=1).broadcast_to([B, LT, B]),
                              ident[0:B, 0:B].rearrange("p (o b) -> p o b", o=1).broadcast_to([B, LT, B]),
                              ALU.mult).then_inc(sem("pos_spread"), 1)
            dve.memset(ones_b[:], 1.0).then_inc(sem("pos_spread"), 1)
            dve.wait_ge(sem("araw_in"), 16)
            dve.tensor_scalar(atmp[:], araw[:], 40.0, None, ALU.min).then_inc(sem("a_capped"), 1)
            dve.wait_ge(sem("bcs_in"), 64)
            dve.tensor_tensor(posb[:], posb[:], bpb[:], ALU.add).then_inc(sem("posb"), 1)
            dve.tensor_copy(sel[:], ident[0:LI, 0:LI].rearrange("p (t o) -> p t o", o=1).broadcast_to([LI, LI, B])
                            ).then_inc(sem("posb"), 1)
            for step in A_STEPS:
                if step[0] == "ring":
                    q = step[1]
                    kind, *rest = A_RING[q]
                    ps = bank[q % 4]
                    if a_reader(q) != "dve":
                        continue
                    dve.wait_ge(sem("a_ps"), q + 1)
                    if kind == "vec":
                        dve.tensor_copy(vec[:, 0:NV], ps[:, 0:NV]).then_inc(sem("a_read_dve"), 1)
                    elif kind == "pos":
                        k = rest[0]
                        dve.wait_ge(sem("consts"), 6)
                        signal(dve.tensor_scalar(OH[:, k * 512:(k + 1) * 512], ps[0:LT + 2, :], rowid[0:LT + 2, :], None,
                                                 ALU.is_equal), "onehot", k + 1)
                        dve.sem_inc(sem("a_read_dve"), 1)
                    elif kind == "w":
                        w, dc = rest
                        dve.wait_ge(sem("w_hi"), w * DC + dc + 1)
                        dve.tensor_tensor(WT[w][1][:, dc, :], ps[:], WT[w][0][:, dc, :].bitcast(F32), ALU.subtract
                                          ).then_inc(sem("a_read_dve"), 1)
                    else:
                        dve.tensor_copy(*patches(ps, *rest)).then_inc(sem("a_read_dve"), 1)
                    continue
                kind, i = step
                m = TILE_ORDER.index(i)
                if kind == "a2":
                    dve.wait_ge(sem("h0_copied"), m + 1)
                    link(dve.bn_stats(bst[:], h0s[:, m % 3, :]))
                    signal(dve.bn_aggr(mv0[:, i, :], bst[:]), "mv0", m + 1)
                elif kind == "a3":
                    dve.wait_ge(sem("sd0"), m + 1)
                    link(dve.reciprocal(rs0[:, i:i + 1], sd0[:, i:i + 1]))
                    if m >= 2:
                        dve.wait_ge(sem("xT_ps"), m - 1)
                    dve.tensor_scalar(xs[:, m % 2, :], h0s[:, m % 3, :], mv0[:, i, 0:1], rs0[:, i:i + 1], ALU.subtract,
                                      ALU.mult).then_inc(sem("x"), 1)
                elif kind == "a4":
                    dve.wait_ge(sem("xT_hi"), m + 1)
                    dve.tensor_tensor(xT_lo[:, :, i * P:(i + 1) * P],
                                      bank[6 + m % 2][:, 0:D].rearrange("p (c n) -> p c n", c=DC),
                                      xT_hi[:, :, i * P:(i + 1) * P].bitcast(F32), ALU.subtract).then_inc(sem("xT"), 1)
            dve.wait_ge(sem("x"), NT)
            dve.scalar_tensor_tensor(nmr0[:], mv0[:, :, 0], -1.0, rs0[:], ALU.mult, ALU.mult).then_inc(sem("nmr0"), 1)
            dve.wait_ge(sem("a_ln"), 1)
            link(dve.tensor_tensor(amat[:], araw[:], atmp[:], ALU.max))
            link(dve.tensor_scalar(amat[:], amat[:], -1.0, None, ALU.mult))
            link(dve.tensor_scalar(winv[:], amat[:], 1e-6, None, ALU.add))
            link(dve.reciprocal(winv[:], winv[:]))
            dve.wait_ge(sem("xT_ps"), NT)
            for q in range(HC * NB + 2):
                if q < HC * NB:
                    w, j = BLOCKS[BLOCK_ORDER[q // HC]][1], q % HC
                    dve.wait_ge(sem("dt_mm"), q + 1)
                    dve.tensor_scalar(spt[:, q % 4, 0:w], bank[q % 4][:, 0:w], vec[:, bdt0 + j:bdt0 + j + 1], 40.0,
                                      ALU.add, ALU.min).then_inc(sem("dt_capped"), 1)
                if q >= 2:
                    k = q - 2
                    w, j = BLOCKS[BLOCK_ORDER[k // HC]][1], k % HC
                    dve.wait_ge(sem("dt_ln"), k + 1)
                    if k >= 2:
                        dve.wait_ge(sem("dt_read"), k - 1)
                    dve.scalar_tensor_tensor(spj[:, k % 2, 0:w], bank[k % 4][:, 0:w], vec[:, bdt0 + j:bdt0 + j + 1],
                                             spt[:, k % 4, 0:w], ALU.add, ALU.max,
                                             accum_out=dts[:, j, k // HC:k // HC + 1]).then_inc(sem("dt_read"), 1)
            dve.wait_ge(sem("dt_read"), HC * NB)
            link(dve.reduce_sum(dt1[:], dts[:], AX))
            link(dve.tensor_scalar(dtc[:], dt1[:], 1.0 / N, 0.001, ALU.mult, ALU.max))
            link(dve.tensor_scalar(dt1[:], dtc[:], 2.0, None, ALU.min))
            dve.tensor_tensor(adt[:], amat[:], dt1[:].rearrange("p (c o) -> p c o", o=1).broadcast_to([P, HC, S]),
                              ALU.mult).then_inc(sem("adt"), 1)
            who, n = a_read(len(A_RING) - 2)
            dve.wait_ge(sem("a_ps"), len(A_RING))
            for k in range(2):
                dve.memset(ur[:, k].rearrange("p (a c) -> p a c", c=B)[:, ::N // B + 1, :], 0.0).then_inc(
                    sem("ur_pads"), 1)

            def mix(c):
                j, (a, b) = c // NB, reached(c % NB, 2)
                dve.wait_ge(sem("gated"), c + 1)
                h = hb[:, j % 2, a:b]
                dve.tensor_tensor(h, h, ur[:, j % 2, B + a:B + b], ALU.add).then_inc(sem("mixed"), 1)

            for step in C_STEPS:
                if step[0] == "proj":
                    j = step[1]
                    for nb in range(NB):
                        c, (a, b) = j * NB + nb, reached(nb, 1)
                        dve.wait_ge(sem("h_init"), c + 1)
                        if nb == NB - 1:
                            dve.wait_ge(sem("ur_pads"), 2)
                        u, h = ur[:, j % 2], hb[:, j % 2, a:b]
                        link(dve.scalar_tensor_tensor(h, u[:, a:b], cw[:, j, 0:1], h, ALU.mult, ALU.add))
                        dve.scalar_tensor_tensor(h, u[:, 2 * B + a:2 * B + b], cw[:, j, 2:3], h, ALU.mult, ALU.add
                                                 ).then_inc(sem("conv"), 1)
                        if (j, nb) in KERNEL_SUMS:
                            k = KERNEL_SUMS.index((j, nb))
                            if k == 0:
                                dve.wait_ge(sem("a_d"), 1)
                                link(dve.scalar_tensor_tensor(wmix[:], wmix[:], 1.0, winv[:], ALU.subtract, ALU.mult))
                                link(dve.tensor_tensor(wmix[:], wmix[:], bcs[:, 0], ALU.mult))
                                link(dve.tensor_tensor(wmix[:], wmix[:], bcs[:, 1], ALU.mult))
                            dve.wait_ge(sem("powers"), k + 1)
                            signal(dve.tensor_tensor(Eb[:, k], Eb[:, k],
                                                     wmix[:, k].rearrange("p (o s) -> p o s", o=1).broadcast_to(
                                                         [P, L, S]), ALU.mult), "power_w", k + 1)
                            signal(dve.reduce_sum(Kk[:, k, :], Eb[:, k], AX), "kernel_sum", k + 1)
                        if c >= 2:
                            mix(c - 2)
                elif step[0] == "turn":
                    turned(dve, step[1], "dve")
                else:
                    q = C_RING.index(("kT",))
                    dve.wait_ge(sem("c_ps"), q + 1)
                    dve.tensor_copy(kt[:].rearrange("k q j h -> k j q h"),
                                    bank[4 + q % 4][0:L, :].rearrange("k (j q h) -> k j q h", j=HC, h=QH)).then_inc(
                                        sem("kt_ready"), 1)
                    dve.wait_ge(sem("kt_ready"), 1)
                    dve.sem_inc(sem("c_read_dve"), 1)
                if step == ("proj", HC - 1):
                    mix(HC * NB - 2)
                    mix(HC * NB - 1)
            for v in range(1, 2 * QN, 2):
                dve.wait_ge(sem("ssm_mm"), v + 1)
                dve.tensor_copy(y[:, 4 * v:4 * v + 4, :].rearrange("p k t -> p (k t)"), bank[v % 4][:, 0:4 * L]).then_inc(
                    sem("y_dve"), 1)
                if v == 9:
                    dve.wait_ge(sem("w1_in"), 16 * E)
                    link(dve.reduce_sum(w1m[:], w1c[:].rearrange("p e c h -> p (e c) h"), AX))
                    link(dve.tensor_scalar(w1m[:], w1m[:], -1.0 / HF, None, ALU.mult))
                if v in (11, 13, 15, 17):
                    e = (v - 11) // 2
                    for dc in range(DC):
                        k = e * DC + dc
                        dve.tensor_scalar(w1c[:, e, dc, :], w1c[:, e, dc, :], w1m[:, k:k + 1], None, ALU.add).then_inc(
                            sem("w1_centred"), 1)
                if v in (23, 25):
                    dc = (v - 23) // 2
                    dve.wait_ge(sem("w1g_hi"), dc + 1)
                    dve.tensor_tensor(w1g_lo[:, :, dc, :], w1p[:, :, dc, :], w1g_hi[:, :, dc, :].bitcast(F32),
                                      ALU.subtract).then_inc(sem("w1g_split"), 1)
            for q, (kind, *rest) in enumerate(G_RING):
                ps = bank[4 + q % 4]
                if kind == "rw":
                    dve.wait_ge(sem("g_ps"), q + 1)
                    signal(dve.tensor_copy(rwT[:].rearrange("p c e -> p (c e)"), ps[:, 0:DC * E]), "rwT", 1)
                    dve.sem_inc(sem("g_read_dve"), 1)
                    for dc in range(DC):
                        dve.tensor_copy(zjunk[:, 0, dc * P:(dc + 1) * P],
                                        vec[:, rnb0 + dc:rnb0 + dc + 1].broadcast_to([P, P])).then_inc(
                                            sem("rnb_spread"), 1)
                        link(dve.tensor_scalar(rg[:, dc, :], rwT[:, dc, :], vec[:, rng0 + dc:rng0 + dc + 1], None,
                                               ALU.mult))
                    signal(dve.tensor_copy(rg_hi[:], rg[:]), "router_split", 1)
                    dve.tensor_tensor(rg_lo[:], rg[:], rg_hi[:].bitcast(F32), ALU.subtract).then_inc(
                        sem("router_split"), 1)
                elif kind == "cbc":
                    dve.wait_ge(sem("g_ps"), q + 1)
                    dve.tensor_copy(cbc[:], ps[:, 0:E]).then_inc(sem("g_read_dve"), 1)
                elif kind == "gram":
                    e = rest[0]
                    dve.wait_ge(sem("G_hi"), len(GRAM) * (e + 1))
                    for dc, c0, times in GRAM:
                        cols = slice(e * D + c0, e * D + c0 + P)
                        last = dve.scalar_tensor_tensor(G_lo[:, dc, cols], ps[:, dc * D + c0:dc * D + c0 + P], times,
                                                        G_hi[:, dc, cols].bitcast(F32), ALU.mult, ALU.subtract)
                        last.then_inc(sem("G_lo"), 1)
                    dve.wait_ge(sem("G_lo"), len(GRAM) * (e + 1))
                    dve.sem_inc(sem("g_read_dve"), 1)
                    if e == 0:
                        dve.wait_ge(sem("lb_in"), 16)
                        dve.wait_ge(sem("std_zero"), 2)
                        dve.wait_ge(sem("mAB"), 4)
                        dve.wait_ge(sem("m12"), 4)
                        b12 = Bst[0:12]
                        link(dve.tensor_copy(b12, lb12[:]))
                        link(dve.tensor_tensor(lb12[:], lb12[:], b12.bitcast(F32), ALU.subtract))
                        link(dve.tensor_scalar(lb12[:], lb12[:], mB[:], None, ALU.mult))
                        link(dve.scalar_tensor_tensor(b12.rearrange("p e h -> p (e h)"),
                                                      b12.bitcast(F32).rearrange("p e h -> p (e h)"), mA[:],
                                                      lb12[:].rearrange("p e h -> p (e h)"), ALU.mult, ALU.add))
                        for k in range(E):
                            last = dve.tensor_scalar(b12[:, k, :], b12[:, k, :].bitcast(F32), m12[:, k:k + 1], None,
                                                     ALU.mult)
                            if k < E - 1:
                                link(last)
                        last.then_inc(sem("Bst"), 1)
                    if e == 1:
                        dve.wait_ge(sem("w2_hi"), 1)
                        for k in range(2):
                            es = slice(2 * k, 2 * k + 2)
                            dve.tensor_tensor(w2_lo[:, es], w2raw[:, es], w2_hi[:, es].bitcast(F32), ALU.subtract
                                              ).then_inc(sem("w2_split"), 1)
            for kind, *rest in F_STEPS:
                i = rest[0]
                if kind == "out":
                    n = AUX.index((kind, i))
                    dve.wait_ge(sem("out_mm"), i + 1)
                    dve.wait_ge(sem("xb"), i + 1)
                    signal(dve.tensor_tensor(r1[:, i % 2, :], bank[4 + n % 4][:, 0:D], xb[:, i % 2, :], ALU.add), "r1", i + 1)
                    dve.sem_inc(sem("aux_read_dve"), 1)
                elif kind == "ln1":
                    tiles, ts = FB[i], slice(FB[i][0], FB[i][-1] + 1)
                    rs = [r1[:, t % 2, :] for t in tiles]
                    at_ = [mark(dve.bn_stats(bst1[:, t % 2], rs[n])) for n, t in enumerate(tiles)]
                    for n, t in enumerate(tiles):
                        need(at_[n])
                        dve.bn_aggr(mv1[:, t, :], bst1[:, t % 2]).then_inc(sem("mv1"), 1)
                    dve.wait_ge(sem("mv1"), ts.stop)
                    dve.wait_ge(sem("sd1"), i + 1)
                    link(dve.reciprocal(rs1[:, ts], sd1[:, ts]))
                    at_ = [mark(dve.tensor_scalar(r, r, mv1[:, t, 0:1], rs1[:, t:t + 1], ALU.subtract, ALU.mult))
                           for t, r in zip(tiles, rs)]
                    for n, r in enumerate(rs):
                        need(at_[n])
                        at_[n] = mark(dve.tensor_tensor(r, r, lng_b[:], ALU.mult))
                    for n, t in enumerate(tiles):
                        need(at_[n])
                        dve.wait_ge(sem("h0b"), t + 1)
                        dve.tensor_tensor(h1[:, t, :], rs[n], h0r[:, t % 2, :], ALU.add).then_inc(sem("h1"), 1)
                elif kind == "h1":
                    tiles = FB[i]
                    at_ = []
                    for t in tiles:
                        dve.wait_ge(sem("h1"), t + 1)
                        at_.append(mark(dve.bn_stats(bst2[:, t % 2], h1[:, t, :])))
                    for n, t in enumerate(tiles):
                        need(at_[n])
                        dve.bn_aggr(mv2[:, t, :], bst2[:, t % 2]).then_inc(sem("mv2"), 1)
                elif kind == "x2":
                    tiles, ts = FB[i], slice(FB[i][0], FB[i][-1] + 1)
                    dve.wait_ge(sem("mv2"), ts.stop)
                    dve.wait_ge(sem("sd2"), i + 1)
                    link(dve.reciprocal(rs2[:, ts], sd2[:, ts]))
                    if i >= 1:
                        dve.wait_ge(sem("x2T_ps"), ts.start)
                        dve.wait_ge(sem("varE"), E * ts.start)
                    for t in tiles:
                        dve.tensor_scalar(x2s[:, t % 2, :], h1[:, t, :], mv2[:, t, 0:1], rs2[:, t:t + 1], ALU.subtract,
                                          ALU.mult).then_inc(sem("x2"), 1)
                    link(dve.tensor_tensor(v2n[:, ts], mv2[:, ts, 1], rs2[:, ts], ALU.mult))
                    dve.tensor_tensor(v2n[:, ts], v2n[:, ts], rs2[:, ts], ALU.mult).then_inc(sem("v2n"), 1)
                elif kind == "x2T":
                    n = AUX.index((kind, i))
                    ts = slice(i % 2 * P, (i % 2 + 1) * P)
                    dve.wait_ge(sem("x2T_hi"), i + 1)
                    signal(dve.tensor_tensor(x2T_lo[:, i // 2 % 2, :, ts],
                                             bank[4 + n % 4][:, 0:D].rearrange("p (c n) -> p c n", c=DC),
                                             x2T_hi[:, i // 2 % 2, :, ts].bitcast(F32), ALU.subtract), "x2T", i + 1)
                elif kind in ("z0", "z1"):
                    if kind == "z0":
                        n = AUX.index(("x2T", i))
                        if i % 2 == 0:
                            own = slice(i, FB[i // 2][-1] + 1)
                            dve.wait_ge(sem("sdr"), i // 2 + 1)
                            link(dve.reciprocal(rs2r[:, own], rs2r[:, own]))
                        dve.wait_ge(sem("logit_mm"), i + 1)
                        dve.scalar_tensor_tensor(lg[:, i, :], bank[4 + n % 4][:, D:D + E], rs2r[:, i:i + 1], cbc[:],
                                                 ALU.mult, ALU.add).then_inc(sem("logits"), 1)
                    n = AUX.index((kind, i))
                    half = int(kind == "z1")
                    dve.wait_ge(sem("z_mm"), z_count(kind, i))
                    for k in range(2):
                        e, done = 2 * half + k, var_count(kind, i) - 2 + k
                        if done >= 2:
                            dve.wait_ge(sem("varE"), done - 1)
                        dve.tensor_tensor_reduce(zjunk[:, k], bank[4 + n % 4][:, k * D:(k + 1) * D], x2s[:, i % 2, :],
                                                 1.0, 0.0, ALU.mult, ALU.add, varE[:, i, e:e + 1]).then_inc(
                                                     sem("varE"), 1)
                    dve.wait_ge(sem("varE"), var_count(kind, i))
                    dve.sem_inc(sem("aux_read_dve"), 1)
                elif kind == "std":
                    tiles, ts = FB[i], slice(FB[i][0], FB[i][-1] + 1)
                    w = len(tiles)
                    dve.wait_ge(sem("stdE"), i + 1)
                    if i >= 1:
                        dve.wait_ge(sem("stdT_ps"), ts.start)
                    signal(dve.tensor_copy(s3[:, 0:w, 0, :], stdE[:, ts, :]), "s3", 3 * i + 1)
                    dve.tensor_tensor(s3[:, 0:w, 1, :], stdE[:, ts, :], s3[:, 0:w, 0, :].bitcast(F32),
                                      ALU.subtract).then_inc(sem("s3"), 1)
                    dve.tensor_copy(s3[:, 0:w, 2, :], s3[:, 0:w, 0, :].bitcast(F32)).then_inc(sem("s3"), 1)
                elif kind == "route1":
                    t0, t1 = FB[i][0], FB[i][-1] + 1
                    ts, w = slice(t0, t1), t1 - t0
                    dve.wait_ge(sem("logits"), t1)
                    link(dve.tensor_reduce(rsum[:, ts], lg[:, ts, :], AX, ALU.max))
                    dve.tensor_tensor(gx[:, ts, :], lg[:, ts, :], spread(rsum[:, ts], w), ALU.subtract).then_inc(
                        sem("logit_rel"), 1)
                elif kind == "route3":
                    ts = slice(FB[i][0], FB[i][-1] + 1)
                    dve.wait_ge(sem("top2"), i + 1)
                    link(dve.reciprocal(rank[:, ts, :], rank[:, ts, :]))
                    signal(dve.tensor_tensor(wE[:, ts, :], top[:, ts, :], rank[:, ts, :], ALU.mult), "wE", i + 1)
                elif kind == "hid":
                    b, e, k = rest
                    q, w = hid_job(b, e, k), P * len(FB[b])
                    dve.wait_ge(sem("hid_hi"), q + 1)
                    hs = slice(2 * k, 2 * k + 2)
                    dve.scalar_tensor_tensor(hid_lo[:, e % 2, hs, 0:w],
                                             bank[q % 2][:].rearrange("p (c n) -> p c n", c=2)[:, :, 0:w], 0.0,
                                             hid_hi[:, e % 2, hs, 0:w].bitcast(F32), ALU.max, ALU.subtract).then_inc(
                                                 sem("hid_lo"), 1)
                elif kind == "w2":
                    b, e = rest
                    q = b * E + e
                    dve.wait_ge(sem("w2_mm"), q + 1)
                    if e:
                        dve.wait_ge(sem("combined"), q)
                    else:
                        dve.wait_ge(sem("wE"), b + 1)
                    for n, i in enumerate(FB[b]):
                        a, ps = acc[:, b % 2, n, :], bank[2 + q % 2][:, n * D:(n + 1) * D]
                        if e == 0:
                            if i >= 4:
                                dve.wait_ge(sem(f"out_stored{i % 4}"), 16 * (i // 4))
                            last = dve.tensor_scalar(a, ps, wE[:, i, 0:1], None, ALU.mult)
                        else:
                            last = dve.scalar_tensor_tensor(a, ps, wE[:, i, e:e + 1], a, ALU.mult, ALU.add)
                    last.then_inc(sem("combined"), 1)
                elif kind == "fin1":
                    dve.wait_ge(sem("combined"), E * (i + 1))
                    at_ = [mark(dve.bn_stats(bst3[:, n], acc[:, i % 2, n, :])) for n in range(len(FB[i]))]
                    for n, t in enumerate(FB[i]):
                        need(at_[n])
                        dve.bn_aggr(mv3[:, t, :], bst3[:, n]).then_inc(sem("mv3"), 1)
                elif kind == "fin2":
                    ts = slice(FB[i][0], FB[i][-1] + 1)
                    dve.wait_ge(sem("mv3"), ts.stop)
                    dve.wait_ge(sem("sd3"), i + 1)
                    link(dve.reciprocal(rs3[:, ts], sd3[:, ts]))
                    for n, t in enumerate(FB[i]):
                        a = acc[:, i % 2, n, :]
                        dve.tensor_scalar(a, a, mv3[:, t, 0:1], rs3[:, t:t + 1], ALU.subtract, ALU.mult).then_inc(
                            sem("fin_norm"), 1)



def kernel(**inputs):
    import concourse.bacc as _bacc
    from concourse.bass_utils import run_bass_kernel_spmd as _run
    import numpy as _np

    nc = _bacc.Bacc("TRN2", target_bir_lowering=False, num_devices=1)
    arrays, ins = {}, {}
    for name, value in inputs.items():
        a = _np.ascontiguousarray(value)
        arrays[f"in_{name}_dram"] = a
        ins[name] = nc.dram_tensor(f"in_{name}_dram", a.shape, mybir.dt.from_np(a.dtype), kind="ExternalInput").ap()
    batch, seq = inputs["x"].shape[0], 36 + inputs["x_txt"].shape[1]
    out = nc.dram_tensor("out_0_dram", (batch, seq, inputs["L0_tok_W_proj"].shape[0]), F32, kind="ExternalOutput").ap()
    build_kernel(nc, ins, out)
    r = _run(nc, [arrays], core_ids=[0])
    return r.results[0]["out_0_dram"]
```

```python
from contextlib import ExitStack

import concourse.bass as bass
from concourse import mybir

F32 = mybir.dt.float32
F32R = mybir.dt.float32r
I32 = mybir.dt.int32
ALU = mybir.AluOpType
ACT = mybir.ActivationFunctionType
AX = mybir.AxisListType.X
P = 128


def build_kernel(nc, ins, out):
    B, IMG, _, CH = ins["x"].shape
    LT = ins["x_txt"].shape[1]
    D, PD = ins["L0_tok_W_proj"].shape
    PS = 16
    HP = IMG // PS
    LI = HP * HP
    L = LI + LT
    H, S = ins["L0_attn_A_raw"].shape
    E, _, HF = ins["L0_ffn_w1"].shape
    N = L * B
    NT = N // P
    TPT = P // B
    NTI = LI // TPT
    DC, HC = D // P, H // P
    EPS = 1e-5
    BLOCKS = [(n, min(512, N - n)) for n in range(0, N, 512)]
    NB = len(BLOCKS)
    GB = B // 2
    ROWS = GB * HP
    CK = PD // P
    KT = CK // 2
    PWC = PS * CH
    NH0 = NT - NTI
    QN, QH = 16, H // HC // 16
    QC = QH * HC

    stack = ExitStack()
    with stack:
        def sb(name, shape, dt=F32):
            return stack.enter_context(nc.sbuf_tensor(name, shape, dt))

        sems = {}

        def sem(name):
            if name not in sems:
                sems[name] = stack.enter_context(nc.semaphore(name))
            return sems[name]

        ident = sb("ident", [P, P])
        vec = sb("vec", [P, 52])
        cw = sb("cw", [P, HC, 3])
        rowid = sb("rowid", [P, 1])
        mv0 = sb("mv0", [P, NT, 2])
        sd0 = sb("sd0", [P, NT])
        rs0 = sb("rs0", [P, NT])
        nmr0 = sb("nmr0", [P, NT])
        bst = sb("bst", [P, 6])
        bst1 = sb("bst1", [P, 2, 6])
        bst2 = sb("bst2", [P, 2, 6])
        bst3 = sb("bst3", [P, 2, 6])
        mv1 = sb("mv1", [P, NT, 2])
        sd1 = sb("sd1", [P, NT])
        rs1 = sb("rs1", [P, NT])
        mv2 = sb("mv2", [P, NT, 2])
        sd2 = sb("sd2", [P, NT])
        rs2 = sb("rs2", [P, NT])
        v2n = sb("v2n", [P, NT])
        rs2r = sb("rs2r", [P, NT])
        ones_b = sb("ones_b", [B, LT + 2])
        mv3 = sb("mv3", [P, NT, 2])
        sd3 = sb("sd3", [P, NT])
        rs3 = sb("rs3", [P, NT])
        epsc = sb("epsc", [P, 1])
        onec = sb("onec", [P, 1])
        dts = sb("dts", [P, HC, NB])
        dt1 = sb("dt1", [P, HC])
        dtc = sb("dtc", [P, HC])
        rwT = sb("rwT", [P, DC, E])
        rg = sb("rg", [P, DC, E])
        rg_hl = sb("rg_hl", [P, DC, 2, E], F32R)
        cbc = sb("cbc", [P, E])
        bout_b = sb("bout_b", [P, D])
        lng_b = sb("lng_b", [P, D])
        lnb_b = sb("lnb_b", [P, D])
        ong_b = sb("ong_b", [P, D])
        onb_b = sb("onb_b", [P, D])
        varE = sb("varE", [P, NT, E])
        stdE = sb("stdE", [P, NT, E])
        s3 = sb("s3", [P, 2, 3, E], F32R)
        lg = sb("lg", [P, NT, E])
        gx = sb("gx", [P, NT, E])
        rank = sb("rank", [P, NT, E])
        top = sb("top", [P, NT, E])
        pair = sb("pair", [P, 2, 6])
        rsum = sb("rsum", [P, NT])
        wE = sb("wE", [P, NT, E])
        eid = sb("eid", [P, E])
        m12 = sb("m12", [12, E])
        mA = sb("mA", [12, 1])
        mB = sb("mB", [12, 1])
        w1m = sb("w1m", [P, E * DC])

        base = (nc.sbuf_base + 63) // 64 * 64

        def at(name, shape, offset, dt=F32):
            return nc.alloc_sbuf_tensor_at(name, shape, dt, offset=offset)

        def size(*shape):
            n = 4
            for s in shape:
                n *= s
            return (n + 63) // 64 * 64

        def place(start, end, *wanted):
            got = []
            for name, shape, *dt in wanted:
                got.append(at(name, shape, start, *dt))
                start += size(*shape[1:])
            assert start <= end, (wanted[-1][0], start, end)
            return got

        R1 = base
        R2 = R1 + 2 * size(DC, N)
        R3 = R2 + 6 * size(DC, H)
        R4 = R3 + size(5 * N + 4 * B)
        R5 = R4 + size(H * B)
        R6 = R5 + 3 * size(L * QC)
        R7 = R6 + size(2, D) + size(D)
        TOP = nc.sbuf_usable_end

        xT_hi, xT_lo = place(R1, R2, ("xT_hi", [P, DC, N], F32R), ("xT_lo", [P, DC, N], F32R))
        y = at("y", [P, H // HC, L], R1)
        WT = place(R2, R3, *[(f"WT{w}_{v}", [P, DC, H], F32R) for w in ("dt", "x", "g") for v in ("hi", "lo")])
        WT = [WT[0:2], WT[2:4], WT[4:6]]
        w1c, gfb = place(R2, R3, ("w1c", [P, E, DC, HF]), ("gfb", [P, E, HF]))
        h0r, xb, r1, x2s, yT_hi, acc = place(R2, R2 + size(E, DC, HF), ("h0r", [P, 2, D]), ("xb", [P, 2, D]),
                                          ("r1", [P, 2, D]), ("x2s", [P, 2, D]), ("yT_hi", [P, 2, HC, P], F32R), ("acc", [P, 2, 2, D]))
        (w1p,) = place(R3 + size(E, DC, HF), R4, ("w1p", [P, E, DC, HF]))
        (Bst,) = place(R2 + size(E, DC, HF), R3, ("Bst", [P, E, HF], F32R))
        (XI,) = place(R3, R4, ("XI", [ROWS, 2, HP, PD]))
        ur, hb, gb0 = place(R3, R4, ("ur", [P, 2, N + 2 * B]), ("hb", [P, 2, N]), ("gb0", [P, N]))
        w1g_hi, w1g_lo, x2T_hi, x2T_lo, stdT = place(
            R3, R4, ("w1g_hi", [P, E, DC, HF], F32R), ("w1g_lo", [P, E, DC, HF], F32R),
            ("x2T_hi", [P, 2, DC, 2 * P], F32R), ("x2T_lo", [P, 2, DC, 2 * P], F32R), ("stdT", [P, 2, 2 * P], F32R))
        patchT, WpT, Wpr, Wr0, Wr1, Wr2, posD = place(
            R4, R5, ("patchT", [P, CK, LI, B]), ("WpT", [P, CK, D]), ("Wpr", [P, DC, PD]), ("Wr0", [P, HC, D]),
            ("Wr1", [P, HC, D]), ("Wr2", [P, HC, D]), ("posD", [B, LT, B]))
        Wr = [Wr0, Wr1, Wr2]
        spt, spj = place(R4, R5, ("spt", [P, 4, 512]), ("spj", [P, 2, 512]))
        (U2,) = place(R4, R5, ("U2", [L, HC, H // HC, B]))
        w2_hi, w2_lo, hid_hi, hid_lo, G_hi, G_lo = place(
            R4, R5, ("w2_hi", [P, E, HC, D], F32R), ("w2_lo", [P, E, HC, D], F32R),
            ("hid_hi", [P, 2, HC, 2 * P], F32R), ("hid_lo", [P, 2, HC, 2 * P], F32R),
            ("G_hi", [P, DC, E * D], F32R), ("G_lo", [P, DC, E * D], F32R))
        w2raw = at("w2raw", [P, E, HC, D], R4 + size(E, HC, D))
        w1cT = place(R4 + 2 * size(E, HC, D), R5, *[(f"w1cT{e}", [P, HC, D]) for e in range(E)])
        OH, tabl, posb, bpb, sel, h0s, xs, tok, tf, zrow = place(
            R5, R6, ("OH", [LT + 2, LT * B]), ("tabl", [LT + 2, D]), ("posb", [LI, D]), ("bpb", [LI, D]),
            ("sel", [LI, LI, B]), ("h0s", [P, NH0, D]), ("xs", [P, 2, D]), ("tok", [B, LT], I32), ("tf", [B, 8, LT]),
            ("zrow", [QN, (L - 1) * QC // 4]))
        Eb, gb1 = place(R5, R6, ("Eb", [P, HC, L, S]), ("gb1", [P, N]))
        gb = [gb0, gb1]
        Tb = place(R5, R6, *[(f"Tb{i}", [L, L, QC]) for i in range(3)])
        h1, Wo_hi, Wo_lo = place(R5, R6, ("h1", [P, NT, D]), ("Wo_hi", [P, HC, D], F32R), ("Wo_lo", [P, HC, D], F32R))
        zjunk, rwt = place(R6, TOP, ("zjunk", [P, 2, D]), ("rwt", [E, D]))
        (Kk,) = place(R6, TOP, ("Kk", [P, HC, L]))
        (kt,) = place(R6, TOP, ("kt", [L, QN, HC, QH]))
        lb12, lbr = place(R3 + 2 * size(E, DC, HF), R4, ("lb12", [3 * E, HF]), ("lbr", [3 * E, HF], F32R))
        (Wor0,) = place(R3 + 2 * size(E, DC, HF) + 2 * size(2, DC, 2 * P), R4, ("Wor0", [P, H]))
        (Wor1,) = place(R6, TOP, ("Wor1", [P, H]))
        Wor = [Wor0, Wor1]

        vec_rows, araw, bcs, amat, atmp, adt, wmix, winv, kio = place(
            R7, TOP, ("vec_rows", [52, P]), ("araw", [P, HC, S]), ("bcs", [P, 2, HC, S]), ("amat", [P, HC, S]),
            ("atmp", [P, HC, S]), ("adt", [P, HC, S]), ("wmix", [P, HC, S]), ("winv", [P, HC, S]), ("kio", [P, L]))
        (yT_lo,) = place(R7, TOP, ("yT_lo", [P, HC, P], F32R))

        h0d = nc.dram_tensor("h0_spill", [NT, P, D], F32).ap()
        kpd = nc.dram_tensor("ssm_kernels", [QN, 2 * L - 1, QC], F32).ap()
        bank = [stack.enter_context(nc.psum_tensor(f"bank{i}", [P, 512], F32)) for i in range(8)]

        x = ins["x"]
        img = x.rearrange("(g b) (hp py) w c -> g (b hp) py (w c)", g=2, py=PS)
        w_dram = [ins[n].rearrange("(c p) d -> p c d", p=P) for n in ("L0_attn_W_dt", "L0_attn_W_x", "L0_attn_W_g")]

        def rows(name):
            a = ins[name]
            while len(a.shape) > 1:
                a = a.rearrange("a b -> (a b)")
            return a.rearrange("(r p) -> r p", p=P)

        def vecs(name):
            first = 0
            for n in VECS:
                count = rows(n).shape[0]
                if n == name:
                    return first, count
                first += count

        VECS = ["L0_attn_b_x", "L0_attn_b_g", "L0_attn_b_dt", "L0_attn_conv_b", "L0_ffn_rn_g", "L0_ffn_rn_b"]
        NV = sum(rows(n).shape[0] for n in VECS)
        bx0, bg0, bdt0, cb0, rng0, rnb0 = (vecs(n)[0] for n in VECS)
        state = lambda n: ins[n].rearrange("(c p) s -> p c s", p=P)

        TILE_ORDER = list(range(NTI, NT)) + list(range(NTI))
        BLOCK_ORDER = [3, 4, 0, 1, 2]
        H0_OUT = [(0, NH0), (NH0, NH0 + 3), (NH0 + 3, NH0 + 6), (NH0 + 6, NT)]

        def ready_tiles(nb):
            t0, t1 = BLOCKS[nb][0] // P, (BLOCKS[nb][0] + BLOCKS[nb][1]) // P
            return 1 + max(TILE_ORDER.index(t) for t in range(t0, t1))

        PREP = [("pos", 0), ("pos", 1), ("vec",)] + [("wp", c) for c in range(0, CK, 2)]
        IMAGES = [("img", half, g, wp) for g in range(2) for wp in range(HP) for half in range(2)]
        WEIGHTS = [("w", w, dc) for w in range(3) for dc in range(DC)]
        A_RING = PREP + IMAGES + WEIGHTS
        LAST_IMAGES = (len(PREP) + len(IMAGES) - 2, len(PREP) + len(IMAGES) - 1)

        def a_reader(q):
            kind = A_RING[q][0]
            if kind == "img":
                return "act" if q % 2 else "dve"
            return "act" if kind == "wp" else "dve"

        def a_read(q):
            who = a_reader(q)
            return who, sum(a_reader(k) == who for k in range(q + 1))

        A_STEPS = [("ring", q) for q in range(len(PREP))]
        ahead = list(range(len(PREP), len(A_RING)))
        for k in range(NT + 3):
            A_STEPS += [(f"a{s + 1}", TILE_ORDER[k - s]) for s in (3, 2, 1, 0) if 0 <= k - s < NT]
            count = 3 if k < NH0 else 1
            A_STEPS += [("ring", q) for q in ahead[:count]]
            ahead = ahead[count:]
            if k in (NT, NT + 1):
                A_STEPS.append(("dt", k - NT))
        assert not ahead

        FB = [list(range(i, min(i + 2, NT))) for i in range(0, NT, 2)]
        PAIR0 = {1: 0, 2: 3, 3: 5}
        EXPERTS = [("hid", 0, 0), ("hid", 0, 1), ("hid", 1, 0), ("hid", 1, 1), ("w2", 0), ("hid", 2, 0), ("hid", 2, 1),
                   ("w2", 1), ("hid", 3, 0), ("hid", 3, 1), ("w2", 2), ("w2", 3)]
        BESIDE = [["x2"], [], ["x2T0", "x2T1"], ["z00"], ["z10"], ["z01"], ["z11"], ["std", "+yT0"],
                  ["stdT0", "stdT1", "+out0", "+yT1"], ["+out1", "+ln1"], ["route1", "+h1"], ["route2"]]

        def beside(b, n):
            got = []
            for s in BESIDE[n]:
                nb = b + 1 + s.startswith("+")
                s = s.lstrip("+")
                if not 0 <= nb < len(FB):
                    continue
                if s[:-1] in ("yT", "out", "x2T", "z0", "z1", "stdT"):
                    if int(s[-1]) < len(FB[nb]):
                        got.append((s[:-1], FB[nb][int(s[-1])]))
                else:
                    got.append((s, nb))
            return got

        PROLOGUE = {(-2, 7): [("gram", 0)], (-2, 8): [("gram", 1)], (-2, 9): [("gram", 2)], (-2, 10): [("gram", 3)],
                    (-1, 2): [("w2split", 0)], (0, 3): [("w2split", 1)]}
        F_STEPS = []
        for b in range(-2, len(FB)):
            for n, (kind, *rest) in enumerate(EXPERTS):
                if b >= 0:
                    F_STEPS.append((kind, b, *rest))
                F_STEPS += beside(b, n) + PROLOGUE.get((b, n), [])
                if b >= 1 and n in (1, 2):
                    F_STEPS.append((f"fin{(1, 2).index(n) + 1}", b - 1))
                if b >= 0 and n == 2:
                    F_STEPS.append(("route3", b))
        F_STEPS += [("fin1", len(FB) - 1), ("fin2", len(FB) - 1)]
        AUX = [s for s in F_STEPS if s[0] in ("yT", "out", "x2T", "z0", "z1", "stdT", "gram")]
        C_STEPS = [("proj", 0), ("proj", 1), ("turn", 0), ("proj", 2), ("turn", 1), ("proj", 3), ("kernels",), ("turn", 2),
                   ("turn", 3)]

        KERNEL_SUMS = {("turn", 0): [0], ("turn", 1): [1, 2], (3, 1): [3]}
        MIX_LAG = 3

        def reached(nb, lag):
            n0, w = BLOCKS[nb]
            return max(0, n0 - lag * B), (N if nb == NB - 1 else n0 + w - lag * B)

        C_RING = []
        for step in C_STEPS:
            if step[0] == "kernels":
                C_RING.append(("kT",))
            if step[0] == "turn":
                C_RING += [("uT", step[1], k) for k in range(B // 4)]

        def c_reader(q):
            if C_RING[q][0] != "uT":
                return "dve"
            _, j, k = C_RING[q]
            return "act" if (k < 3, True, k % 2 == 0, k % 2 == 0)[j] else "dve"

        def c_read(q):
            who = c_reader(q)
            return who, sum(c_reader(k) == who for k in range(q + 1))

        G_RING = [("rw",), ("cbc",), ("wo", 0), ("wo", 1)] + [("w1T", e, k) for e in range(E) for k in range(2)]
        BEHIND = {15: [0], 19: [1], 29: [2, 3]}

        GRAM = [(0, 0, 1.0), (1, 0, 2.0), (1, P, 1.0)]

        AUX = G_RING + AUX

        AUX_READ = {"yT": "aux_read_dve", "stdT": "aux_read_act", "out": "aux_read_dve", "x2T": "logits",
                    "z0": "aux_read_dve", "z1": "aux_read_dve", "gram": "aux_read_dve", "rw": "aux_read_dve",
                    "cbc": "aux_read_dve", "wo": "aux_read_dve"}

        def reader(job):
            if job[0] == "w1T":
                return ("aux_read_act", "aux_read_dve")[job[2]]
            return AUX_READ[job[0]]

        def aux_read(q):
            name = reader(AUX[q])
            return name, sum(reader(j) == name for j in AUX[:q + 1])

        def hid_job(b, e, k):
            return (b * E + e) * 2 + k

        def store(eng, i):
            if i < 0:
                return
            eng.wait_ge(sem("result"), i + 1)
            src = acc[:, i // 2 % 2, i % 2, :]
            eng.dma_start(out[:, TPT * i:TPT * (i + 1), :].rearrange("b t d -> t b d"), src).then_inc(
                sem(f"out_stored{i % 4}"), 16)

        def h0_out(eng):
            for n in range(len(H0_OUT)):
                eng.wait_ge(sem(f"h0_stored{n}"), 32 if n == len(H0_OUT) - 1 else 16)

        def split3(pe, out_ap, a_hi, a_lo, b_hi, b_lo, start, stop):
            pe.matmul(out_ap, a_hi, b_hi, start=start, stop=False)
            pe.matmul(out_ap, a_hi, b_lo, start=False, stop=False)
            return pe.matmul(out_ap, a_lo, b_hi, start=False, stop=stop)

        def copy_b(act, o, i, bias):
            return act.activation(o, i, ACT.Identity, bias=bias)

        def log1p(act, q):
            w = BLOCKS[BLOCK_ORDER[q // HC]][1]
            act.wait_ge(sem("dt_exp"), q + 1)
            act.activation(spt[:, q % 4, 0:w], spt[:, q % 4, 0:w], ACT.Ln, bias=onec[:]).then_inc(sem("dt_ln"), 1)

        def patches(ps, half, g, wp):
            dst = patchT[:].rearrange("p c (hp wp) b -> p c hp wp b", wp=HP)[
                :, half * KT:(half + 1) * KT, :, wp, g * GB:(g + 1) * GB]
            return dst, ps[:, 0:KT * ROWS].rearrange("p (k b hp) -> p k hp b", k=KT, hp=HP)

        def mix(dve, c):
            j, (a, b) = c // NB, reached(c % NB, 2)
            dve.wait_ge(sem("gated"), c + 1)
            h = hb[:, j % 2, a:b]
            dve.tensor_tensor(h, h, ur[:, j % 2, B + a:B + b], ALU.add).then_inc(sem("mixed"), 1)

        def turned(eng, j, who, behind=()):
            for k in range(B // 4):
                q = C_RING.index(("uT", j, k))
                if c_reader(q) != who:
                    continue
                eng.wait_ge(sem("c_ps"), q + 1)
                dst = U2[:, j, :, 4 * k:4 * k + 4]
                src = bank[4 + q % 4][0:L, :].rearrange("p (b h) -> p h b", b=4)
                ins_ = (eng.activation(dst, src, ACT.Identity) if who == "act" else eng.tensor_copy(dst, src))
                ins_.then_inc(sem(f"c_read_{who}"), 1)
                for c in behind[:1]:
                    mix(eng, c)
                behind = behind[1:]
            for c in behind:
                mix(eng, c)

        Z_ORDER = [s for s in F_STEPS if s[0] in ("z0", "z1")]

        def z_count(kind, i):
            return Z_ORDER.index((kind, i)) + 1

        def var_count(kind, i):
            return 2 * z_count(kind, i)

        def spread(a, w):
            return a.rearrange("p (t o) -> p t o", o=1).broadcast_to([P, w, E])
        block = stack.enter_context(nc.Block())

        @block.sync
        def _(sp):
            sp.dma_start(tok[:], ins["x_txt"]).then_inc(sem("tok_in"), 16)
            at_row = 0
            for n in VECS:
                a = rows(n)
                sp.dma_start(vec_rows[at_row:at_row + a.shape[0], :], a).then_inc(sem("vecs_in"), 16)
                at_row += a.shape[0]
            sp.dma_start(tabl[:], ins["L0_txt_weights"][0:LT + 2, :]).then_inc(sem("table_in"), 16)
            for g in range(2):
                for wp in range(HP):
                    sp.dma_start(XI[:, g, wp].rearrange("p (y k) -> p y k", k=PWC),
                                 img[g][:, :, wp * PWC:(wp + 1) * PWC]).then_inc(sem(f"img_in{g}{wp // 2}"), 16)
            for w in range(3):
                sp.dma_start(Wr[w][:], w_dram[w]).then_inc(sem(f"w_in{w}"), 16)
            for n, (m0, m1) in enumerate(H0_OUT):
                sp.wait_ge(sem("h0_copied"), m1)
                t0 = TILE_ORDER[m0]
                if m0 % NH0 + m1 - m0 <= NH0:
                    sp.dma_start(h0d[t0:t0 + m1 - m0].rearrange("t p d -> p t d"),
                                 h0s[:, m0 % NH0:m0 % NH0 + m1 - m0, :]).then_inc(sem(f"h0_stored{n}"), 16)
                else:
                    cut = NH0 - m0 % NH0
                    sp.dma_start(h0d[t0:t0 + cut].rearrange("t p d -> p t d"),
                                 h0s[:, m0 % NH0:, :]).then_inc(sem(f"h0_stored{n}"), 16)
                    sp.dma_start(h0d[t0 + cut:t0 + m1 - m0].rearrange("t p d -> p t d"),
                                 h0s[:, 0:m1 - m0 - cut, :]).then_inc(sem(f"h0_stored{n}"), 16)
                if n == 0:
                    for k in range(2):
                        sp.dma_start(bcs[:, k], state(("L0_attn_B_ssm", "L0_attn_C_ssm")[k])).then_inc(sem("bcs_in"), 16)
                    sp.dma_start(cw[:], ins["L0_attn_conv_w"].rearrange("(c p) o k -> p c (o k)", p=P)).then_inc(
                        sem("cw_in"), 16)
                    for t, name in ((bout_b, "L0_attn_b_out"), (lng_b, "L0_attn_ln_g"), (lnb_b, "L0_attn_ln_b"),
                                    (ong_b, "L0_ffn_on_g"), (onb_b, "L0_ffn_on_b")):
                        sp.dma_start(t[:], ins[name].partition_broadcast(P)).then_inc(sem("rows_in"), 16)
                    sp.wait_ge(sem("zrow"), 1)
                    for k in range(4):
                        part = (L - 1) * QC // 4
                        sp.dma_start(kpd.rearrange("q k c -> q (k c)")[:, L * QC + k * part:L * QC + (k + 1) * part],
                                     zrow[:]).then_inc(sem("zrow_stored"), 16)
            sp.wait_ge(sem("kt_ready"), 1)
            sp.wait_ge(sem("zrow_stored"), 64)
            sp.dma_start(kpd[:, 0:L, :].rearrange("q k c -> k q c"),
                         kt[:].rearrange("k q j h -> k q (j h)")).then_inc(sem("kernels_stored"), 16)
            sp.wait_ge(sem("kernels_stored"), 16)
            sp.dma_start(rwt[:], ins["L0_ffn_router_w"]).then_inc(sem("router_in"), 16)
            for q in range(QN):
                if q == 0:
                    sp.wait_ge(sem("kernel_sum"), HC)
                if q == 2:
                    sp.wait_ge(sem("gated"), HC * NB)
                if q >= 3:
                    sp.wait_ge(sem("ssm_mm"), 2 * (q - 2))
                src = bass.AP(kpd.tensor, kpd.offset + q * (2 * L - 1) * QC, [[QC, L], [1, L * QC]])
                sp.dma_start(Tb[q % 3][:].rearrange("s t c -> s (t c)"), src).then_inc(sem(f"toep_in{q % 3}"), 16)
                if q == 2:
                    sp.wait_ge(sem("g_mm"), HC * NB)
                if 2 <= q < 2 + E:
                    sp.dma_start(w1c[:, q - 2], ins["L0_ffn_w1"][q - 2].rearrange("(c p) h -> p c h", p=P)).then_inc(
                        sem("w1_in"), 16)
                if q == 2 + E:
                    sp.dma_start(gfb[:], ins["L0_ffn_ln_g"].partition_broadcast(P)).then_inc(sem("gfb_in"), 16)
                    sp.wait_ge(sem("c_ps"), len(C_RING))
                    for n in range(3):
                        sp.dma_start(lb12[n * E:(n + 1) * E, :], ins["L0_ffn_ln_b"]).then_inc(sem("lb_in"), 16)
                if q == QN - 4:
                    sp.wait_ge(sem("g_ps"), 2)
                    for c in range(DC):
                        sp.dma_start(Wor[c][:], ins["L0_attn_W_out"][c * P:(c + 1) * P, :]).then_inc(sem("wo_in"), 16)
            sp.wait_ge(sem("ssm_mm"), 2 * QN)
            sp.dma_start(w2raw[:], ins["L0_ffn_w2"].rearrange("e (c p) d -> p e c d", p=P)).then_inc(sem("w2_in"), 16)
            sp.wait_ge(sem("g_ps"), len(G_RING))
            sp.wait_ge(sem("w1g_mult"), DC)
            h0_out(sp)
            for i in range(NT):
                if i >= 2:
                    sp.wait_ge(sem("h1"), i - 1)
                sp.dma_start(h0r[:, i % 2, :], h0d[i]).then_inc(sem(f"h0_back{i % 2}"), 16)
                store(sp, i - 6)
            for i in range(NT - 6, NT):
                store(sp, i)
            for k in range(4):
                sp.wait_ge(sem(f"out_stored{k}"), 16 * len(range(k, NT, 4)))

        @block.gpsimd
        def _(pool):
            pool.memset(ident[:], 0.0).then_inc(sem("ident0"), 1)
            pool.wait_ge(sem("ident0"), 1)
            pool.affine_select(out=ident[:], in_=ident[:], compare_op=ALU.not_equal, fill=1.0, base=0,
                               pattern=[[-1, P]], channel_multiplier=1).then_inc(sem("ident"), 1)
            pool.iota(rowid[:], pattern=[[0, 1]], base=0, channel_multiplier=1,
                      allow_small_or_imprecise_dtypes=True).then_inc(sem("consts"), 1)
            pool.iota(tf[:, 7, :], pattern=[[1, LT]], base=0, channel_multiplier=0,
                      allow_small_or_imprecise_dtypes=True).then_inc(sem("consts"), 1)
            pool.memset(zrow[:], 0.0).then_inc(sem("zrow"), 1)
            pool.memset(epsc[:], EPS).then_inc(sem("consts"), 1)
            pool.memset(onec[:], 1.0).then_inc(sem("consts"), 1)
            pool.iota(kio[:], pattern=[[-1, L]], base=L - 1, channel_multiplier=0,
                      allow_small_or_imprecise_dtypes=True).then_inc(sem("consts"), 1)
            pool.iota(eid[:], pattern=[[1, E]], base=0, channel_multiplier=0,
                      allow_small_or_imprecise_dtypes=True).then_inc(sem("consts"), 1)
            pool.memset(m12[:], 0.0).then_inc(sem("m12"), 1)
            for n in range(3):
                pool.wait_ge(sem("m12"), n + 1)
                pool.affine_select(out=m12[:], in_=m12[:], compare_op=ALU.not_equal, fill=1.0, base=-E * n,
                                   pattern=[[-1, E]], channel_multiplier=1).then_inc(sem("m12"), 1)
            pool.memset(mA[:], 1.0).then_inc(sem("mAB"), 1)
            pool.memset(mB[:], 0.0).then_inc(sem("mAB"), 1)
            pool.wait_ge(sem("mAB"), 2)
            pool.affine_select(out=mA[:], in_=mA[:], compare_op=ALU.is_ge, fill=0.0, base=2 * E - 1,
                               pattern=[[0, 1]], channel_multiplier=-1).then_inc(sem("mAB"), 1)
            pool.affine_select(out=mB[:], in_=mB[:], compare_op=ALU.is_ge, fill=1.0, base=2 * E - 1,
                               pattern=[[0, 1]], channel_multiplier=-1).then_inc(sem("mAB"), 1)
            pool.wait_ge(sem("adt"), 1)
            pool.wait_ge(sem("consts"), 6)
            h0_out(pool)
            pool.wait_ge(sem("zrow_stored"), 64)
            for j in range(HC):
                pool.tensor_tensor(Eb[:, j], adt[:, j].rearrange("p (o s) -> p o s", o=1).broadcast_to([P, L, S]),
                                   kio[:].rearrange("p (k o) -> p k o", o=1).broadcast_to([P, L, S]),
                                   ALU.mult).then_inc(sem("exponent"), 1)
            for c in range(HC * NB):
                j, (a, b) = c // NB, reached(c % NB, 2)
                pool.wait_ge(sem("conv"), c + 1)
                mid = ur[:, j % 2, B + a:B + b]
                pool.tensor_tensor(mid, mid, hb[:, j % 2, a:b], ALU.subtract).then_inc(sem("u_minus_h"), 1)
                pool.wait_ge(sem("u_minus_h"), c + 1)
                pool.wait_ge(sem("gate"), c + 1)
                pool.tensor_tensor(mid, mid, gb[j % 2][:, a:b], ALU.mult).then_inc(sem("gated"), 1)
            pool.wait_ge(sem("w1g_mult"), DC)
            pool.memset(Bst[:].bitcast(F32), 0.0).then_inc(sem("std_zero"), 1)
            pool.wait_ge(sem("g_ps"), 4)
            pool.memset(stdT[:].bitcast(F32), 0.0).then_inc(sem("std_zero"), 1)
            linked = [0]

            def link(ins_):
                linked[0] += 1
                ins_.then_inc(sem("pool_link"), 1)
                pool.wait_ge(sem("pool_link"), linked[0])

            def row_inputs(i):
                pool.wait_ge(sem(f"h0_back{i % 2}"), 16 * (i // 2 + 1))
                pool.wait_ge(sem("nmr0"), 1)
                if i >= 2:
                    pool.wait_ge(sem("r1"), i - 1)
                pool.tensor_scalar(xb[:, i % 2, :], h0r[:, i % 2, :], rs0[:, i:i + 1], nmr0[:, i:i + 1],
                                   ALU.mult, ALU.add).then_inc(sem("xb0"), 1)
                pool.wait_ge(sem("xb0"), i + 1)
                pool.wait_ge(sem("rows_in"), 80)
                pool.tensor_tensor(xb[:, i % 2, :], xb[:, i % 2, :], bout_b[:], ALU.add).then_inc(sem("xb"), 1)
                pool.tensor_tensor(h0r[:, i % 2, :], h0r[:, i % 2, :], lnb_b[:], ALU.add).then_inc(sem("h0b"), 1)

            row_inputs(0)
            for kind, *rest in F_STEPS:
                i = rest[0]
                if kind == "out" and i + 1 < NT:
                    row_inputs(i + 1)
                elif kind == "x2T":
                    pool.wait_ge(sem("x2"), i + 1)
                    pool.tensor_tensor(h1[:, i, :], h1[:, i, :], onb_b[:], ALU.add).then_inc(sem("h1b"), 1)
                elif kind == "route2":
                    t0, t1 = FB[i][0], FB[i][-1] + 1
                    ts, w = slice(t0, t1), t1 - t0
                    pool.wait_ge(sem("gexp"), i + 1)
                    g, rk, cp, pr = gx[:, ts, :], rank[:, ts, :], top[:, ts, :], pair[:, 0:w, :]
                    for d in range(1, E):
                        o = PAIR0[d]
                        pool.tensor_tensor(pr[:, :, o:o + E - d], g[:, :, d:E], g[:, :, 0:E - d], ALU.subtract).then_inc(
                            sem("pair"), 1)
                    pool.wait_ge(sem("pair"), 3 * (i + 1))
                    link(pool.tensor_scalar(pr, pr, 0.0, None, ALU.is_gt))
                    before = eid[:].rearrange("p (o e) -> p o e", o=1).broadcast_to([P, w, E])
                    link(pool.tensor_tensor(rk[:, :, 0:E - 1], before[:, :, 0:E - 1], pr[:, :, 0:E - 1], ALU.add))
                    link(pool.tensor_copy(rk[:, :, E - 1:E], before[:, :, E - 1:E]))
                    link(pool.tensor_tensor(rk[:, :, 1:E], rk[:, :, 1:E], pr[:, :, 0:E - 1], ALU.subtract))
                    for d in range(2, E):
                        o = PAIR0[d]
                        link(pool.tensor_tensor(rk[:, :, 0:E - d], rk[:, :, 0:E - d], pr[:, :, o:o + E - d], ALU.add))
                        link(pool.tensor_tensor(rk[:, :, d:E], rk[:, :, d:E], pr[:, :, o:o + E - d], ALU.subtract))
                    link(pool.tensor_scalar(cp, rk, 2.0, None, ALU.is_lt))
                    link(pool.tensor_tensor(rk[:, :, 0:2], g[:, :, 0:2], g[:, :, 2:4], ALU.add))
                    link(pool.tensor_tensor(cp, cp, g, ALU.mult))
                    link(pool.tensor_tensor(rk[:, :, 2:4], cp[:, :, 0:2], cp[:, :, 2:4], ALU.add))
                    link(pool.tensor_tensor(pr[:, :, 0:2], rk[:, :, 0:E:2], rk[:, :, 1:E:2], ALU.add))
                    link(pool.tensor_scalar(pr[:, :, 2], pr[:, :, 0], 1e-8, None, ALU.mult))
                    link(pool.tensor_tensor(pr[:, :, 3], pr[:, :, 1], pr[:, :, 2], ALU.add))
                    pool.wait_ge(sem("stdE"), i + 1)
                    pool.tensor_tensor(rk, stdE[:, ts, :], pr[:, :, 3:4].broadcast_to([P, w, E]), ALU.mult).then_inc(
                        sem("top2"), 1)
                elif kind == "fin2":
                    for n, t in enumerate(FB[i]):
                        a = acc[:, i % 2, n, :]
                        pool.wait_ge(sem("fin_norm"), t + 1)
                        link(pool.tensor_tensor(a, a, ong_b[:], ALU.mult))
                        pool.wait_ge(sem("h1b"), t + 1)
                        pool.tensor_tensor(a, a, h1[:, t, :], ALU.add).then_inc(sem("result"), 1)

        @block.tensor
        def _(pe):
            def project_dt(q):
                nb, j = BLOCK_ORDER[q // HC], q % HC
                n0, w = BLOCKS[nb]
                pe.wait_ge(sem("xT"), ready_tiles(nb))
                if q >= 4:
                    pe.wait_ge(sem("dt_read"), q - 3)
                elif q >= 2:
                    pe.wait_ge(sem("xT"), NT)
                else:
                    pe.wait_ge(sem("h0_copied"), NT)
                for dc in range(DC):
                    mm = split3(pe, bank[4 + q % 4][:, 0:w], WT[0][0][:, dc, j * P:(j + 1) * P],
                                WT[0][1][:, dc, j * P:(j + 1) * P], xT_hi[:, dc, n0:n0 + w],
                                xT_lo[:, dc, n0:n0 + w], dc == 0, dc == DC - 1)
                mm.then_inc(sem("dt_mm"), 1)

            pe.wait_ge(sem("ident"), 1)
            for step in A_STEPS:
                if step[0] == "ring":
                    q = step[1]
                    kind, *rest = A_RING[q]
                    if q >= 4:
                        who, n = a_read(q - 4)
                        pe.wait_ge(sem(f"a_read_{who}"), n)
                    ps = bank[q % 4]
                    if kind == "vec":
                        pe.wait_ge(sem("vecs_in"), 16 * len(VECS))
                        mm = pe.transpose(ps[:, 0:NV], vec_rows[0:NV, :], ident[0:NV, 0:NV])
                    elif kind == "pos":
                        pe.wait_ge(sem("pos_spread"), 2)
                        k = rest[0]
                        mm = pe.matmul(ps[0:LT + 2, :], ones_b[:, 0:LT + 2],
                                       posD[:].rearrange("p j b -> p (j b)")[:, k * 512:(k + 1) * 512],
                                       start=True, stop=True)
                    elif kind == "wp":
                        pe.wait_ge(sem("wp_in"), 16)
                        for c in range(rest[0], rest[0] + 2):
                            for eh in range(DC):
                                mm = pe.transpose(ps[:, (c % 2) * D + eh * P:(c % 2) * D + (eh + 1) * P],
                                                  Wpr[:, eh, c * P:(c + 1) * P], ident[:])
                    elif kind == "w":
                        w, dc = rest
                        pe.wait_ge(sem(f"w_in{w}"), 16)
                        for j in range(HC):
                            mm = pe.transpose(ps[:, j * P:(j + 1) * P], Wr[w][:, j, dc * P:(dc + 1) * P], ident[:])
                    else:
                        half, g, wp = rest
                        pe.wait_ge(sem(f"img_in{g}{wp // 2}"), 32)
                        for kk in range(KT):
                            c0 = (half * KT + kk) * P
                            mm = pe.transpose(ps[:, kk * ROWS:(kk + 1) * ROWS], XI[:, g, wp, c0:c0 + P],
                                              ident[0:ROWS, 0:ROWS])
                    mm.then_inc(sem("a_ps"), 1)
                elif step[0] == "a1":
                    i = step[1]
                    m = TILE_ORDER.index(i)
                    ps = bank[4 + m % 2][:, 0:D]
                    if m >= 2:
                        pe.wait_ge(sem("h0_copied"), m - 1)
                    if i >= NTI:
                        pe.wait_ge(sem("onehot"), 2)
                        pe.wait_ge(sem("table_in"), 16)
                        mm = pe.matmul(ps, OH[:, (i - NTI) * P:(i - NTI + 1) * P], tabl[:], start=True, stop=True)
                    else:
                        pe.wait_ge(sem("posb"), 2)
                        for q in LAST_IMAGES:
                            who, n = a_read(q)
                            pe.wait_ge(sem(f"a_read_{who}"), n)
                        for c in range(CK):
                            pe.matmul(ps, patchT[:, c, TPT * i:TPT * (i + 1), :].rearrange("p t b -> p (t b)"),
                                      WpT[:, c, :], start=(c == 0), stop=False)
                        mm = pe.matmul(ps, sel[:, TPT * i:TPT * (i + 1), :].rearrange("p t b -> p (t b)"), posb[:],
                                       start=False, stop=True)
                    mm.then_inc(sem("h0_ps"), 1)
                elif step[0] == "a4":
                    m = TILE_ORDER.index(step[1])
                    pe.wait_ge(sem("x"), m + 1)
                    if m >= 2:
                        pe.wait_ge(sem("xT"), m - 1)
                    for dc in range(DC):
                        mm = pe.transpose(bank[6 + m % 2][:, dc * P:(dc + 1) * P], xs[:, m % 2, dc * P:(dc + 1) * P],
                                          ident[:])
                    mm.then_inc(sem("xT_ps"), 1)
                elif step[0] == "dt":
                    project_dt(step[1])

            for q in range(2, HC * NB):
                project_dt(q)

            ring = 0
            for step in C_STEPS:
                if step[0] == "proj":
                    j = step[1]
                    for nb, (n0, w) in enumerate(BLOCKS):
                        c = j * NB + nb
                        for wt, first, done, read in ((1, 0, "u_mm", "ur"), (2, 2, "g_mm", "gate")):
                            if c >= 2:
                                pe.wait_ge(sem(read), c - 1)
                            for dc in range(DC):
                                mm = split3(pe, bank[first + c % 2][:, 0:w], WT[wt][0][:, dc, j * P:(j + 1) * P],
                                            WT[wt][1][:, dc, j * P:(j + 1) * P], xT_hi[:, dc, n0:n0 + w],
                                            xT_lo[:, dc, n0:n0 + w], dc == 0, dc == DC - 1)
                            mm.then_inc(sem(done), 1)
                    continue
                count = 1 if step[0] == "kernels" else B // 4
                for k in range(count):
                    if ring >= 4:
                        who, n = c_read(ring - 4)
                        pe.wait_ge(sem(f"c_read_{who}"), n)
                    ps = bank[4 + ring % 4]
                    if step[0] == "kernels":
                        pe.wait_ge(sem("kernel_sum"), HC)
                        for j in range(HC):
                            mm = pe.transpose(ps[0:L, j * P:(j + 1) * P], Kk[:, j, :], ident[:])
                    else:
                        j = step[1]
                        if j == 0:
                            pe.wait_ge(sem("dt_read"), HC * NB)
                        pe.wait_ge(sem("mixed"), NB * (j + 1))
                        for b in range(4 * k, 4 * k + 4):
                            mm = pe.transpose(ps[0:L, (b % 4) * P:(b % 4 + 1) * P],
                                              hb[:, j % 2, :].rearrange("p (t b) -> p t b", b=B)[:, :, b], ident[:])
                    mm.then_inc(sem("c_ps"), 1)
                    ring += 1

            pe.wait_ge(sem("ur"), HC * NB)
            pe.wait_ge(sem("gate"), HC * NB)
            for q in (len(C_RING) - 2, len(C_RING) - 1):
                who, n = c_read(q)
                pe.wait_ge(sem(f"c_read_{who}"), n)
            aux = 0

            def aux_bank():
                nonlocal aux
                if aux >= 4:
                    name, n = aux_read(aux - 4)
                    pe.wait_ge(sem(name), n)
                aux += 1
                return bank[4 + (aux - 1) % 4]

            def weights(q):
                kind, *rest = G_RING[q]
                ps = aux_bank()
                if kind == "wo":
                    pe.wait_ge(sem("wo_in"), 32)
                    for j in range(2):
                        for c in range(DC):
                            h0_ = (2 * rest[0] + j) * P
                            mm = pe.transpose(ps[:, j * D + c * P:j * D + (c + 1) * P], Wor[c][:, h0_:h0_ + P], ident[:])
                elif kind == "rw":
                    pe.wait_ge(sem("router_in"), 16)
                    for dc in range(DC):
                        mm = pe.transpose(ps[:, dc * E:(dc + 1) * E], rwt[:, dc * P:(dc + 1) * P], ident[0:E, 0:E])
                elif kind == "cbc":
                    pe.wait_ge(sem("rnb_spread"), DC)
                    pe.wait_ge(sem("rwT"), 1)
                    for dc in range(DC):
                        mm = pe.matmul(ps[:, 0:E], zjunk[:, 0, dc * P:(dc + 1) * P], rwT[:, dc, :], start=(dc == 0),
                                       stop=(dc == DC - 1))
                else:
                    e, k = rest
                    pe.wait_ge(sem("w1_centred"), E * DC)
                    for hc in range(2):
                        for dc in range(DC):
                            c0 = (2 * k + hc) * P
                            mm = pe.transpose(ps[:, hc * D + dc * P:hc * D + (dc + 1) * P], w1c[:, e, dc, c0:c0 + P],
                                              ident[:])
                mm.then_inc(sem("g_ps"), 1)

            for v in range(2 * QN):
                q = v // 2
                pe.wait_ge(sem(f"toep_in{q % 3}"), 16 * (q // 3 + 1))
                if v >= 4:
                    pe.wait_ge(sem("y_dve" if v % 2 else "y_act"), (v - 4) // 2 + 1)
                for k in range(4):
                    hq = 4 * v + k
                    for j in range(HC):
                        mm = pe.matmul(bank[v % 4][j * B:(j + 1) * B, k * L:(k + 1) * L], U2[:, j, hq, :],
                                       Tb[q % 3][:, :, j * QH + hq % QH], start=True, stop=True)
                mm.then_inc(sem("ssm_mm"), 1)
                for q in BEHIND.get(v, []):
                    weights(q)
            for q in range(4, len(G_RING)):
                weights(q)

            for kind, *rest in F_STEPS:
                i = rest[0]
                if kind == "yT":
                    ps = aux_bank()
                    if i == 0:
                        pe.wait_ge(sem("y_act"), QN)
                        pe.wait_ge(sem("y_dve"), QN)
                    for tt in range(TPT):
                        mm = pe.transpose(ps[:, tt * P:(tt + 1) * P], y[:, :, L - 1 - (TPT * i + tt)], ident[:])
                    mm.then_inc(sem("yT_ps"), 1)
                elif kind == "out":
                    ps = aux_bank()
                    pe.wait_ge(sem("yT"), i + 1)
                    for j in range(HC):
                        mm = split3(pe, ps[:, 0:D], yT_hi[:, i % 2, j, :], yT_lo[:, j, :], Wo_hi[:, j, :],
                                    Wo_lo[:, j, :], j == 0, j == HC - 1)
                    mm.then_inc(sem("out_mm"), 1)
                elif kind == "x2T":
                    ps = aux_bank()
                    pe.wait_ge(sem("x2"), i + 1)
                    for dc in range(DC):
                        mm = pe.transpose(ps[:, dc * P:(dc + 1) * P], x2s[:, i % 2, dc * P:(dc + 1) * P], ident[:])
                    mm.then_inc(sem("x2T_ps"), 1)
                elif kind == "gram":
                    ps = aux_bank()
                    if i == 0:
                        for q in (len(G_RING) - 2, len(G_RING) - 1):
                            pe.wait_ge(sem(aux_read(q)[0]), aux_read(q)[1])
                    for dc in range(DC):
                        w = (dc + 1) * P
                        for hc in range(HC):
                            mm = pe.matmul(ps[:, dc * D:dc * D + w], w1cT[i][:, hc, dc * P:(dc + 1) * P],
                                           w1cT[i][:, hc, 0:w], start=(hc == 0), stop=(hc == HC - 1))
                    mm.then_inc(sem("gram_mm"), 1)
                elif kind in ("z0", "z1"):
                    pe.wait_ge(sem("x2T"), i + 1)
                    tok_ = slice(i % 2 * P, (i % 2 + 1) * P)
                    hi, lo = x2T_hi[:, i // 2 % 2, :, tok_], x2T_lo[:, i // 2 % 2, :, tok_]
                    ps = aux_bank()
                    pl = bank[4 + AUX.index(("x2T", i)) % 4][:, D:D + 2 * E]
                    if kind == "z0":
                        pe.wait_ge(sem("router_split"), 2)
                    if i == 0:
                        pe.wait_ge(sem("G_lo"), len(GRAM) * E)
                    cols = slice(0, 512) if kind == "z0" else slice(512, 1024)
                    own = lambda a: a.rearrange("p (e k d) -> p e k d", e=2, k=DC)[:, :, 0, :]
                    for dc in (1, 0):
                        o, g_hi, g_lo = ps[:], G_hi[:, dc, cols], G_lo[:, dc, cols]
                        if dc == 0:
                            o, g_hi, g_lo = own(o), own(g_hi), own(g_lo)
                        for n, (a, g) in enumerate(((hi, g_hi), (hi, g_lo), (lo, g_hi))):
                            first, final = dc == 1 and n == 0, dc == 0 and n == 2
                            if kind == "z0" and n != 1:
                                w = E if n else 2 * E
                                mm = pe.matmul(pl[:, 0:w], a[:, dc, :],
                                               rg_hl[:, dc].rearrange("p a e -> p (a e)")[:, 0:w], start=first, stop=final)
                                if final:
                                    mm.then_inc(sem("logit_mm"), 1)
                            mm = pe.matmul(o, a[:, dc, :], g, start=first, stop=final)
                    mm.then_inc(sem("z_mm"), 1)
                elif kind == "stdT":
                    ps = aux_bank()
                    pe.wait_ge(sem("s3"), 3 * (i // 2 + 1))
                    mm = pe.transpose(ps[0:3 * E, 0:P], s3[:, i % 2].rearrange("p a e -> p (a e)").bitcast(F32), ident[:])
                    mm.then_inc(sem("stdT_ps"), 1)
                elif kind == "hid":
                    b, e, k = rest
                    q, w = hid_job(b, e, k), P * len(FB[b])
                    if q == 0:
                        pe.wait_ge(sem("w1g_split"), 2)
                        pe.wait_ge(sem("Bst"), E)
                    if q >= 2:
                        pe.wait_ge(sem("hid_lo"), q - 1)
                    pe.wait_ge(sem("stdT"), FB[b][-1] + 1)
                    for hc in (2 * k, 2 * k + 1):
                        ps = bank[q % 2][:, (hc % 2) * 2 * P:(hc % 2) * 2 * P + w]
                        hs = slice(hc * P, (hc + 1) * P)
                        for dc in range(DC):
                            split3(pe, ps, w1g_hi[:, e, dc, hs], w1g_lo[:, e, dc, hs], x2T_hi[:, b % 2, dc, 0:w],
                                   x2T_lo[:, b % 2, dc, 0:w], dc == 0, False)
                        mm = pe.matmul(ps, Bst[:, e, hs], stdT[:, b % 2, 0:w], start=False, stop=True)
                    mm.then_inc(sem("hid_mm"), 1)
                elif kind == "w2":
                    b, e = rest
                    q = b * E + e
                    if q == 0:
                        pe.wait_ge(sem("w2_split"), 1)
                    if q == 2:
                        pe.wait_ge(sem("w2_split"), 2)
                    if q >= 2:
                        pe.wait_ge(sem("combined"), q - 1)
                    pe.wait_ge(sem("hid_lo"), hid_job(b, e, 1) + 1)
                    for n in range(len(FB[b])):
                        ts = slice(n * P, (n + 1) * P)
                        for hc in range(HC):
                            mm = split3(pe, bank[2 + q % 2][:, n * D:(n + 1) * D], hid_hi[:, e % 2, hc, ts],
                                        hid_lo[:, e % 2, hc, ts], w2_hi[:, e, hc, :], w2_lo[:, e, hc, :],
                                        hc == 0, hc == HC - 1)
                    mm.then_inc(sem("w2_mm"), 1)

        @block.scalar
        def _(act):
            act.dma_start(Wpr[:], ins["L0_tok_W_proj"].rearrange("(c p) d -> p c d", p=P)).then_inc(sem("wp_in"), 16)
            act.dma_start(araw[:], state("L0_attn_A_raw")).then_inc(sem("araw_in"), 16)
            act.dma_start(posb[:], ins["L0_tok_pos_emb"]).then_inc(sem("pos_in"), 16)
            act.dma_start(bpb[:], ins["L0_tok_b_proj"].partition_broadcast(LI)).then_inc(sem("pos_in"), 16)

            def copy(o, i):
                return act.activation(o, i, ACT.Identity)

            act.preload_act_table_set("natural_log_exp_and_others")
            act.wait_ge(sem("a_capped"), 1)
            act.activation(atmp[:], atmp[:], ACT.Exp).then_inc(sem("a_exp"), 1)
            act.wait_ge(sem("a_exp"), 1)
            act.wait_ge(sem("consts"), 6)
            act.activation(atmp[:], atmp[:], ACT.Ln, bias=onec[:]).then_inc(sem("a_ln"), 1)
            for step in A_STEPS:
                if step[0] == "ring":
                    q = step[1]
                    kind, *rest = A_RING[q]
                    ps = bank[q % 4]
                    if kind == "wp":
                        act.wait_ge(sem("a_ps"), q + 1)
                        c = rest[0]
                        copy(WpT[:, c:c + 2, :].rearrange("p c e -> p (c e)"), ps[:]).then_inc(sem("a_read_act"), 1)
                    elif kind == "w":
                        w, dc = rest
                        act.wait_ge(sem("a_ps"), q + 1)
                        copy(WT[w][0][:, dc, :], ps[:]).then_inc(sem("w_hi"), 1)
                    elif kind == "img" and a_reader(q) == "act":
                        act.wait_ge(sem("a_ps"), q + 1)
                        copy(*patches(ps, *rest)).then_inc(sem("a_read_act"), 1)
                    continue
                if step[0] == "dt":
                    continue
                kind, m = step[0], TILE_ORDER.index(step[1])
                i = step[1]
                if kind == "a1":
                    act.wait_ge(sem("h0_ps"), m + 1)
                    if m >= NH0:
                        act.wait_ge(sem(f"h0_stored{(m - NH0) // NH0}"), 16)
                        act.wait_ge(sem("x"), m - NH0 + 1)
                    copy(h0s[:, m % NH0, :], bank[4 + m % 2][:, 0:D]).then_inc(sem("h0_copied"), 1)
                elif kind == "a3":
                    act.wait_ge(sem("mv0"), m + 1)
                    act.activation(sd0[:, i:i + 1], mv0[:, i, 1:2], ACT.Sqrt, bias=epsc[:]).then_inc(sem("sd0"), 1)
                elif kind == "a4":
                    act.wait_ge(sem("xT_ps"), m + 1)
                    copy(xT_hi[:, :, i * P:(i + 1) * P], bank[6 + m % 2][:, 0:D].rearrange("p (c n) -> p c n", c=DC)
                         ).then_inc(sem("xT_hi"), 1)
            act.preload_act_table_set("natural_log_exp_and_others")
            for q in range(HC * NB):
                w = BLOCKS[BLOCK_ORDER[q // HC]][1]
                act.wait_ge(sem("dt_capped"), q + 1)
                act.activation(spt[:, q % 4, 0:w], spt[:, q % 4, 0:w], ACT.Exp).then_inc(sem("dt_exp"), 1)
                if q >= 1:
                    log1p(act, q - 1)
            log1p(act, HC * NB - 1)
            for step in C_STEPS:
                if step[0] == "proj":
                    j = step[1]
                    if j == 0:
                        act.wait_ge(sem("ur_pads"), 2)
                    for nb, (n0, w) in enumerate(BLOCKS):
                        c = j * NB + nb
                        act.wait_ge(sem("u_mm"), c + 1)
                        if j >= 2:
                            act.wait_ge(sem("mixed"), NB * (j - 1))
                        copy_b(act, ur[:, j % 2, B + n0:B + n0 + w], bank[c % 2][:, 0:w], vec[:, bx0 + j:bx0 + j + 1]
                               ).then_inc(sem("ur"), 1)
                        act.wait_ge(sem("g_mm"), c + 1)
                        if j >= 2:
                            act.wait_ge(sem("gated"), NB * (j - 1))
                        if j == 1:
                            act.wait_ge(sem("zrow_stored"), 64)
                            h0_out(act)
                        act.activation(gb[j % 2][:, n0:n0 + w], bank[2 + c % 2][:, 0:w], ACT.Sigmoid,
                                       bias=vec[:, bg0 + j:bg0 + j + 1]).then_inc(sem("gate"), 1)
                        a, b = reached(nb, 1)
                        act.wait_ge(sem("ur"), c + 1)
                        act.wait_ge(sem("cw_in"), 16)
                        if j >= 2:
                            act.wait_ge(sem("c_ps"), 1 + max(q for q, r in enumerate(C_RING) if r[0:2] == ("uT", j - 2)))
                        act.activation(hb[:, j % 2, a:b], ur[:, j % 2, B + a:B + b], ACT.Identity, scale=cw[:, j, 1:2],
                                       bias=vec[:, cb0 + j:cb0 + j + 1]).then_inc(sem("h_init"), 1)
                elif step[0] == "turn":
                    turned(act, step[1], "act")
                if step == ("turn", 0):
                    act.wait_ge(sem("adt"), 1)
                    act.activation(wmix[:], adt[:], ACT.Exp).then_inc(sem("a_d"), 1)
                    for j in range(HC):
                        act.wait_ge(sem("exponent"), j + 1)
                        act.activation(Eb[:, j], Eb[:, j], ACT.Exp).then_inc(sem("powers"), 1)
            for v in range(0, 2 * QN, 2):
                act.wait_ge(sem("ssm_mm"), v + 1)
                copy(y[:, 4 * v:4 * v + 4, :].rearrange("p k t -> p (k t)"), bank[v % 4][:, 0:4 * L]).then_inc(
                    sem("y_act"), 1)
                if v in (22, 24):
                    dc = (v - 22) // 2
                    act.wait_ge(sem("w1g_mult"), dc + 1)
                    copy(w1g_hi[:, :, dc, :], w1p[:, :, dc, :]).then_inc(sem("w1g_hi"), 1)
            for q in range(2, len(G_RING)):
                kind, *rest = G_RING[q]
                ps = bank[4 + q % 4]
                if kind == "wo":
                    act.wait_ge(sem("g_ps"), q + 1)
                    act.wait_ge(sem("ssm_mm"), 2 * QN - 2)
                    j = 2 * rest[0]
                    copy(Wo_hi[:, j:j + 2, :].rearrange("p j d -> p (j d)"), ps[:]).then_inc(sem("Wo_hi"), 1)
                elif rest[1] == 0:
                    act.wait_ge(sem("g_ps"), q + 1)
                    copy(w1cT[rest[0]][:, 0:2, :].rearrange("p j d -> p (j d)"), ps[:]).then_inc(sem("aux_read_act"), 1)
            for kind, *rest in F_STEPS:
                i = rest[0]
                if kind == "yT":
                    act.wait_ge(sem("yT_ps"), i + 1)
                    act.wait_ge(sem("w1g_mult"), DC)
                    act.wait_ge(sem("g_ps"), len(G_RING))
                    if i >= 2:
                        act.wait_ge(sem("out_mm"), i - 1)
                    n = AUX.index((kind, i))
                    copy(yT_hi[:, i % 2].rearrange("p j (t b) -> p j t b", b=B),
                         bank[4 + n % 4][:].rearrange("p (t j b) -> p j t b", j=HC, b=B)).then_inc(sem("yT_hi"), 1)
                elif kind == "gram":
                    n = AUX.index((kind, i))
                    act.wait_ge(sem("gram_mm"), i + 1)
                    for dc, c0, times in GRAM:
                        act.activation(G_hi[:, dc, i * D + c0:i * D + c0 + P],
                                       bank[4 + n % 4][:, dc * D + c0:dc * D + c0 + P], ACT.Identity,
                                       scale=times).then_inc(sem("G_hi"), 1)
                elif kind == "w2split":
                    act.wait_ge(sem("w2_in"), 16)
                    es = slice(2 * i, 2 * i + 2)
                    copy(w2_hi[:, es], w2raw[:, es]).then_inc(sem("w2_hi"), 1)
                elif kind == "ln1":
                    ts = slice(FB[i][0], FB[i][-1] + 1)
                    act.wait_ge(sem("mv1"), ts.stop)
                    act.activation(sd1[:, ts], mv1[:, ts, 1], ACT.Sqrt, bias=epsc[:]).then_inc(sem("sd1"), 1)
                elif kind == "x2":
                    ts = slice(FB[i][0], FB[i][-1] + 1)
                    act.wait_ge(sem("mv2"), ts.stop)
                    act.activation(sd2[:, ts], mv2[:, ts, 1], ACT.Sqrt, bias=epsc[:]).then_inc(sem("sd2"), 1)
                elif kind == "x2T":
                    if i % 2 == 0:
                        ts = slice(i, FB[i // 2][-1] + 1)
                        act.wait_ge(sem("v2n"), i // 2 + 1)
                        act.activation(rs2r[:, ts], v2n[:, ts], ACT.Sqrt, bias=epsc[:]).then_inc(sem("sdr"), 1)
                    act.wait_ge(sem("x2T_ps"), i + 1)
                    if i == 0:
                        act.wait_ge(sem("Bst"), E)
                    n = AUX.index((kind, i))
                    copy(x2T_hi[:, i // 2 % 2, :, i % 2 * P:(i % 2 + 1) * P],
                         bank[4 + n % 4][:, 0:D].rearrange("p (c n) -> p c n", c=DC)).then_inc(sem("x2T_hi"), 1)
                elif kind == "std":
                    ts = slice(FB[i][0], FB[i][-1] + 1)
                    act.wait_ge(sem("var_ok"), ts.stop)
                    act.activation(stdE[:, ts, :], varE[:, ts, :], ACT.Sqrt, bias=epsc[:], scale=1.0 / HF).then_inc(
                        sem("stdE"), 1)
                elif kind == "stdT":
                    act.wait_ge(sem("stdT_ps"), i + 1)
                    act.wait_ge(sem("std_zero"), 2)
                    n = AUX.index((kind, i))
                    copy(stdT[0:3 * E, i // 2 % 2, i % 2 * P:(i % 2 + 1) * P], bank[4 + n % 4][0:3 * E, 0:P]).then_inc(
                        sem("stdT"), 1)
                    act.wait_ge(sem("stdT"), i + 1)
                    act.sem_inc(sem("aux_read_act"), 1)
                elif kind == "route1":
                    act.wait_ge(sem("logit_rel"), i + 1)
                    ts = slice(FB[i][0], FB[i][-1] + 1)
                    act.activation(gx[:, ts, :], gx[:, ts, :], ACT.Exp).then_inc(sem("gexp"), 1)
                    act.preload_act_table_set("sqrt_and_others")
                elif kind == "hid":
                    b, e, k = rest
                    q, w = hid_job(b, e, k), P * len(FB[b])
                    act.wait_ge(sem("hid_mm"), q + 1)
                    if b * E + e >= 2:
                        act.wait_ge(sem("w2_mm"), b * E + e - 1)
                    act.activation(hid_hi[:, e % 2, 2 * k:2 * k + 2, 0:w],
                                   bank[q % 2][:].rearrange("p (c n) -> p c n", c=2)[:, :, 0:w], ACT.Relu).then_inc(
                                       sem("hid_hi"), 1)
                elif kind == "fin2":
                    ts = slice(FB[i][0], FB[i][-1] + 1)
                    act.wait_ge(sem("mv3"), ts.stop)
                    act.activation(sd3[:, ts], mv3[:, ts, 1], ACT.Sqrt, bias=epsc[:]).then_inc(sem("sd3"), 1)

        @block.vector
        def _(dve):
            linked = [0]

            def link(ins_):
                linked[0] += 1
                ins_.then_inc(sem("dve_link"), 1)
                dve.wait_ge(sem("dve_link"), linked[0])

            def mark(ins_):
                linked[0] += 1
                ins_.then_inc(sem("dve_link"), 1)
                return linked[0]

            def need(n):
                dve.wait_ge(sem("dve_link"), n)

            def signal(ins_, name, n):
                ins_.then_inc(sem(name), 1)
                dve.wait_ge(sem(name), n)

            dve.wait_ge(sem("tok_in"), 16)
            dve.wait_ge(sem("consts"), 6)
            jp = tf[:, 7, :]
            link(dve.tensor_copy(tf[:, 0, :], tok[:]))
            link(dve.tensor_scalar(tf[:, 1, :], tf[:, 0, :], 1.0, None, ALU.not_equal))
            link(dve.tensor_tensor_scan(tf[:, 2, :], tf[:, 1, :], tf[:, 1, :], 1.0, ALU.mult, ALU.mult))
            link(dve.scalar_tensor_tensor(tf[:, 3, :], tf[:, 0, :], 4.0, jp, ALU.is_equal, ALU.mult))
            link(dve.tensor_tensor_scan(tf[:, 4, :], tf[:, 3, :], tf[:, 3, :], 0.0, ALU.max, ALU.max))
            link(dve.tensor_tensor(tf[:, 5, :], jp, tf[:, 4, :], ALU.subtract))
            link(dve.scalar_tensor_tensor(tf[:, 6, :], tf[:, 5, :], 1.0, tf[:, 2, :], ALU.add, ALU.mult))
            link(dve.tensor_scalar(tf[:, 5, :], tf[:, 6, :], 1.0, None, ALU.add))
            dve.wait_ge(sem("ident"), 1)
            dve.tensor_tensor(posD[:], tf[:, 5, :].rearrange("p (j o) -> p j o", o=1).broadcast_to([B, LT, B]),
                              ident[0:B, 0:B].rearrange("p (o b) -> p o b", o=1).broadcast_to([B, LT, B]),
                              ALU.mult).then_inc(sem("pos_spread"), 1)
            dve.memset(ones_b[:], 1.0).then_inc(sem("pos_spread"), 1)
            dve.wait_ge(sem("araw_in"), 16)
            dve.tensor_scalar(atmp[:], araw[:], 40.0, None, ALU.min).then_inc(sem("a_capped"), 1)
            dve.tensor_copy(sel[:], ident[0:LI, 0:LI].rearrange("p (t o) -> p t o", o=1).broadcast_to([LI, LI, B])
                            ).then_inc(sem("posb"), 1)
            dve.wait_ge(sem("pos_in"), 32)
            dve.tensor_tensor(posb[:], posb[:], bpb[:], ALU.add).then_inc(sem("posb"), 1)
            for step in A_STEPS:
                if step[0] == "ring":
                    q = step[1]
                    kind, *rest = A_RING[q]
                    ps = bank[q % 4]
                    if a_reader(q) != "dve":
                        continue
                    dve.wait_ge(sem("a_ps"), q + 1)
                    if kind == "vec":
                        dve.tensor_copy(vec[:, 0:NV], ps[:, 0:NV]).then_inc(sem("a_read_dve"), 1)
                    elif kind == "pos":
                        k = rest[0]
                        dve.wait_ge(sem("consts"), 6)
                        signal(dve.tensor_scalar(OH[:, k * 512:(k + 1) * 512], ps[0:LT + 2, :], rowid[0:LT + 2, :], None,
                                                 ALU.is_equal), "onehot", k + 1)
                        dve.sem_inc(sem("a_read_dve"), 1)
                    elif kind == "w":
                        w, dc = rest
                        dve.wait_ge(sem("w_hi"), w * DC + dc + 1)
                        dve.tensor_tensor(WT[w][1][:, dc, :], ps[:], WT[w][0][:, dc, :].bitcast(F32), ALU.subtract
                                          ).then_inc(sem("a_read_dve"), 1)
                    else:
                        dve.tensor_copy(*patches(ps, *rest)).then_inc(sem("a_read_dve"), 1)
                    continue
                if step[0] == "dt":
                    continue
                kind, i = step
                m = TILE_ORDER.index(i)
                if kind == "a2":
                    dve.wait_ge(sem("h0_copied"), m + 1)
                    link(dve.bn_stats(bst[:], h0s[:, m % NH0, :]))
                    signal(dve.bn_aggr(mv0[:, i, :], bst[:]), "mv0", m + 1)
                elif kind == "a3":
                    dve.wait_ge(sem("sd0"), m + 1)
                    link(dve.reciprocal(rs0[:, i:i + 1], sd0[:, i:i + 1]))
                    if m >= 2:
                        dve.wait_ge(sem("xT_ps"), m - 1)
                    dve.tensor_scalar(xs[:, m % 2, :], h0s[:, m % NH0, :], mv0[:, i, 0:1], rs0[:, i:i + 1], ALU.subtract,
                                      ALU.mult).then_inc(sem("x"), 1)
                elif kind == "a4":
                    dve.wait_ge(sem("xT_hi"), m + 1)
                    dve.tensor_tensor(xT_lo[:, :, i * P:(i + 1) * P],
                                      bank[6 + m % 2][:, 0:D].rearrange("p (c n) -> p c n", c=DC),
                                      xT_hi[:, :, i * P:(i + 1) * P].bitcast(F32), ALU.subtract).then_inc(sem("xT"), 1)
            dve.wait_ge(sem("xT_ps"), NT)
            for q in range(HC * NB + 2):
                if q < HC * NB:
                    w, j = BLOCKS[BLOCK_ORDER[q // HC]][1], q % HC
                    dve.wait_ge(sem("dt_mm"), q + 1)
                    dve.tensor_scalar(spt[:, q % 4, 0:w], bank[4 + q % 4][:, 0:w], vec[:, bdt0 + j:bdt0 + j + 1], 40.0,
                                      ALU.add, ALU.min).then_inc(sem("dt_capped"), 1)
                if q >= 2:
                    k = q - 2
                    w, j = BLOCKS[BLOCK_ORDER[k // HC]][1], k % HC
                    dve.wait_ge(sem("dt_ln"), k + 1)
                    if k >= 2:
                        dve.wait_ge(sem("dt_read"), k - 1)
                    dve.scalar_tensor_tensor(spj[:, k % 2, 0:w], bank[4 + k % 4][:, 0:w], vec[:, bdt0 + j:bdt0 + j + 1],
                                             spt[:, k % 4, 0:w], ALU.add, ALU.max,
                                             accum_out=dts[:, j, k // HC:k // HC + 1]).then_inc(sem("dt_read"), 1)
            dve.wait_ge(sem("a_ln"), 1)
            link(dve.tensor_tensor(amat[:], araw[:], atmp[:], ALU.max))
            link(dve.tensor_scalar(amat[:], amat[:], -1.0, None, ALU.mult))
            dve.wait_ge(sem("dt_read"), HC * NB)
            link(dve.reduce_sum(dt1[:], dts[:], AX))
            link(dve.tensor_scalar(dtc[:], dt1[:], 1.0 / N, 0.001, ALU.mult, ALU.max))
            link(dve.tensor_scalar(dt1[:], dtc[:], 2.0, None, ALU.min))
            dve.tensor_tensor(adt[:], amat[:], dt1[:].rearrange("p (c o) -> p c o", o=1).broadcast_to([P, HC, S]),
                              ALU.mult).then_inc(sem("adt"), 1)
            dve.wait_ge(sem("x"), NT)
            dve.scalar_tensor_tensor(nmr0[:], mv0[:, :, 0], -1.0, rs0[:], ALU.mult, ALU.mult).then_inc(sem("nmr0"), 1)
            dve.wait_ge(sem("a_ps"), len(A_RING))
            for k in range(2):
                dve.memset(ur[:, k].rearrange("p (a c) -> p a c", c=B)[:, ::N // B + 1, :], 0.0).then_inc(
                    sem("ur_pads"), 1)

            def kernel_sum(j):
                if j == 0:
                    link(dve.tensor_scalar(winv[:], amat[:], 1e-6, None, ALU.add))
                    link(dve.reciprocal(winv[:], winv[:]))
                    dve.wait_ge(sem("a_d"), 1)
                    link(dve.scalar_tensor_tensor(wmix[:], wmix[:], 1.0, winv[:], ALU.subtract, ALU.mult))
                    dve.wait_ge(sem("bcs_in"), 32)
                    link(dve.tensor_tensor(wmix[:], wmix[:], bcs[:, 0], ALU.mult))
                    link(dve.tensor_tensor(wmix[:], wmix[:], bcs[:, 1], ALU.mult))
                dve.wait_ge(sem("powers"), j + 1)
                signal(dve.tensor_tensor(Eb[:, j], Eb[:, j],
                                         wmix[:, j].rearrange("p (o s) -> p o s", o=1).broadcast_to([P, L, S]),
                                         ALU.mult), "power_w", j + 1)
                dve.reduce_sum(Kk[:, j, :], Eb[:, j], AX).then_inc(sem("kernel_sum"), 1)

            for step in C_STEPS:
                if step[0] == "proj":
                    j = step[1]
                    for nb in range(NB):
                        c, (a, b) = j * NB + nb, reached(nb, 1)
                        dve.wait_ge(sem("h_init"), c + 1)
                        if nb == NB - 1:
                            dve.wait_ge(sem("ur_pads"), 2)
                        u, h = ur[:, j % 2], hb[:, j % 2, a:b]
                        link(dve.scalar_tensor_tensor(h, u[:, a:b], cw[:, j, 0:1], h, ALU.mult, ALU.add))
                        dve.scalar_tensor_tensor(h, u[:, 2 * B + a:2 * B + b], cw[:, j, 2:3], h, ALU.mult, ALU.add
                                                 ).then_inc(sem("conv"), 1)
                        for k in KERNEL_SUMS.get((j, nb), []):
                            kernel_sum(k)
                        if c >= MIX_LAG:
                            mix(dve, c - MIX_LAG)
                elif step[0] == "turn":
                    last = range(HC * NB - MIX_LAG, HC * NB) if step[1] == HC - 2 else ()
                    turned(dve, step[1], "dve", last)
                    for k in KERNEL_SUMS.get(step, []):
                        kernel_sum(k)
                else:
                    q = C_RING.index(("kT",))
                    dve.wait_ge(sem("c_ps"), q + 1)
                    dve.tensor_copy(kt[:].rearrange("k q j h -> k j q h"),
                                    bank[4 + q % 4][0:L, :].rearrange("k (j q h) -> k j q h", j=HC, h=QH)).then_inc(
                                        sem("kt_ready"), 1)
                    dve.wait_ge(sem("kt_ready"), 1)
                    dve.sem_inc(sem("c_read_dve"), 1)
            for v in range(1, 2 * QN, 2):
                dve.wait_ge(sem("ssm_mm"), v + 1)
                dve.tensor_copy(y[:, 4 * v:4 * v + 4, :].rearrange("p k t -> p (k t)"), bank[v % 4][:, 0:4 * L]).then_inc(
                    sem("y_dve"), 1)
                if v == 9:
                    dve.wait_ge(sem("w1_in"), 16 * E)
                    link(dve.reduce_sum(w1m[:], w1c[:].rearrange("p e c h -> p (e c) h"), AX))
                    link(dve.tensor_scalar(w1m[:], w1m[:], -1.0 / HF, None, ALU.mult))
                if v in (11, 13, 15, 17):
                    e = (v - 11) // 2
                    for dc in range(DC):
                        k = e * DC + dc
                        dve.tensor_scalar(w1c[:, e, dc, :], w1c[:, e, dc, :], w1m[:, k:k + 1], None, ALU.add).then_inc(
                            sem("w1_centred"), 1)
                if v == 17:
                    q = 0
                    dve.wait_ge(sem("g_ps"), q + 1)
                    signal(dve.tensor_copy(rwT[:].rearrange("p c e -> p (c e)"), bank[4 + q][:, 0:DC * E]), "rwT", 1)
                    dve.sem_inc(sem("aux_read_dve"), 1)
                    for dc in range(DC):
                        dve.tensor_copy(zjunk[:, 0, dc * P:(dc + 1) * P],
                                        vec[:, rnb0 + dc:rnb0 + dc + 1].broadcast_to([P, P])).then_inc(
                                            sem("rnb_spread"), 1)
                        link(dve.tensor_scalar(rg[:, dc, :], rwT[:, dc, :], vec[:, rng0 + dc:rng0 + dc + 1], None,
                                               ALU.mult))
                    signal(dve.tensor_copy(rg_hl[:, :, 0, :], rg[:]), "router_split", 1)
                    dve.tensor_tensor(rg_hl[:, :, 1, :], rg[:], rg_hl[:, :, 0, :].bitcast(F32), ALU.subtract).then_inc(
                        sem("router_split"), 1)
                if v in (19, 21):
                    dc = (v - 19) // 2
                    if dc == 0:
                        dve.wait_ge(sem("gfb_in"), 16)
                        dve.wait_ge(sem("w1_centred"), E * DC)
                    dve.tensor_tensor(w1p[:, :, dc, :], w1c[:, :, dc, :], gfb[:], ALU.mult).then_inc(sem("w1g_mult"), 1)
                if v == 23:
                    q = 1
                    dve.wait_ge(sem("g_ps"), q + 1)
                    dve.tensor_copy(cbc[:], bank[4 + q][:, 0:E]).then_inc(sem("aux_read_dve"), 1)
                if v in (25, 27):
                    dc = (v - 25) // 2
                    dve.wait_ge(sem("w1g_hi"), dc + 1)
                    dve.tensor_tensor(w1g_lo[:, :, dc, :], w1p[:, :, dc, :], w1g_hi[:, :, dc, :].bitcast(F32),
                                      ALU.subtract).then_inc(sem("w1g_split"), 1)
                if v == 29:
                    dve.wait_ge(sem("lb_in"), 48)
                    dve.wait_ge(sem("std_zero"), 1)
                    dve.wait_ge(sem("mAB"), 4)
                    dve.wait_ge(sem("m12"), 4)
                    link(dve.tensor_copy(lbr[:], lb12[:]))
                    link(dve.tensor_tensor(lb12[:], lb12[:], lbr[:].bitcast(F32), ALU.subtract))
                    link(dve.tensor_scalar(lb12[:], lb12[:], mB[:], None, ALU.mult))
                    link(dve.scalar_tensor_tensor(lb12[:], lbr[:].bitcast(F32), mA[:], lb12[:], ALU.mult, ALU.add))
                    for k in range(E):
                        dve.tensor_scalar(Bst[0:3 * E, k, :], lb12[:], m12[:, k:k + 1], None, ALU.mult).then_inc(
                            sem("Bst"), 1)
            for k in range(2):
                js = slice(2 * k, 2 * k + 2)
                dve.wait_ge(sem("Wo_hi"), k + 1)
                dve.tensor_tensor(Wo_lo[:, js, :].rearrange("p j d -> p (j d)"), bank[4 + G_RING.index(("wo", k)) % 4][:],
                                  Wo_hi[:, js, :].rearrange("p j d -> p (j d)").bitcast(F32), ALU.subtract).then_inc(
                                      sem("aux_read_dve"), 1)
            for q in range(4, len(G_RING)):
                _, e, k = G_RING[q]
                if k == 1:
                    dve.wait_ge(sem("g_ps"), q + 1)
                    dve.tensor_copy(w1cT[e][:, 2:4, :].rearrange("p j d -> p (j d)"), bank[4 + q % 4][:]).then_inc(
                        sem("aux_read_dve"), 1)
            for kind, *rest in F_STEPS:
                i = rest[0]
                if kind == "gram":
                    ps = bank[4 + AUX.index((kind, i)) % 4]
                    dve.wait_ge(sem("G_hi"), len(GRAM) * (i + 1))
                    for dc, c0, times in GRAM:
                        cols = slice(i * D + c0, i * D + c0 + P)
                        dve.scalar_tensor_tensor(G_lo[:, dc, cols], ps[:, dc * D + c0:dc * D + c0 + P], times,
                                                 G_hi[:, dc, cols].bitcast(F32), ALU.mult, ALU.subtract).then_inc(
                                                     sem("G_lo"), 1)
                    dve.wait_ge(sem("G_lo"), len(GRAM) * (i + 1))
                    dve.sem_inc(sem("aux_read_dve"), 1)
                elif kind == "yT":
                    n = AUX.index((kind, i))
                    dve.wait_ge(sem("yT_hi"), i + 1)
                    if i >= 1:
                        dve.wait_ge(sem("out_mm"), i)
                    signal(dve.tensor_tensor(yT_lo[:].rearrange("p j (t b) -> p j t b", b=B),
                                             bank[4 + n % 4][:].rearrange("p (t j b) -> p j t b", j=HC, b=B),
                                             yT_hi[:, i % 2].bitcast(F32).rearrange("p j (t b) -> p j t b", b=B),
                                             ALU.subtract), "yT", i + 1)
                    dve.sem_inc(sem("aux_read_dve"), 1)
                elif kind == "w2split":
                    dve.wait_ge(sem("w2_hi"), i + 1)
                    es = slice(2 * i, 2 * i + 2)
                    dve.tensor_tensor(w2_lo[:, es], w2raw[:, es], w2_hi[:, es].bitcast(F32), ALU.subtract).then_inc(
                        sem("w2_split"), 1)
                elif kind == "out":
                    n = AUX.index((kind, i))
                    dve.wait_ge(sem("out_mm"), i + 1)
                    dve.wait_ge(sem("xb"), i + 1)
                    signal(dve.tensor_tensor(r1[:, i % 2, :], bank[4 + n % 4][:, 0:D], xb[:, i % 2, :], ALU.add), "r1", i + 1)
                    dve.sem_inc(sem("aux_read_dve"), 1)
                elif kind == "ln1":
                    tiles, ts = FB[i], slice(FB[i][0], FB[i][-1] + 1)
                    rs = [r1[:, t % 2, :] for t in tiles]
                    at_ = [mark(dve.bn_stats(bst1[:, t % 2], rs[n])) for n, t in enumerate(tiles)]
                    for n, t in enumerate(tiles):
                        need(at_[n])
                        dve.bn_aggr(mv1[:, t, :], bst1[:, t % 2]).then_inc(sem("mv1"), 1)
                    dve.wait_ge(sem("mv1"), ts.stop)
                    dve.wait_ge(sem("sd1"), i + 1)
                    link(dve.reciprocal(rs1[:, ts], sd1[:, ts]))
                    at_ = [mark(dve.tensor_scalar(r, r, mv1[:, t, 0:1], rs1[:, t:t + 1], ALU.subtract, ALU.mult))
                           for t, r in zip(tiles, rs)]
                    for n, r in enumerate(rs):
                        need(at_[n])
                        at_[n] = mark(dve.tensor_tensor(r, r, lng_b[:], ALU.mult))
                    for n, t in enumerate(tiles):
                        need(at_[n])
                        dve.wait_ge(sem("h0b"), t + 1)
                        dve.tensor_tensor(h1[:, t, :], rs[n], h0r[:, t % 2, :], ALU.add).then_inc(sem("h1"), 1)
                elif kind == "h1":
                    tiles = FB[i]
                    at_ = []
                    for t in tiles:
                        dve.wait_ge(sem("h1"), t + 1)
                        at_.append(mark(dve.bn_stats(bst2[:, t % 2], h1[:, t, :])))
                    for n, t in enumerate(tiles):
                        need(at_[n])
                        dve.bn_aggr(mv2[:, t, :], bst2[:, t % 2]).then_inc(sem("mv2"), 1)
                elif kind == "x2":
                    tiles, ts = FB[i], slice(FB[i][0], FB[i][-1] + 1)
                    dve.wait_ge(sem("mv2"), ts.stop)
                    dve.wait_ge(sem("sd2"), i + 1)
                    link(dve.reciprocal(rs2[:, ts], sd2[:, ts]))
                    if i >= 1:
                        dve.wait_ge(sem("x2T_ps"), ts.start)
                        dve.wait_ge(sem("varE"), E * ts.start)
                    for t in tiles:
                        dve.tensor_scalar(x2s[:, t % 2, :], h1[:, t, :], mv2[:, t, 0:1], rs2[:, t:t + 1], ALU.subtract,
                                          ALU.mult).then_inc(sem("x2"), 1)
                    link(dve.tensor_tensor(v2n[:, ts], mv2[:, ts, 1], rs2[:, ts], ALU.mult))
                    dve.tensor_tensor(v2n[:, ts], v2n[:, ts], rs2[:, ts], ALU.mult).then_inc(sem("v2n"), 1)
                elif kind == "x2T":
                    n = AUX.index((kind, i))
                    ts = slice(i % 2 * P, (i % 2 + 1) * P)
                    dve.wait_ge(sem("x2T_hi"), i + 1)
                    signal(dve.tensor_tensor(x2T_lo[:, i // 2 % 2, :, ts],
                                             bank[4 + n % 4][:, 0:D].rearrange("p (c n) -> p c n", c=DC),
                                             x2T_hi[:, i // 2 % 2, :, ts].bitcast(F32), ALU.subtract), "x2T", i + 1)
                elif kind in ("z0", "z1"):
                    if kind == "z0":
                        n = AUX.index(("x2T", i))
                        if i % 2 == 0:
                            own = slice(i, FB[i // 2][-1] + 1)
                            dve.wait_ge(sem("sdr"), i // 2 + 1)
                            link(dve.reciprocal(rs2r[:, own], rs2r[:, own]))
                        dve.wait_ge(sem("logit_mm"), i + 1)
                        link(dve.scalar_tensor_tensor(lg[:, i, :], bank[4 + n % 4][:, D:D + E], rs2r[:, i:i + 1],
                                                      cbc[:], ALU.mult, ALU.add))
                        dve.scalar_tensor_tensor(lg[:, i, :], bank[4 + n % 4][:, D + E:D + 2 * E], rs2r[:, i:i + 1],
                                                 lg[:, i, :], ALU.mult, ALU.add).then_inc(sem("logits"), 1)
                    n = AUX.index((kind, i))
                    half = int(kind == "z1")
                    dve.wait_ge(sem("z_mm"), z_count(kind, i))
                    for k in range(2):
                        e, done = 2 * half + k, var_count(kind, i) - 2 + k
                        if done >= 2:
                            dve.wait_ge(sem("varE"), done - 1)
                        dve.tensor_tensor_reduce(zjunk[:, k], bank[4 + n % 4][:, k * D:(k + 1) * D], x2s[:, i % 2, :],
                                                 1.0, 0.0, ALU.mult, ALU.add, varE[:, i, e:e + 1]).then_inc(
                                                     sem("varE"), 1)
                    dve.wait_ge(sem("varE"), var_count(kind, i))
                    dve.sem_inc(sem("aux_read_dve"), 1)
                    if kind == "z1":
                        dve.tensor_scalar(varE[:, i, :], varE[:, i, :], 0.0, None, ALU.max).then_inc(sem("var_ok"), 1)
                elif kind == "std":
                    tiles, ts = FB[i], slice(FB[i][0], FB[i][-1] + 1)
                    w = len(tiles)
                    dve.wait_ge(sem("stdE"), i + 1)
                    if i >= 1:
                        dve.wait_ge(sem("stdT_ps"), ts.start)
                    signal(dve.tensor_copy(s3[:, 0:w, 0, :], stdE[:, ts, :]), "s3", 3 * i + 1)
                    dve.tensor_tensor(s3[:, 0:w, 1, :], stdE[:, ts, :], s3[:, 0:w, 0, :].bitcast(F32),
                                      ALU.subtract).then_inc(sem("s3"), 1)
                    dve.tensor_copy(s3[:, 0:w, 2, :], s3[:, 0:w, 0, :].bitcast(F32)).then_inc(sem("s3"), 1)
                elif kind == "route1":
                    t0, t1 = FB[i][0], FB[i][-1] + 1
                    ts, w = slice(t0, t1), t1 - t0
                    dve.wait_ge(sem("logits"), t1)
                    link(dve.tensor_reduce(rsum[:, ts], lg[:, ts, :], AX, ALU.max))
                    dve.tensor_tensor(gx[:, ts, :], lg[:, ts, :], spread(rsum[:, ts], w), ALU.subtract).then_inc(
                        sem("logit_rel"), 1)
                elif kind == "route3":
                    ts = slice(FB[i][0], FB[i][-1] + 1)
                    dve.wait_ge(sem("top2"), i + 1)
                    link(dve.reciprocal(rank[:, ts, :], rank[:, ts, :]))
                    signal(dve.tensor_tensor(wE[:, ts, :], top[:, ts, :], rank[:, ts, :], ALU.mult), "wE", i + 1)
                elif kind == "hid":
                    b, e, k = rest
                    q, w = hid_job(b, e, k), P * len(FB[b])
                    dve.wait_ge(sem("hid_hi"), q + 1)
                    hs = slice(2 * k, 2 * k + 2)
                    dve.scalar_tensor_tensor(hid_lo[:, e % 2, hs, 0:w],
                                             bank[q % 2][:].rearrange("p (c n) -> p c n", c=2)[:, :, 0:w], 0.0,
                                             hid_hi[:, e % 2, hs, 0:w].bitcast(F32), ALU.max, ALU.subtract).then_inc(
                                                 sem("hid_lo"), 1)
                elif kind == "w2":
                    b, e = rest
                    q = b * E + e
                    dve.wait_ge(sem("w2_mm"), q + 1)
                    if e:
                        dve.wait_ge(sem("combined"), q)
                    else:
                        dve.wait_ge(sem("wE"), b + 1)
                    for n, i in enumerate(FB[b]):
                        a, ps = acc[:, b % 2, n, :], bank[2 + q % 2][:, n * D:(n + 1) * D]
                        if e == 0:
                            if i >= 4:
                                dve.wait_ge(sem(f"out_stored{i % 4}"), 16 * (i // 4))
                            last = dve.tensor_scalar(a, ps, wE[:, i, 0:1], None, ALU.mult)
                        else:
                            last = dve.scalar_tensor_tensor(a, ps, wE[:, i, e:e + 1], a, ALU.mult, ALU.add)
                    last.then_inc(sem("combined"), 1)
                elif kind == "fin1":
                    dve.wait_ge(sem("combined"), E * (i + 1))
                    at_ = [mark(dve.bn_stats(bst3[:, n], acc[:, i % 2, n, :])) for n in range(len(FB[i]))]
                    for n, t in enumerate(FB[i]):
                        need(at_[n])
                        dve.bn_aggr(mv3[:, t, :], bst3[:, n]).then_inc(sem("mv3"), 1)
                elif kind == "fin2":
                    ts = slice(FB[i][0], FB[i][-1] + 1)
                    dve.wait_ge(sem("mv3"), ts.stop)
                    dve.wait_ge(sem("sd3"), i + 1)
                    link(dve.reciprocal(rs3[:, ts], sd3[:, ts]))
                    for n, t in enumerate(FB[i]):
                        a = acc[:, i % 2, n, :]
                        dve.tensor_scalar(a, a, mv3[:, t, 0:1], rs3[:, t:t + 1], ALU.subtract, ALU.mult).then_inc(
                            sem("fin_norm"), 1)



def kernel(**inputs):
    import concourse.bacc as _bacc
    from concourse.bass_utils import run_bass_kernel_spmd as _run
    import numpy as _np

    nc = _bacc.Bacc("TRN2", target_bir_lowering=False, num_devices=1)
    arrays, ins = {}, {}
    for name, value in inputs.items():
        a = _np.ascontiguousarray(value)
        arrays[f"in_{name}_dram"] = a
        ins[name] = nc.dram_tensor(f"in_{name}_dram", a.shape, mybir.dt.from_np(a.dtype), kind="ExternalInput").ap()
    batch, seq = inputs["x"].shape[0], 36 + inputs["x_txt"].shape[1]
    out = nc.dram_tensor("out_0_dram", (batch, seq, inputs["L0_tok_W_proj"].shape[0]), F32, kind="ExternalOutput").ap()
    build_kernel(nc, ins, out)
    r = _run(nc, [arrays], core_ids=[0])
    return r.results[0]["out_0_dram"]
```
